# Optimizing a Trainium2 kernel written in Bass

```python
import numpy as np
import jax
import jax.numpy as jnp

def _softmax(x, axis=-1):
    return jax.nn.softmax(x, axis=axis)

def _gelu(x):
    return jax.nn.gelu(x, approximate=True)

def _silu(x):
    return jax.nn.silu(x)

def _sigmoid(x):
    return jax.nn.sigmoid(x)

def _layernorm(x, axis=-1, eps=1e-05):
    m = jnp.mean(x, axis=axis, keepdims=True)
    v = jnp.var(x, axis=axis, keepdims=True)
    return (x - m) / jnp.sqrt(v + eps)

def _scatter_add(tgt, idx, src, axis=0):
    return tgt.at[idx].add(src)

def _segment_sum(src, seg, n):
    return jax.ops.segment_sum(src, seg, n)
kernel_name = 'mk_gnn_resnorm_d4_gnn_r64_d4931b'

def setup_inputs(seed: int=0):
    np.random.seed(seed)
    _w = jnp.asarray

    def _rec_inputs():
        import jax
        import jax.numpy as jnp
        _gk = jax.random.key(seed)
        x = -8.776e-05 + 1 * jax.random.normal(jax.random.fold_in(_gk, 1), (100000, 128), jnp.float32)
        src = jax.random.randint(jax.random.fold_in(_gk, 2), (50000,), 0, 100000, jnp.int32)
        dst = jnp.minimum((100000 * jax.random.uniform(jax.random.fold_in(_gk, 3), (50000,)) ** 2.0).astype(jnp.int32), 99999)
        _o = jnp.argsort(dst, stable=True)
        src = src[_o]
        dst = dst[_o]
        edge_attr_16 = 0.00028786 + 0.999816 * jax.random.normal(jax.random.fold_in(_gk, 12), (50000, 16), jnp.float32)
        return (x, src, dst, edge_attr_16)
    x, src, dst, edge_attr_16 = _rec_inputs()

    def _L0_gnn_setup():
        import jax, jax.numpy as jnp
        import numpy as np
        N_NODES = 625

        def gcn_layer(x, src, dst, W, b, n_nodes):
            h = x @ W
            deg = jax.ops.segment_sum(jnp.ones(src.shape[0], x.dtype), dst, num_segments=n_nodes) + 1.0
            dis = jax.lax.rsqrt(deg)
            norm = dis[src] * dis[dst]
            msg = h[src] * norm[:, None]
            agg = jax.ops.segment_sum(msg, dst, num_segments=n_nodes)
            agg = agg + h * (dis * dis)[:, None]
            return agg + b
        key = jax.random.key(seed)
        k1, k2, k3, k4, k5, k6 = jax.random.split(key, 6)
        n, e = (N_NODES, 10000)
        c_in, c_hid, c_out = (128, 128, 128)
        x_piece = jax.random.normal(k1, (n, c_in), dtype=jnp.float32)
        edge_index_piece = jax.random.randint(k2, (2, e), 0, n, dtype=jnp.int64)
        s = 1.0 / np.sqrt(c_in)
        W1 = jax.random.uniform(k3, (c_in, c_hid), jnp.float32, -s, s)
        b1 = jnp.zeros((c_hid,), jnp.float32)
        W2 = jax.random.uniform(k4, (c_hid, c_out), jnp.float32, -s, s)
        b2 = jnp.zeros((c_out,), jnp.float32)
        return {'x_piece': x_piece, 'edge_index_piece': edge_index_piece, 'W1': W1, 'b1': b1, 'W2': W2, 'b2': b2}
    _L0_gnn_all = _L0_gnn_setup()
    _L0_gnn_in = {k: v for k, v in _L0_gnn_all.items() if k in ('W1', 'b1', 'W2', 'b2')}
    del _L0_gnn_all

    def _L1_gnn_setup():
        import jax, jax.numpy as jnp
        import numpy as np
        N, F, ED, E = (20000, 128, 16, 9375)
        EPS = 1e-05
        key = jax.random.key(seed)
        ks = jax.random.split(key, 8)
        x = jax.random.normal(ks[0], (N, F), dtype=jnp.float32)
        edge_index = jax.random.randint(ks[1], (2, E), 0, N, dtype=jnp.int64)
        edge_attr = jax.random.normal(ks[2], (E, ED), dtype=jnp.float32)
        zdim = 2 * F + ED
        sc = 1.0 / np.sqrt(zdim)
        Wf = jax.random.uniform(ks[3], (F, zdim), jnp.float32, -sc, sc)
        bf = jax.random.uniform(ks[4], (F,), jnp.float32, -sc, sc)
        Ws = jax.random.uniform(ks[5], (F, zdim), jnp.float32, -sc, sc)
        bs = jax.random.uniform(ks[6], (F,), jnp.float32, -sc, sc)
        bn_gamma = jnp.ones((F,), jnp.float32)
        bn_beta = jnp.zeros((F,), jnp.float32)
        ln_gamma = jnp.ones((F,), jnp.float32)
        ln_beta = jnp.zeros((F,), jnp.float32)
        return {'x': x, 'edge_index': edge_index, 'edge_attr': edge_attr, 'Wf': Wf, 'bf': bf, 'Ws': Ws, 'bs': bs, 'bn_gamma': bn_gamma, 'bn_beta': bn_beta, 'ln_gamma': ln_gamma, 'ln_beta': ln_beta}
    _L1_gnn_all = _L1_gnn_setup()
    _L1_gnn_in = {k: v for k, v in _L1_gnn_all.items() if k in ('Wf', 'bf', 'Ws', 'bs', 'bn_gamma', 'bn_beta', 'ln_gamma', 'ln_beta')}
    del _L1_gnn_all

    def _L2_gnn_setup():
        import jax, jax.numpy as jnp
        import numpy as np
        N, IN, OUT, H, ED, E = (50000, 128, 128, 3, 16, 12500)
        NEG_SLOPE = 0.2
        LN_EPS = 1e-05

        def gat_block(x, edge_index, edge_attr, W, W_edge, att_src, att_dst, att_edge, gat_bias, lin_W, lin_b, ln_g, ln_b):
            row, col = (edge_index[0], edge_index[1])
            n = x.shape[0]
            deg = jax.ops.segment_sum(jnp.ones((edge_attr.shape[0],), x.dtype), col, num_segments=n)
            loop_attr = jax.ops.segment_sum(edge_attr, col, num_segments=n) / jnp.maximum(deg, 1.0)[:, None]
            loop = jnp.arange(n, dtype=row.dtype)
            row2 = jnp.concatenate([row, loop])
            col2 = jnp.concatenate([col, loop])
            ea2 = jnp.concatenate([edge_attr, loop_attr], axis=0)
            xp = (x @ W).reshape(n, H, OUT)
            a_src = jnp.einsum('nhc,hc->nh', xp, att_src)
            a_dst = jnp.einsum('nhc,hc->nh', xp, att_dst)
            ep = (ea2 @ W_edge).reshape(-1, H, OUT)
            a_edge = jnp.einsum('ehc,hc->eh', ep, att_edge)
            alpha = a_src[row2] + a_dst[col2] + a_edge
            alpha = jnp.where(alpha >= 0, alpha, NEG_SLOPE * alpha)
            m = jax.ops.segment_max(alpha, col2, num_segments=n)
            ex = jnp.exp(alpha - m[col2])
            denom = jax.ops.segment_sum(ex, col2, num_segments=n)
            attn = ex / denom[col2]
            msg = attn[:, :, None] * xp[row2]
            agg = jax.ops.segment_sum(msg, col2, num_segments=n)
            x_gat = agg.reshape(n, H * OUT) + gat_bias
            y = x_gat @ lin_W + lin_b
            h = x + y
            mu = h.mean(-1, keepdims=True)
            var = ((h - mu) ** 2).mean(-1, keepdims=True)
            return (h - mu) * jax.lax.rsqrt(var + LN_EPS) * ln_g + ln_b
        key = jax.random.key(seed)
        ks = jax.random.split(key, 12)
        s = lambda k, shape, fan: jax.random.normal(k, shape, jnp.float32) / np.sqrt(fan)
        return {'x': jax.random.normal(ks[0], (N, IN), jnp.float32), 'edge_index': jax.random.randint(ks[1], (2, E), 0, N, jnp.int64), 'edge_attr': jax.random.normal(ks[2], (E, ED), jnp.float32), 'W': s(ks[3], (IN, H * OUT), IN), 'W_edge': s(ks[4], (ED, H * OUT), ED), 'att_src': s(ks[5], (H, OUT), OUT), 'att_dst': s(ks[6], (H, OUT), OUT), 'att_edge': s(ks[7], (H, OUT), OUT), 'gat_bias': jnp.zeros((H * OUT,), jnp.float32), 'lin_W': s(ks[8], (H * OUT, OUT), H * OUT), 'lin_b': jnp.zeros((OUT,), jnp.float32), 'ln_g': jnp.ones((OUT,), jnp.float32), 'ln_b': jnp.zeros((OUT,), jnp.float32)}
    _L2_gnn_all = _L2_gnn_setup()
    _L2_gnn_in = {k: v for k, v in _L2_gnn_all.items() if k in ('W', 'W_edge', 'att_src', 'att_dst', 'att_edge', 'gat_bias', 'lin_W', 'lin_b', 'ln_g', 'ln_b')}
    del _L2_gnn_all

    def _L3_gnn_setup():
        import jax, jax.numpy as jnp
        import numpy as np
        N = 100000
        E = 50000
        F_IN = 128
        H = 64

        def _glorot(key, fan_in, fan_out):
            lim = jnp.sqrt(6.0 / (fan_in + fan_out))
            return jax.random.uniform(key, (fan_in, fan_out), minval=-lim, maxval=lim, dtype=jnp.float32)

        def _gcn_norm(edge_index, num_nodes):
            loop = jnp.arange(num_nodes, dtype=edge_index.dtype)
            row = jnp.concatenate([edge_index[0], loop])
            col = jnp.concatenate([edge_index[1], loop])
            deg = jax.ops.segment_sum(jnp.ones_like(col, dtype=jnp.float32), col, num_segments=num_nodes)
            dinv = jnp.where(deg > 0, jax.lax.rsqrt(deg), 0.0)
            norm = dinv[row] * dinv[col]
            return (row, col, norm)

        def _gcn_conv(h, W, b, row, col, norm, num_nodes):
            h = h @ W
            msg = h[row] * norm[:, None]
            agg = jax.ops.segment_sum(msg, col, num_segments=num_nodes)
            return agg + b
        key = jax.random.key(seed)
        ks = jax.random.split(key, 16)
        x = jax.random.normal(ks[0], (N, F_IN), dtype=jnp.float32)
        edge_index = jax.random.randint(ks[1], (2, E), 0, N, dtype=jnp.int32)
        batch = jnp.zeros((N,), dtype=jnp.int32)
        dims = [(F_IN, H), (H, H // 2), (H // 2, H // 4), (H // 4, H // 2), (H // 2, H), (H, F_IN)]
        params = {}
        for i, (fi, fo) in enumerate(dims):
            params[f'W{i + 1}'] = _glorot(ks[2 + i], fi, fo)
            params[f'b{i + 1}'] = jnp.zeros((fo,), dtype=jnp.float32)
        params['Wf'] = _glorot(ks[10], F_IN, F_IN)
        params['bf'] = jnp.zeros((F_IN,), dtype=jnp.float32)
        return {'x': x, 'edge_index': edge_index, 'batch': batch, **params}
    _L3_gnn_all = _L3_gnn_setup()
    _L3_gnn_in = {k: v for k, v in _L3_gnn_all.items() if k in ('W1', 'b1', 'W2', 'b2', 'W3', 'b3', 'W4', 'b4', 'W5', 'b5', 'W6', 'b6', 'Wf', 'bf')}
    del _L3_gnn_all
    return {'x': x, 'src': src, 'dst': dst, 'edge_attr_16': edge_attr_16, 'L0_gnn_W1': _L0_gnn_in['W1'], 'L0_gnn_b1': _L0_gnn_in['b1'], 'L0_gnn_W2': _L0_gnn_in['W2'], 'L0_gnn_b2': _L0_gnn_in['b2'], 'L1_gnn_Wf': _L1_gnn_in['Wf'], 'L1_gnn_bf': _L1_gnn_in['bf'], 'L1_gnn_Ws': _L1_gnn_in['Ws'], 'L1_gnn_bs': _L1_gnn_in['bs'], 'L1_gnn_bn_gamma': _L1_gnn_in['bn_gamma'], 'L1_gnn_bn_beta': _L1_gnn_in['bn_beta'], 'L1_gnn_ln_gamma': _L1_gnn_in['ln_gamma'], 'L1_gnn_ln_beta': _L1_gnn_in['ln_beta'], 'L2_gnn_W': _L2_gnn_in['W'], 'L2_gnn_W_edge': _L2_gnn_in['W_edge'], 'L2_gnn_att_src': _L2_gnn_in['att_src'], 'L2_gnn_att_dst': _L2_gnn_in['att_dst'], 'L2_gnn_att_edge': _L2_gnn_in['att_edge'], 'L2_gnn_gat_bias': _L2_gnn_in['gat_bias'], 'L2_gnn_lin_W': _L2_gnn_in['lin_W'], 'L2_gnn_lin_b': _L2_gnn_in['lin_b'], 'L2_gnn_ln_g': _L2_gnn_in['ln_g'], 'L2_gnn_ln_b': _L2_gnn_in['ln_b'], 'L3_gnn_W1': _L3_gnn_in['W1'], 'L3_gnn_b1': _L3_gnn_in['b1'], 'L3_gnn_W2': _L3_gnn_in['W2'], 'L3_gnn_b2': _L3_gnn_in['b2'], 'L3_gnn_W3': _L3_gnn_in['W3'], 'L3_gnn_b3': _L3_gnn_in['b3'], 'L3_gnn_W4': _L3_gnn_in['W4'], 'L3_gnn_b4': _L3_gnn_in['b4'], 'L3_gnn_W5': _L3_gnn_in['W5'], 'L3_gnn_b5': _L3_gnn_in['b5'], 'L3_gnn_W6': _L3_gnn_in['W6'], 'L3_gnn_b6': _L3_gnn_in['b6'], 'L3_gnn_Wf': _L3_gnn_in['Wf'], 'L3_gnn_bf': _L3_gnn_in['bf']}

def reference(x, src, dst, edge_attr_16, L0_gnn_W1, L0_gnn_b1, L0_gnn_W2, L0_gnn_b2, L1_gnn_Wf, L1_gnn_bf, L1_gnn_Ws, L1_gnn_bs, L1_gnn_bn_gamma, L1_gnn_bn_beta, L1_gnn_ln_gamma, L1_gnn_ln_beta, L2_gnn_W, L2_gnn_W_edge, L2_gnn_att_src, L2_gnn_att_dst, L2_gnn_att_edge, L2_gnn_gat_bias, L2_gnn_lin_W, L2_gnn_lin_b, L2_gnn_ln_g, L2_gnn_ln_b, L3_gnn_W1, L3_gnn_b1, L3_gnn_W2, L3_gnn_b2, L3_gnn_W3, L3_gnn_b3, L3_gnn_W4, L3_gnn_b4, L3_gnn_W5, L3_gnn_b5, L3_gnn_W6, L3_gnn_b6, L3_gnn_Wf, L3_gnn_bf):
    import jax
    import jax.numpy as jnp

    def _L0_gnn_ref(x_piece, edge_index_piece, W1, b1, W2, b2):
        import jax, jax.numpy as jnp
        import numpy as np
        N_NODES = 625

        def gcn_layer(x, src, dst, W, b, n_nodes):
            h = x @ W
            deg = jax.ops.segment_sum(jnp.ones(src.shape[0], x.dtype), dst, num_segments=n_nodes) + 1.0
            dis = jax.lax.rsqrt(deg)
            norm = dis[src] * dis[dst]
            msg = h[src] * norm[:, None]
            agg = jax.ops.segment_sum(msg, dst, num_segments=n_nodes)
            agg = agg + h * (dis * dis)[:, None]
            return agg + b
        src, dst = (edge_index_piece[0], edge_index_piece[1])
        n = x_piece.shape[0]
        x = gcn_layer(x_piece, src, dst, W1, b1, n)
        x = jax.nn.relu(x)
        x = gcn_layer(x, src, dst, W2, b2, n)
        return x

    def _L1_gnn_ref(x, edge_index, edge_attr, Wf, bf, Ws, bs, bn_gamma, bn_beta, ln_gamma, ln_beta):
        import jax, jax.numpy as jnp
        import numpy as np
        N, F, ED, E = (20000, 128, 16, 9375)
        EPS = 1e-05
        n = x.shape[0]
        src, dst = (edge_index[0], edge_index[1])
        z = jnp.concatenate([x[dst], x[src], edge_attr], axis=-1)
        msg = jax.nn.sigmoid(z @ Wf.T + bf) * jax.nn.softplus(z @ Ws.T + bs)
        agg = jax.ops.segment_sum(msg, dst, num_segments=n)
        mu_b = agg.mean(axis=0)
        var_b = agg.var(axis=0)
        agg = (agg - mu_b) * jax.lax.rsqrt(var_b + EPS) * bn_gamma + bn_beta
        h = agg + x
        mu = h.mean(axis=-1, keepdims=True)
        var = h.var(axis=-1, keepdims=True)
        h = (h - mu) * jax.lax.rsqrt(var + EPS) * ln_gamma + ln_beta
        h = jax.nn.relu(h)
        return h + x

    def _L2_gnn_ref(x, edge_index, edge_attr, W, W_edge, att_src, att_dst, att_edge, gat_bias, lin_W, lin_b, ln_g, ln_b):
        import jax, jax.numpy as jnp
        import numpy as np
        N, IN, OUT, H, ED, E = (50000, 128, 128, 3, 16, 12500)
        NEG_SLOPE = 0.2
        LN_EPS = 1e-05

        def gat_block(x, edge_index, edge_attr, W, W_edge, att_src, att_dst, att_edge, gat_bias, lin_W, lin_b, ln_g, ln_b):
            row, col = (edge_index[0], edge_index[1])
            n = x.shape[0]
            deg = jax.ops.segment_sum(jnp.ones((edge_attr.shape[0],), x.dtype), col, num_segments=n)
            loop_attr = jax.ops.segment_sum(edge_attr, col, num_segments=n) / jnp.maximum(deg, 1.0)[:, None]
            loop = jnp.arange(n, dtype=row.dtype)
            row2 = jnp.concatenate([row, loop])
            col2 = jnp.concatenate([col, loop])
            ea2 = jnp.concatenate([edge_attr, loop_attr], axis=0)
            xp = (x @ W).reshape(n, H, OUT)
            a_src = jnp.einsum('nhc,hc->nh', xp, att_src)
            a_dst = jnp.einsum('nhc,hc->nh', xp, att_dst)
            ep = (ea2 @ W_edge).reshape(-1, H, OUT)
            a_edge = jnp.einsum('ehc,hc->eh', ep, att_edge)
            alpha = a_src[row2] + a_dst[col2] + a_edge
            alpha = jnp.where(alpha >= 0, alpha, NEG_SLOPE * alpha)
            m = jax.ops.segment_max(alpha, col2, num_segments=n)
            ex = jnp.exp(alpha - m[col2])
            denom = jax.ops.segment_sum(ex, col2, num_segments=n)
            attn = ex / denom[col2]
            msg = attn[:, :, None] * xp[row2]
            agg = jax.ops.segment_sum(msg, col2, num_segments=n)
            x_gat = agg.reshape(n, H * OUT) + gat_bias
            y = x_gat @ lin_W + lin_b
            h = x + y
            mu = h.mean(-1, keepdims=True)
            var = ((h - mu) ** 2).mean(-1, keepdims=True)
            return (h - mu) * jax.lax.rsqrt(var + LN_EPS) * ln_g + ln_b
        return gat_block(x, edge_index, edge_attr, W, W_edge, att_src, att_dst, att_edge, gat_bias, lin_W, lin_b, ln_g, ln_b)

    def _L3_gnn_ref(x, edge_index, batch, W1, b1, W2, b2, W3, b3, W4, b4, W5, b5, W6, b6, Wf, bf):
        import jax, jax.numpy as jnp
        import numpy as np
        N = 100000
        E = 50000
        F_IN = 128
        H = 64

        def _glorot(key, fan_in, fan_out):
            lim = jnp.sqrt(6.0 / (fan_in + fan_out))
            return jax.random.uniform(key, (fan_in, fan_out), minval=-lim, maxval=lim, dtype=jnp.float32)

        def _gcn_norm(edge_index, num_nodes):
            loop = jnp.arange(num_nodes, dtype=edge_index.dtype)
            row = jnp.concatenate([edge_index[0], loop])
            col = jnp.concatenate([edge_index[1], loop])
            deg = jax.ops.segment_sum(jnp.ones_like(col, dtype=jnp.float32), col, num_segments=num_nodes)
            dinv = jnp.where(deg > 0, jax.lax.rsqrt(deg), 0.0)
            norm = dinv[row] * dinv[col]
            return (row, col, norm)

        def _gcn_conv(h, W, b, row, col, norm, num_nodes):
            h = h @ W
            msg = h[row] * norm[:, None]
            agg = jax.ops.segment_sum(msg, col, num_segments=num_nodes)
            return agg + b
        n = x.shape[0]
        row, col, norm = _gcn_norm(edge_index, n)
        h = jax.nn.relu(_gcn_conv(x, W1, b1, row, col, norm, n))
        h = jax.nn.relu(_gcn_conv(h, W2, b2, row, col, norm, n))
        h = jax.nn.relu(_gcn_conv(h, W3, b3, row, col, norm, n))
        h = jax.nn.relu(_gcn_conv(h, W4, b4, row, col, norm, n))
        h = jax.nn.relu(_gcn_conv(h, W5, b5, row, col, norm, n))
        h = jax.nn.relu(_gcn_conv(h, W6, b6, row, col, norm, n))
        return h @ Wf + bf
    edge_index = jnp.stack([src, dst])
    batch0 = jnp.zeros((100000,), jnp.int32)
    x = _layernorm(x + _L0_gnn_ref(x, edge_index, L0_gnn_W1, L0_gnn_b1, L0_gnn_W2, L0_gnn_b2), axis=-1)
    x = _layernorm(x + _L1_gnn_ref(x, edge_index, edge_attr_16, L1_gnn_Wf, L1_gnn_bf, L1_gnn_Ws, L1_gnn_bs, L1_gnn_bn_gamma, L1_gnn_bn_beta, L1_gnn_ln_gamma, L1_gnn_ln_beta), axis=-1)
    x = _layernorm(x + _L2_gnn_ref(x, edge_index, edge_attr_16, L2_gnn_W, L2_gnn_W_edge, L2_gnn_att_src, L2_gnn_att_dst, L2_gnn_att_edge, L2_gnn_gat_bias, L2_gnn_lin_W, L2_gnn_lin_b, L2_gnn_ln_g, L2_gnn_ln_b), axis=-1)
    x = _layernorm(x + _L3_gnn_ref(x, edge_index, batch0, L3_gnn_W1, L3_gnn_b1, L3_gnn_W2, L3_gnn_b2, L3_gnn_W3, L3_gnn_b3, L3_gnn_W4, L3_gnn_b4, L3_gnn_W5, L3_gnn_b5, L3_gnn_W6, L3_gnn_b6, L3_gnn_Wf, L3_gnn_bf), axis=-1)
    return x

_drawn_inputs = setup_inputs


def setup_inputs(seed=0):
    import zlib

    import numpy as np

    out = dict(_drawn_inputs(seed))
    spreads = {'L0_gnn_b1': (0.0, 0.1),
     'L0_gnn_b2': (0.0, 0.1),
     'L1_gnn_bn_gamma': (1.0, 0.2),
     'L1_gnn_bn_beta': (0.0, 0.283),
     'L1_gnn_ln_gamma': (1.0, 0.2),
     'L1_gnn_ln_beta': (0.0, 0.318),
     'L2_gnn_gat_bias': (0.0, 0.1),
     'L2_gnn_lin_b': (0.0, 0.1),
     'L2_gnn_ln_g': (1.0, 0.2),
     'L2_gnn_ln_b': (0.0, 0.1),
     'L3_gnn_b1': (0.0, 0.683),
     'L3_gnn_b2': (0.0, 0.71),
     'L3_gnn_b3': (0.0, 0.397),
     'L3_gnn_b4': (0.0, 0.378),
     'L3_gnn_b5': (0.0, 0.1),
     'L3_gnn_b6': (0.0, 0.1),
     'L3_gnn_bf': (0.0, 0.1)}
    factors = {'L1_gnn_bf': 64.0, 'L1_gnn_bs': 64.0, 'L2_gnn_att_dst': 2.676}
    for name, (base, spread) in spreads.items():
        noise = np.random.default_rng([zlib.crc32(name.encode()), seed]).standard_normal(out[name].shape)
        drawn = base * np.exp(spread * noise) if base else spread * noise
        out[name] = jnp.asarray(drawn.astype(out[name].dtype))
    for name, factor in factors.items():
        out[name] = (out[name] * factor).astype(out[name].dtype)
    return out
```

```python
from contextlib import ExitStack

import concourse.bass as bass
from concourse import mybir

P = 128
F32 = mybir.dt.float32
I32 = mybir.dt.int32
U32 = mybir.dt.uint32
BF16 = mybir.dt.bfloat16
ALU = mybir.AluOpType
ACT = mybir.ActivationFunctionType
AX = mybir.AxisListType.X

NODE_BLOCK = 1024
J = NODE_BLOCK // P
EDGE_BLOCK = 512
CH = EDGE_BLOCK // P
DMA = 16
NOWHERE = 1 << 20
FAR = 1.0e30
EPS = 1e-5
ZERO_RUN = 2048
D = 128
AUXW = 20
ADW = 8
GATW = 132


class Block:

    def __init__(self, pair, slot, tail):
        self.pair, self.s, self.tail = pair, slot, tail
        self.n = pair * 2 + slot

    def after(self, k):
        return not isinstance(self.n, int) or self.n >= k


def pipeline(eng, blocks, stages):
    most = max(lag for _, lag in stages)
    start = most + 2 + most % 2
    end = max(start, blocks - 2)
    end -= (end - start) % 2

    def step(pair, u, last_step):
        for fn, lag in stages:
            down, slot = divmod(u - lag, 2)
            at = pair + down
            if isinstance(at, int):
                n = 2 * at + slot
                if 0 <= n < blocks:
                    fn(Block(at, slot, n == blocks - 1))
            else:
                fn(Block(at, slot, False))

    for t in range(min(start, blocks + most)):
        step(t // 2, t % 2, False)
    if end > start:
        with eng.Fori(start // 2, end // 2) as i:
            step(i, 0, False)
            step(i, 1, False)
    for t in range(end, blocks + most):
        step(t // 2, t % 2, False)


def build(nc, a, out):
    N = a["x"].shape[0]
    E = a["src"].shape[0]
    NB = -(-N // NODE_BLOCK)
    EB = -(-E // EDGE_BLOCK)
    EP = EB * EDGE_BLOCK
    node_left = N - (NB - 1) * NODE_BLOCK
    tail_p = max(p for p in range(16, P + 1, 16) if node_left % p == 0 and node_left // p <= J)
    tail_j = node_left // tail_p
    edge_left = E - (EB - 1) * EDGE_BLOCK
    assert edge_left % CH == 0
    edge_tail_p = edge_left // CH

    def pj(b):
        return (tail_p, tail_j) if b.tail else (P, J)

    def rows(table, b, width=None):
        p, j = pj(b)
        return table[bass.ds(b.n * NODE_BLOCK, p * j), :].rearrange("(p j) f -> p (j f)", p=p)

    def lanes(t, s, p, j, w=D):
        return t[0:p, s, 0:j * w]

    with ExitStack() as whole:
        def keep(name, shape, dt=F32):
            return whole.enter_context(nc.sbuf_tensor(name, shape, dt))

        def dram(name, shape, dt=F32):
            return nc.dram_tensor(name, shape, dt, kind="Internal").ap()

        def sem(name):
            return whole.enter_context(nc.semaphore(name))

        src_i = dram("src_idx", [EP // CH, CH], U32)
        dst_i = dram("dst_idx", [EP // CH, CH], U32)
        end_i = dram("end_idx", [EP // CH, CH], U32)
        aux = dram("aux", [N, AUXW])
        dinv = dram("dinv", [N, 1])
        att = dram("att", [N, ADW])
        x1, x2, x3 = (dram(f"x{i}", [N, D]) for i in (1, 2, 3))
        wide = [dram(f"wide{i}", [N, D]) for i in range(2)]
        scaled = {w: dram(f"scaled{w}", [N, w]) for w in (64, 32, 16)}
        scaled2 = {w: dram(f"scaled2_{w}", [N, w]) for w in (64, 32, 16)}
        sums = {w: dram(f"sums{w}", [N, w]) for w in (GATW, 128, 64, 32, 16)}

        gathered = [sem(f"gathered{s}") for s in range(2)]
        gathered_dst = [sem(f"gathered_dst{s}") for s in range(2)]
        scattered = [sem(f"scattered{s}") for s in range(2)]
        so_far = {s.num: 0 for s in (*gathered, *gathered_dst, *scattered)}
        setup_loaded = sem("setup_loaded")
        setup_step = sem("setup_step")
        setup_pe = sem("setup_pe")
        setup_stored = sem("setup_stored")
        src_loaded = [sem(f"src_loaded{s}") for s in range(2)]
        dst_loaded = [sem(f"dst_loaded{s}") for s in range(2)]
        end_loaded = [sem(f"end_loaded{s}") for s in range(2)]
        attr_loaded = [sem(f"attr_loaded{s}") for s in range(2)]
        zeroed = sem("zeroed")
        prepared = sem("prepared")
        evicted = sem("evicted")
        piece_loaded = sem("piece_loaded")
        compared = sem("compared")
        indexed = sem("indexed")
        turned = sem("turned")
        evacuated = sem("evacuated")
        gates_in = sem("gates_in")
        act_step = sem("act_step")
        vec_step = sem("vec_step")
        scanned = sem("scanned")
        spread = sem("spread")
        turned_back = sem("turned_back")
        rows_ready = sem("rows_ready")
        loaded = [sem(f"loaded{s}") for s in range(2)]
        loaded_b = [sem(f"loaded_b{s}") for s in range(2)]
        stored = [sem(f"stored{s}") for s in range(2)]
        multiplied = sem("multiplied")
        summed = sem("summed")
        rooted = sem("rooted")
        rooted_b = sem("rooted_b")
        normed = sem("normed")
        normed_b = sem("normed_b")
        turned_b = sem("turned_b")
        evacuated_b = sem("evacuated_b")
        multiplied_b = sem("multiplied_b")
        finished = sem("finished")
        gates_out = sem("gates_out")
        stats = [sem(f"stats{i}") for i in range(2)]
        rooted_x = [sem(f"rooted_x{i}") for i in range(2)]
        factored = [sem(f"factored{i}") for i in range(2)]
        factor_step = [sem(f"factor_step{i}") for i in range(2)]
        normed_x = [sem(f"normed_x{i}") for i in range(2)]
        gained = sem("gained")
        rectified = sem("rectified")
        scored = sem("scored")
        attended = sem("attended")
        leaked = sem("leaked")
        powered = sem("powered")
        taken = sem("taken")
        weights_ready = sem("weights_ready")
        loop_step = sem("loop_step")
        vec_step_b = sem("vec_step_b")
        vec_step_c = sem("vec_step_c")
        vec_step_d = sem("vec_step_d")
        per_pass = [setup_loaded, setup_step, setup_pe, setup_stored, *src_loaded, *dst_loaded, *end_loaded,
                    *attr_loaded, zeroed, prepared, evicted,
                    piece_loaded, compared, indexed, turned, evacuated,
                    gates_in, act_step, vec_step, scanned, spread, turned_back, rows_ready, *loaded, *loaded_b,
                    *stored, multiplied, summed, rooted, rooted_b, normed, normed_b, turned_b, evacuated_b,
                    multiplied_b, finished, gates_out, *stats, *rooted_x, *factored, *factor_step, *normed_x,
                    gained, rectified, scored, attended, leaked, powered, taken,
                    weights_ready, loop_step, vec_step_b, vec_step_c, vec_step_d]

        def past(s):
            return so_far[s.num]

        class Steps:

            def __init__(self, sem_, per):
                self.sem, self.per, self.k, self.base = sem_, per, 0, 0

            def at(self, b):
                assert self.k in (0, self.per)
                self.base, self.k = b.n * self.per, 0

            def count(self):
                self.k += 1
                assert self.k <= self.per
                return self.base + self.k

        def blocks_in(blocks, s):
            return (blocks - s + 1) // 2

        def end_pass(*pool_sems):
            for slots in pool_sems:
                for s in range(2):
                    so_far[slots[s].num] += blocks_in(EB, s) * CH * DMA
            lo = min(s.num for s in per_pass)
            hi = max(s.num for s in per_pass)
            assert hi - lo + 1 == len(per_pass)
            nc.gpsimd.sem_clear(range(lo, hi + 1))
            nc.all_engine_barrier()

        def write_zeros(eng, table, zeros):
            per = table.shape[0] * table.shape[1] // P
            run = max(f for f in range(1, ZERO_RUN + 1) if per % f == 0)
            eng.dma_start(table.rearrange("n f -> (n f)").rearrange("(p k f) -> p k f", p=P, f=run),
                          zeros[:, 0:run].unsqueeze(1).to_broadcast([P, per // run, run])).then_inc(zeroed, DMA)

        ident = keep("ident", [P, P])
        cont = keep("cont", [P, EP + 4], BF16)
        w = {}
        for name, (k, m) in {
            "L0_gnn_W1": (128, 128), "L0_gnn_W2": (128, 128), "L3_gnn_W1": (128, 64), "L3_gnn_W2": (64, 32),
            "L3_gnn_W3": (32, 16), "L3_gnn_W4": (16, 32), "L3_gnn_W5": (32, 64), "L3_gnn_W6": (64, 128),
            "L3_gnn_Wf": (128, 128),
        }.items():
            w[name] = keep("sb_" + name, [k, m])
        brow = {}
        for name in ("L0_gnn_b1", "L0_gnn_b2", "L1_gnn_ln_gamma", "L1_gnn_ln_beta", "L2_gnn_ln_g", "L2_gnn_ln_b",
                     "L3_gnn_b1", "L3_gnn_b2", "L3_gnn_b3", "L3_gnn_b4", "L3_gnn_b5", "L3_gnn_b6", "L3_gnn_bf"):
            brow[name] = keep("row_" + name, [P, a[name].shape[0]])
        gate_w = {g: [keep(f"gate_{g}{i}", [k, D]) for i, k in enumerate((D, D, 17))] for g in "fs"}
        bn_scale = keep("bn_scale", [P, D])
        bn_shift = keep("bn_shift", [P, D])
        bn_part = keep("bn_part", [P, EB * 6])
        head_w = keep("head_w", [P, 3 * D])
        score_w = keep("score_w", [P, 6])
        edge_w = keep("edge_w", [ADW + 16, 6])
        loop_w = keep("loop_w", [P, 3 * 16])
        gat_row = keep("gat_row", [P, D])
        pick = keep("pick", [3, 3 * D])

        with ExitStack() as ctx:
            def sb(name, shape, dt=F32):
                return ctx.enter_context(nc.sbuf_tensor(name, shape, dt))

            dst_a = sb("dst_a", [P, EB, CH], I32)
            dst_n = sb("dst_n", [P, EB, CH], I32)
            src_a = sb("src_a", [P, EB, CH], I32)
            end_a = sb("end_a", [P, EB, CH], I32)
            PIECE = EP // 16
            dst_b = sb("dst_b", [P, PIECE + 1], I32)
            wf = sb("wf", [P, 2 * D + 16])
            ws = sb("ws", [P, 2 * D + 16])
            gat_w = sb("gat_w", [P, 3 * D])
            gat_we = sb("gat_we", [16, 3 * D])
            att_rows = sb("att_rows", [9, D])
            att_cols = sb("att_cols", [P, 9])
            lin_w = sb("lin_w", [P, 3, D])
            gat_b = sb("gat_b", [P, 3])
            gat_bb = sb("gat_bb", [P, 3, P])
            lin_b = sb("lin_b", [P, D])
            turned_w = sb("turned_w", [P, 3, D])
            turned_we = sb("turned_we", [P, 3, 16])
            veb = sb("veb", [P, 3, P])
            zeros = sb("zeros", [P, ZERO_RUN])
            ps_a = ctx.enter_context(nc.psum_tensor("ps_a", [P, 512], F32))
            ps_b = ctx.enter_context(nc.psum_tensor("ps_b", [P, 512], F32))
            main_e = (EB - 1) * EDGE_BLOCK
            n_loads = 7 + len(w) + len(brow) + 2 + 2 + 2 + 3 + 3

            with nc.Block() as block:
                @block.gpsimd
                def _(pool):
                    nc.gpsimd.memset(ident[:, :], 0.0).then_inc(setup_step, 1)
                    nc.gpsimd.memset(pick[:, :], 0.0).then_inc(setup_step, 1)
                    nc.gpsimd.memset(edge_w[:, :], 0.0).then_inc(setup_step, 1)
                    pool.wait_ge(setup_step, 3)
                    nc.gpsimd.affine_select(out=ident[:, :], in_=ident[:, :], compare_op=ALU.not_equal, fill=1.0,
                                            base=0, pattern=[[-1, P]], channel_multiplier=1).then_inc(setup_step, 1)
                    nc.gpsimd.affine_select(out=pick[:, :].rearrange("p (h f) -> p h f", h=3),
                                            in_=pick[:, :].rearrange("p (h f) -> p h f", h=3),
                                            compare_op=ALU.not_equal, fill=1.0, base=0, pattern=[[-1, 3], [0, D]],
                                            channel_multiplier=1).then_inc(setup_step, 1)
                    nc.gpsimd.affine_select(out=edge_w[:, :], in_=edge_w[:, :],
                                            compare_op=ALU.not_equal, fill=1.0, base=0, pattern=[[-1, 6]],
                                            channel_multiplier=1).then_inc(setup_step, 1)
                    nc.gpsimd.memset(src_a[:, :, :], 0).then_inc(setup_step, 1)
                    nc.gpsimd.memset(dst_a[:, :, :], NOWHERE).then_inc(setup_step, 1)
                    nc.gpsimd.memset(dst_n[:, :, :], -1).then_inc(setup_step, 1)

                @block.sync
                def _(sp):
                    def fill(tile, table, shift):
                        n_main = EB - 1 if not shift else EB - 1
                        sp.dma_start(tile[:, 0:n_main, :],
                                     table[shift:shift + main_e].rearrange("(b p c) -> p b c", p=P, c=CH)
                                     ).then_inc(setup_loaded, DMA)
                        if not shift:
                            sp.dma_start(tile[0:edge_tail_p, EB - 1, :],
                                         table[main_e:E].rearrange("(p c) -> p c", c=CH)).then_inc(setup_loaded, DMA)
                        else:
                            sp.dma_start(tile[0:edge_tail_p - 1, EB - 1, :],
                                         table[main_e + 1:E - CH + 1].rearrange("(p c) -> p c", c=CH)
                                         ).then_inc(setup_loaded, DMA)
                            sp.dma_start(tile[edge_tail_p - 1:edge_tail_p, EB - 1, 0:CH - 1],
                                         table[E - CH + 1:E].rearrange("(p c) -> p c", p=1)
                                         ).then_inc(setup_loaded, DMA)

                    sp.wait_ge(setup_step, 9)
                    with nc.allow_non_contiguous_dma(reason="index tables, once"):
                        fill(src_a, a["src"], 0)
                        fill(dst_a, a["dst"], 0)
                        fill(dst_n, a["dst"], 1)
                        for name, t in w.items():
                            sp.dma_start(t[:, :], a[name]).then_inc(setup_loaded, DMA)
                        for name, t in brow.items():
                            sp.dma_start(t[:, :], a[name].partition_broadcast(P)).then_inc(setup_loaded, DMA)
                        sp.dma_start(wf[:, :], a["L1_gnn_Wf"]).then_inc(setup_loaded, DMA)
                        sp.dma_start(ws[:, :], a["L1_gnn_Ws"]).then_inc(setup_loaded, DMA)
                        for g, name in (("f", "L1_gnn_bf"), ("s", "L1_gnn_bs")):
                            sp.dma_start(gate_w[g][2][16:17, :], a[name].rearrange("(o d) -> o d", o=1)
                                         ).then_inc(setup_loaded, DMA)
                        sp.dma_start(gat_w[:, :], a["L2_gnn_W"]).then_inc(setup_loaded, DMA)
                        sp.dma_start(gat_we[:, :], a["L2_gnn_W_edge"]).then_inc(setup_loaded, DMA)
                        for i, name in enumerate(("L2_gnn_att_src", "L2_gnn_att_dst", "L2_gnn_att_edge")):
                            sp.dma_start(att_rows[3 * i:3 * i + 3, :], a[name]).then_inc(setup_loaded, DMA)
                        sp.dma_start(lin_w[:, :, :], a["L2_gnn_lin_W"].rearrange("(h c) o -> c h o", h=3)
                                     ).then_inc(setup_loaded, DMA)
                        sp.dma_start(gat_b[:, :], a["L2_gnn_gat_bias"].rearrange("(h c) -> c h", h=3)
                                     ).then_inc(setup_loaded, DMA)
                        sp.dma_start(lin_b[:, :], a["L2_gnn_lin_b"].partition_broadcast(P)).then_inc(setup_loaded, DMA)
                        for k in range(16):
                            lo, hi = k * PIECE, min((k + 1) * PIECE, E)
                            first = 1 if k == 0 else 0
                            if k:
                                sp.wait_ge(compared, k)
                            sp.dma_start(dst_b[:, first:hi - lo + 1],
                                         a["dst"][lo - 1 + first:hi].partition_broadcast(P)
                                         ).then_inc(piece_loaded, DMA)
                        for t, table in ((src_a, src_i), (dst_a, dst_i), (end_a, end_i)):
                            if t is src_a:
                                sp.wait_ge(setup_loaded, DMA * n_loads)
                                sp.wait_ge(indexed, 1)
                            sp.dma_start(table.rearrange("(b p) c -> p b c", p=P), t[:, :, :].bitcast(U32)
                                         ).then_inc(setup_stored, DMA)
                    sp.wait_ge(setup_stored, DMA * 3)

                def weight_steps(pe, done_moves):
                    bank = [ps_a, ps_b]

                    def emit(fn, shape, to):
                        k = len(done_moves)
                        out_ap = bank[k % 2][0:shape[0], 0:shape[1]]
                        done_moves.append((to, out_ap))
                        if pe is not None:
                            if k >= 2:
                                pe.wait_ge(evicted, k - 1)
                            fn(out_ap).then_inc(setup_pe, 1)

                    def turn(src_ap, to):
                        k, m = src_ap.shape
                        emit(lambda o: nc.tensor.transpose(o, src_ap, ident[0:k, 0:k]), (m, k), to)

                    for g, t in (("f", wf), ("s", ws)):
                        for i in range(2):
                            turn(t[:, i * D:(i + 1) * D], gate_w[g][i][:, :])
                        turn(t[:, 2 * D:2 * D + 16], gate_w[g][2][0:16, :])
                    turn(att_rows[:, :], att_cols)
                    for h in range(3):
                        turn(gat_w[:, h * D:(h + 1) * D], turned_w[:, h, :])
                    for h in range(3):
                        turn(gat_we[:, h * D:(h + 1) * D], turned_we[:, h, :])
                    if pe is not None:
                        pe.wait_ge(evicted, len(done_moves))
                    for h in range(3):
                        emit(lambda o, h=h: nc.tensor.matmul(o, turned_w[:, h, :], lin_w[:, h, :], start=True, stop=True),
                             (P, D), head_w[:, h * D:(h + 1) * D])
                    for i in range(2):
                        for h in range(3):
                            emit(lambda o, h=h, i=i: nc.tensor.matmul(
                                o, turned_w[:, h, :], att_cols[:, 3 * i + h:3 * i + h + 1], start=True, stop=True),
                                (P, 1), score_w[:, 3 * i + h:3 * i + h + 1])
                    for h in range(3):
                        emit(lambda o, h=h: nc.tensor.matmul(o, veb[:, h, :], turned_we[:, h, :], start=True, stop=True),
                             (P, 16), loop_w[:, 16 * h:16 * h + 16])

                    def lin(o):
                        for h in range(3):
                            last = nc.tensor.matmul(o, gat_bb[:, h, :], lin_w[:, h, :], start=(h == 0), stop=(h == 2))
                        return last
                    emit(lin, (P, D), gat_row)


                @block.scalar
                def _(act):
                    act.wait_ge(setup_step, 9)
                    nc.scalar.activation(zeros[:, :], ident[:, 0:1].to_broadcast([P, ZERO_RUN]), ACT.Copy, scale=0.0
                                         ).then_inc(prepared, 1)
                    act.wait_ge(prepared, 1)
                    write_zeros(act, aux, zeros)
                    act.wait_ge(zeroed, DMA)

                moves = []
                weight_steps(None, moves)

                @block.vector
                def _(dve):
                    step = Steps(vec_step, 999)
                    nc.vector.memset(cont[:, :], 0.0).then_inc(step.sem, 1)
                    dve.wait_ge(step.sem, step.count())
                    dve.wait_ge(setup_step, 9)
                    dve.wait_ge(setup_loaded, DMA * n_loads)
                    nc.vector.tensor_tensor(end_a[:, :, :], dst_a[:, :, :], dst_n[:, :, :], ALU.is_equal).then_inc(step.sem, 1)
                    dve.wait_ge(step.sem, step.count())
                    nc.vector.scalar_tensor_tensor(out=end_a[:, :, :], in0=end_a[:, :, :], scalar=float(NOWHERE),
                                                   in1=dst_a[:, :, :], op0=ALU.mult, op1=ALU.add).then_inc(step.sem, 1)
                    dve.wait_ge(step.sem, step.count())
                    nc.vector.tensor_scalar(dst_n[:, :, :], dst_a[:, :, :], float(NOWHERE), None, ALU.is_lt).then_inc(step.sem, 1)
                    dve.wait_ge(step.sem, step.count())
                    nc.vector.tensor_tensor(dst_a[:, :, :], dst_a[:, :, :], dst_n[:, :, :], ALU.mult).then_inc(step.sem, 1)
                    dve.wait_ge(step.sem, step.count())
                    dve.sem_inc(indexed, 1)
                    for g in range(3):
                        nc.vector.tensor_copy(gat_bb[:, g, :], gat_b[:, g:g + 1].to_broadcast([P, P])).then_inc(step.sem, 1)
                        dve.wait_ge(step.sem, step.count())

                    for k, (dst_ap, src_ap) in enumerate(moves):
                        dve.wait_ge(setup_pe, k + 1)
                        if dst_ap is att_cols:
                            nc.vector.tensor_copy(att_cols[:, :], src_ap).then_inc(step.sem, 1)
                            dve.wait_ge(step.sem, step.count())
                            for h in range(3):
                                nc.vector.tensor_copy(veb[:, h, :], att_cols[:, 6 + h:7 + h].to_broadcast([P, P])).then_inc(step.sem, 1)
                                dve.wait_ge(step.sem, step.count())
                        elif dst_ap is gat_row:
                            nc.vector.tensor_tensor(gat_row[:, :], src_ap, lin_b[:, :], ALU.add).then_inc(step.sem, 1)
                            dve.wait_ge(step.sem, step.count())
                        else:
                            nc.vector.tensor_copy(dst_ap, src_ap).then_inc(step.sem, 1)
                            dve.wait_ge(step.sem, step.count())
                        dve.sem_inc(evicted, 1)
                    for k in range(16):
                        lo, hi = k * PIECE, min((k + 1) * PIECE, E)
                        first = 1 if k == 0 else 0
                        dve.wait_ge(piece_loaded, DMA * (k + 1))
                        nc.vector.tensor_tensor(cont[:, lo + first:hi], dst_b[:, 1 + first:hi - lo + 1],
                                                dst_b[:, first:hi - lo], ALU.is_equal).then_inc(step.sem, 1)
                        dve.wait_ge(step.sem, step.count())
                        dve.sem_inc(compared, 1)

                @block.tensor
                def _(pe):
                    pe.wait_ge(setup_step, 9)
                    pe.wait_ge(setup_loaded, DMA * n_loads)
                    pe.wait_ge(vec_step, 8)
                    weight_steps(pe, [])

            end_pass()
            with nc.Block() as block:
                @block.sync
                def _(sp):
                    with nc.allow_non_contiguous_dma(reason="48 numbers"):
                        sp.dma_start(dinv[0:48, :].rearrange("n o -> o n"), loop_w[0:1, :]).then_inc(setup_stored, DMA)
                        sp.wait_ge(setup_stored, DMA)
                        sp.dma_start(edge_w[ADW:ADW + 16, 0:3], dinv[0:48, :].rearrange("(h k) o -> k (h o)", h=3)
                                     ).then_inc(setup_stored, DMA)
                        sp.wait_ge(setup_stored, 2 * DMA)
            end_pass()

        def edge_sum_pass(tag, width, table, sum_table, from_attr=False, zero=()):
            with ExitStack() as ctx:
                def sb(name, shape, dt=F32):
                    return ctx.enter_context(nc.sbuf_tensor(f"{tag}_{name}", shape, dt))

                def ps(name, shape):
                    return ctx.enter_context(nc.psum_tensor(f"{tag}_{name}", shape, F32))

                src_s = [sb(f"src{s}", [P, CH], U32) for s in range(2)]
                end_s = [sb(f"end{s}", [P, CH], U32) for s in range(2)]
                got = [sb(f"got{s}", [P, CH, width]) for s in range(2)]
                run = [sb(f"run{s}", [width, EDGE_BLOCK]) for s in range(2)]
                res = [sb(f"res{s}", [P, CH, width]) for s in range(2)]
                zeros = sb("zeros", [P, ZERO_RUN])
                p_in = [ps(f"p_in{s}", [P, EDGE_BLOCK]) for s in range(2)]
                p_out = [ps(f"p_out{s}", [P, CH * width]) for s in range(2)]
                got_sem, got_count = (attr_loaded, DMA) if from_attr else (gathered, CH * DMA)
                got_before = [0, 0] if from_attr else [past(gathered[s]) for s in range(2)]

                with nc.Block() as block:
                    @block.sync
                    def _(sp):
                        def load_src(b):
                            if b.after(2):
                                sp.wait_ge(gathered[b.s], past(gathered[b.s]) + b.pair * CH * DMA)
                                sp.nop(nofuse=True)
                            sp.dma_start(src_s[b.s][:, :], src_i[bass.ds(b.n * P, P), :]).then_inc(src_loaded[b.s], DMA)

                        def load_attr(b):
                            sp.wait_ge(prepared, 2)
                            if b.after(2):
                                sp.wait_ge(turned, b.n - 1)
                                sp.nop(nofuse=True)
                            p = edge_tail_p if b.tail else P
                            sp.dma_start(got[b.s][0:p, :, 0:16], a["edge_attr_16"][bass.ds(b.n * EDGE_BLOCK, p * CH), :]
                                         .rearrange("(p c) f -> p c f", p=p)).then_inc(attr_loaded[b.s], DMA)

                        def load_end(b):
                            if b.after(2):
                                sp.wait_ge(scattered[b.s], past(scattered[b.s]) + b.pair * CH * DMA)
                                sp.nop(nofuse=True)
                            sp.dma_start(end_s[b.s][:, :], end_i[bass.ds(b.n * P, P), :]).then_inc(end_loaded[b.s], DMA)

                        pipeline(sp, EB, [(load_attr if from_attr else load_src, 0), (load_end, 2)])

                    @block.gpsimd
                    def _(pool):
                        def gather(b):
                            pool.wait_ge(src_loaded[b.s], (b.pair + 1) * DMA)
                            pool.nop(nofuse=True)
                            if b.after(2):
                                pool.wait_ge(turned, b.n - 1)
                                pool.nop(nofuse=True)
                            for j in range(CH):
                                pool.indirect_dma_start(
                                    got[b.s][:, j, :], None, table,
                                    bass.IndirectOffsetOnAxis(ap=src_s[b.s][:, j:j + 1], axis=0)
                                ).then_inc(gathered[b.s], DMA)

                        def scatter(b):
                            pool.wait_ge(end_loaded[b.s], (b.pair + 1) * DMA)
                            pool.nop(nofuse=True)
                            pool.wait_ge(rows_ready, b.n + 1)
                            pool.nop(nofuse=True)
                            for j in range(CH):
                                pool.indirect_dma_start(
                                    sum_table, bass.IndirectOffsetOnAxis(ap=end_s[b.s][:, j:j + 1], axis=0),
                                    res[b.s][:, j, :], None, bounds_check=N - 1, oob_is_err=False
                                ).then_inc(scattered[b.s], DMA)

                        pipeline(pool, EB, [(scatter, 2)] if from_attr else [(gather, 0), (scatter, 2)])
                        for s in range(2):
                            pool.wait_ge(scattered[s], past(scattered[s]) + blocks_in(EB, s) * CH * DMA)

                    @block.tensor
                    def _(pe):
                        def turn(b):
                            pe.wait_ge(got_sem[b.s], got_before[b.s] + (b.pair + 1) * got_count)
                            pe.nop(nofuse=True)
                            if b.after(2):
                                pe.wait_ge(scanned, b.n - 1)
                                pe.nop(nofuse=True)
                            for j in range(CH):
                                last = nc.tensor.transpose(p_in[b.s][0:width, j:EDGE_BLOCK:CH], got[b.s][:, j, :],
                                                           ident[:, :])
                            last.then_inc(turned, 1)

                        def turn_back(b):
                            pe.wait_ge(scanned, b.n + 1)
                            pe.nop(nofuse=True)
                            if b.after(2):
                                pe.wait_ge(rows_ready, b.n - 1)
                                pe.nop(nofuse=True)
                            for j in range(CH):
                                last = nc.tensor.transpose(p_out[b.s][:, j * width:(j + 1) * width],
                                                           run[b.s][:, j:EDGE_BLOCK:CH], ident[0:width, 0:width])
                            last.then_inc(turned_back, 1)

                        pipeline(pe, EB, [(turn, 0), (turn_back, 1)])

                    @block.vector
                    def _(dve):
                        def scan(b):
                            dve.wait_ge(turned, b.n + 1)
                            dve.nop(nofuse=True)
                            if b.after(2):
                                dve.wait_ge(turned_back, b.n - 1)
                                dve.nop(nofuse=True)
                            if b.after(1):
                                dve.wait_ge(scanned, b.n)
                                dve.nop(nofuse=True)
                            first = isinstance(b.n, int) and b.n == 0
                            nc.vector.tensor_tensor_scan(
                                run[b.s][:, :], cont[0:width, bass.ds(b.n * EDGE_BLOCK, EDGE_BLOCK)],
                                p_in[b.s][0:width, :],
                                0.0 if first else run[1 - b.s][:, EDGE_BLOCK - 1:EDGE_BLOCK],
                                ALU.mult, ALU.add).then_inc(scanned, 1)

                        pipeline(dve, EB, [(scan, 0)])

                    @block.scalar
                    def _(act):
                        def copy_rows(b):
                            act.wait_ge(turned_back, b.n + 1)
                            act.nop(nofuse=True)
                            if b.after(2):
                                act.wait_ge(scattered[b.s], past(scattered[b.s]) + b.pair * CH * DMA)
                                act.nop(nofuse=True)
                            nc.scalar.copy(res[b.s][:, :, :].rearrange("p c f -> p (c f)"), p_out[b.s][:, :]
                                           ).then_inc(rows_ready, 1)

                        def fill(ap, value):
                            nc.scalar.activation(ap, ident[:, 0:1].to_broadcast(list(ap.shape)), ACT.Copy, scale=0.0,
                                                 bias=value).then_inc(prepared, 1)

                        if from_attr:
                            for s in range(2):
                                fill(got[s][:, :, :].rearrange("p c f -> p (c f)"), 1.0)
                        if zero:
                            fill(zeros[:, :], 0.0)
                            act.wait_ge(prepared, 3 if from_attr else 1)
                            for z in zero:
                                write_zeros(act, z, zeros)
                        pipeline(act, EB, [(copy_rows, 0)])
                        if zero:
                            act.wait_ge(zeroed, DMA * len(zero))
            end_pass(scattered, *([] if from_attr else [gathered]))


        def per_row(t, p, j, width):
            return t[0:p, 0:j].unsqueeze(2).to_broadcast([p, j, width])

        def split(t, p, j, width=D):
            return t[0:p, 0:j * width].rearrange("p (j f) -> p j f", f=width)

        def turn_rows(dst_psum, tile, p, j, width):
            for q in range(j):
                last = nc.tensor.transpose(dst_psum[0:width, q * P:q * P + p], tile[0:p, q * width:(q + 1) * width],
                                           ident[0:p, 0:p])
            return last

        def times_weight(dst_psum, turned_tile, weight, p, j, k, width):
            for q in range(j):
                last = nc.tensor.matmul(dst_psum[0:p, q * width:(q + 1) * width], turned_tile[0:k, q * P:q * P + p],
                                        weight, start=True, stop=True)
            return last

        def cols(t, k, p, j):
            return t[0:k, 0:j * P].rearrange("k (j p) -> k j p", p=P)[:, :, 0:p]

        def row_stats(link, v, stats, mv, p, j):
            for q in range(j):
                last = nc.vector.bn_stats(stats[0:p, q * 6:q * 6 + 6], v[0:p, q * D:(q + 1) * D])
            last.then_inc(link.sem, 1)
            nc.vector.wait_ge(link.sem, link.count())
            nc.vector.nop(nofuse=True)
            for q in range(j):
                last = nc.vector.bn_aggr(mv[0:p, q * 2:q * 2 + 2], stats[0:p, q * 6:q * 6 + 6])
            last.then_inc(link.sem, 1)
            nc.vector.wait_ge(link.sem, link.count())
            nc.vector.nop(nofuse=True)

        def scale_rows(v_out, v_in, rstd, nmr, p, j):
            for q in range(j):
                last = nc.scalar.activation(v_out[0:p, q * D:(q + 1) * D], v_in[0:p, q * D:(q + 1) * D], ACT.Identity,
                                            bias=nmr[0:p, q:q + 1], scale=rstd[0:p, q:q + 1])
            return last

        class Norm:

            def __init__(self, sb, name):
                self.stats = [sb(f"{name}_stats{s}", [P, J * 6]) for s in range(2)]
                self.mv = [sb(f"{name}_mv{s}", [P, J * 2]) for s in range(2)]
                self.var = [sb(f"{name}_var{s}", [P, J]) for s in range(2)]
                self.sd = [sb(f"{name}_sd{s}", [P, J]) for s in range(2)]
                self.rstd = [sb(f"{name}_rstd{s}", [P, J]) for s in range(2)]
                self.nmr = [sb(f"{name}_nmr{s}", [P, J]) for s in range(2)]

            def variance(self, link, v, b, ready):
                p, j = pj(b)
                row_stats(link, v, self.stats[b.s], self.mv[b.s], p, j)
                nc.vector.tensor_scalar(self.var[b.s][0:p, 0:j], self.mv[b.s][0:p, 1:2 * j:2], EPS, None,
                                        ALU.add).then_inc(ready, 1)

            def root(self, b, ready):
                p, j = pj(b)
                nc.scalar.activation(self.sd[b.s][0:p, 0:j], self.var[b.s][0:p, 0:j], ACT.Sqrt).then_inc(ready, 1)

            def factors(self, link, b, ready):
                p, j = pj(b)
                nc.vector.reciprocal(self.rstd[b.s][0:p, 0:j], self.sd[b.s][0:p, 0:j]).then_inc(link.sem, 1)
                nc.vector.wait_ge(link.sem, link.count())
                nc.vector.nop(nofuse=True)
                nc.vector.scalar_tensor_tensor(out=self.nmr[b.s][0:p, 0:j], in0=self.mv[b.s][0:p, 0:2 * j:2],
                                               scalar=-1.0, in1=self.rstd[b.s][0:p, 0:j], op0=ALU.mult,
                                               op1=ALU.mult).then_inc(ready, 1)

        def degree_pass():
            with ExitStack() as ctx:
                def sb(name, shape, dt=F32):
                    return ctx.enter_context(nc.sbuf_tensor("deg_" + name, shape, dt))

                aux_s = [sb(f"aux{s}", [P, J * AUXW]) for s in range(2)]
                x_s = [sb(f"x{s}", [P, J * D]) for s in range(2)]
                o_s = [sb(f"o{s}", [P, J * D]) for s in range(2)]
                deg = [sb(f"deg{s}", [P, J]) for s in range(2)]
                root = [sb(f"root{s}", [P, J]) for s in range(2)]
                inv = [sb(f"inv{s}", [P, J]) for s in range(2)]
                with nc.Block() as block:
                    @block.sync
                    def _(sp):
                        def load(b):
                            p, j = pj(b)
                            if b.after(2):
                                sp.wait_ge(summed, b.n - 1)
                                sp.nop(nofuse=True)
                            sp.dma_start(aux_s[b.s][0:p, 0:j * AUXW], rows(aux, b)).then_inc(loaded[b.s], DMA)
                            sp.dma_start(x_s[b.s][0:p, 0:j * D], rows(a["x"], b)).then_inc(loaded[b.s], DMA)

                        def store(b):
                            p, j = pj(b)
                            sp.wait_ge(summed, b.n + 1)
                            sp.nop(nofuse=True)
                            sp.dma_start(rows(wide[0], b), o_s[b.s][0:p, 0:j * D]).then_inc(stored[b.s], DMA)
                            sp.dma_start(rows(dinv, b), inv[b.s][0:p, 0:j]).then_inc(stored[b.s], DMA)

                        pipeline(sp, NB, [(load, 0), (store, 1)])
                        for s in range(2):
                            sp.wait_ge(stored[s], blocks_in(NB, s) * 2 * DMA)

                    @block.vector
                    def _(dve):
                        link = Steps(vec_step, 1)

                        def degree(b):
                            p, j = pj(b)
                            dve.wait_ge(loaded[b.s], (b.pair + 1) * 2 * DMA)
                            dve.nop(nofuse=True)
                            if b.after(2):
                                dve.wait_ge(rooted, b.n - 1)
                                dve.nop(nofuse=True)
                            nc.vector.tensor_scalar(deg[b.s][0:p, 0:j], aux_s[b.s][0:p, 16:j * AUXW:AUXW], 1.0, None,
                                                    ALU.add).then_inc(normed, 1)

                        def scale(b):
                            p, j = pj(b)
                            link.at(b)
                            dve.wait_ge(rooted, b.n + 1)
                            dve.nop(nofuse=True)
                            if b.after(2):
                                dve.wait_ge(stored[b.s], b.pair * 2 * DMA)
                                dve.nop(nofuse=True)
                            nc.vector.reciprocal(inv[b.s][0:p, 0:j], root[b.s][0:p, 0:j]).then_inc(link.sem, 1)
                            dve.wait_ge(link.sem, link.count())
                            dve.nop(nofuse=True)
                            nc.vector.tensor_tensor(split(o_s[b.s], p, j), split(x_s[b.s], p, j),
                                                    per_row(inv[b.s], p, j, D), ALU.mult).then_inc(summed, 1)

                        pipeline(dve, NB, [(degree, 0), (scale, 1)])

                    @block.scalar
                    def _(act):
                        def take_root(b):
                            p, j = pj(b)
                            act.wait_ge(normed, b.n + 1)
                            act.nop(nofuse=True)
                            if b.after(2):
                                act.wait_ge(summed, b.n - 1)
                                act.nop(nofuse=True)
                            nc.scalar.activation(root[b.s][0:p, 0:j], deg[b.s][0:p, 0:j], ACT.Sqrt).then_inc(rooted, 1)

                        pipeline(act, NB, [(take_root, 0)])
            end_pass()

        def aggregate_then_weight_pass(tag, own, sum_table, weight, bias, k, m, to, to_width, residual=None, last_w=None,
                                       last_bias=None):
            with ExitStack() as ctx:
                def sb(name, shape, dt=F32):
                    return ctx.enter_context(nc.sbuf_tensor(f"{tag}_{name}", shape, dt))

                def ps(name, shape):
                    return ctx.enter_context(nc.psum_tensor(f"{tag}_{name}", shape, F32))

                own_s = [sb(f"own{s}", [P, J * k]) for s in range(2)]
                sum_s = [sb(f"sum{s}", [P, J * k]) for s in range(2)]
                inv = [sb(f"inv{s}", [P, J]) for s in range(2)]
                u_t = [sb(f"u_t{s}", [k, J * P]) for s in range(2)]
                z_s = [sb(f"z{s}", [P, J * m]) for s in range(2)]
                o_s = [sb(f"o{s}", [P, J * to_width]) for s in range(2)]
                if residual is not None:
                    res_s = [sb(f"res{s}", [P, J * D]) for s in range(2)]
                    norm = Norm(sb, "norm")
                if last_w is not None:
                    h_t = [sb(f"h_t{s}", [P, J * P]) for s in range(2)]
                    y_s = [sb(f"y{s}", [P, J * D]) for s in range(2)]
                    p_h = ps("p_h", [P, J * P])
                    p_y = ps("p_y", [P, J * D])
                p_u = ps("p_u", [P, J * P])
                p_z = ps("p_z", [P, J * m])
                loads = 3 + (residual is not None)

                with nc.Block() as block:
                    @block.sync
                    def _(sp):
                        def load(b):
                            p, j = pj(b)
                            if b.after(2):
                                sp.wait_ge(summed, b.n - 1)
                                sp.nop(nofuse=True)
                            if b.after(2):
                                sp.wait_ge(finished, b.n - 1)
                                sp.nop(nofuse=True)
                            sp.dma_start(own_s[b.s][0:p, 0:j * k], rows(own, b)).then_inc(loaded[b.s], DMA)
                            sp.dma_start(sum_s[b.s][0:p, 0:j * k], rows(sum_table, b)).then_inc(loaded[b.s], DMA)
                            sp.dma_start(inv[b.s][0:p, 0:j], rows(dinv, b)).then_inc(loaded[b.s], DMA)
                            if residual is not None:
                                sp.dma_start(res_s[b.s][0:p, 0:j * D], rows(residual, b)).then_inc(loaded[b.s], DMA)

                        def store(b):
                            p, j = pj(b)
                            sp.wait_ge(finished, b.n + 1)
                            sp.nop(nofuse=True)
                            sp.dma_start(rows(to, b), o_s[b.s][0:p, 0:j * to_width]).then_inc(stored[b.s], DMA)

                        pipeline(sp, NB, [(store, 2), (load, 0)])
                        for s in range(2):
                            sp.wait_ge(stored[s], blocks_in(NB, s) * DMA)

                    @block.vector
                    def _(dve):
                        link = Steps(vec_step, 4 if residual is not None else 0)

                        def add(b):
                            p, j = pj(b)
                            dve.wait_ge(loaded[b.s], (b.pair + 1) * loads * DMA)
                            dve.nop(nofuse=True)
                            nc.vector.tensor_tensor(own_s[b.s][0:p, 0:j * k], own_s[b.s][0:p, 0:j * k],
                                                    sum_s[b.s][0:p, 0:j * k], ALU.add).then_inc(act_step, 1)

                        def bias_rows(b):
                            p, j = pj(b)
                            dve.wait_ge(multiplied, b.n + 1)
                            dve.nop(nofuse=True)
                            if b.after(2):
                                dve.wait_ge(finished, b.n - 1)
                                dve.nop(nofuse=True)
                            for q in range(j):
                                last = nc.vector.scalar_tensor_tensor(
                                    out=z_s[b.s][0:p, q * m:(q + 1) * m], in0=p_z[0:p, q * m:(q + 1) * m],
                                    scalar=inv[b.s][0:p, q:q + 1], in1=bias[0:p, :], op0=ALU.mult, op1=ALU.add)
                            last.then_inc(normed, 1)

                        def add_residual(b):
                            p, j = pj(b)
                            link.at(b)
                            if last_w is None:
                                dve.wait_ge(normed, b.n + 1)
                                dve.nop(nofuse=True)
                                nc.vector.tensor_tensor(z_s[b.s][0:p, 0:j * m], z_s[b.s][0:p, 0:j * m],
                                                        res_s[b.s][0:p, 0:j * D], ALU.add).then_inc(link.sem, 1)
                                dve.wait_ge(link.sem, link.count())
                                dve.nop(nofuse=True)
                                norm.variance(link, z_s[b.s], b, rooted)
                            else:
                                dve.wait_ge(multiplied_b, b.n + 1)
                                dve.nop(nofuse=True)
                                nc.vector.tensor_tensor(split(y_s[b.s], p, j), split(p_y, p, j),
                                                        last_bias[0:p, :].unsqueeze(1).to_broadcast([p, j, D]),
                                                        ALU.add).then_inc(link.sem, 1)
                                dve.wait_ge(link.sem, link.count())
                                dve.nop(nofuse=True)
                                nc.vector.tensor_tensor(y_s[b.s][0:p, 0:j * D], y_s[b.s][0:p, 0:j * D],
                                                        res_s[b.s][0:p, 0:j * D], ALU.add).then_inc(link.sem, 1)
                                dve.wait_ge(link.sem, link.count())
                                dve.nop(nofuse=True)
                                norm.variance(link, y_s[b.s], b, rooted)

                        def factors(b):
                            dve.wait_ge(rooted_b, b.n + 1)
                            dve.nop(nofuse=True)
                            norm.factors(link2, b, normed_b)

                        link.per = 3 if last_w is None else 4
                        link2 = Steps(gates_in, 1)

                        def factors_at(b):
                            link2.at(b)
                            factors(b)

                        stages = [(add, 0), (bias_rows, 1)]
                        if last_w is not None:
                            stages = [(add_residual, 2), (factors_at, 2), *stages]
                        elif residual is not None:
                            stages += [(add_residual, 1), (factors_at, 1)]
                        pipeline(dve, NB, stages)

                    @block.tensor
                    def _(pe):
                        def turn(b):
                            p, j = pj(b)
                            pe.wait_ge(act_step, b.n + 1)
                            pe.nop(nofuse=True)
                            if b.after(1):
                                pe.wait_ge(evacuated, b.n)
                                pe.nop(nofuse=True)
                            turn_rows(p_u, own_s[b.s], p, j, k).then_inc(summed, 1)

                        def multiply(b):
                            p, j = pj(b)
                            pe.wait_ge(evacuated, b.n + 1)
                            pe.nop(nofuse=True)
                            if b.after(1):
                                pe.wait_ge(normed, b.n)
                                pe.nop(nofuse=True)
                            times_weight(p_z, u_t[b.s], weight[:, :], p, j, k, m).then_inc(multiplied, 1)

                        def turn_h(b):
                            p, j = pj(b)
                            pe.wait_ge(spread, b.n + 1)
                            pe.nop(nofuse=True)
                            if b.after(1):
                                pe.wait_ge(evacuated_b, b.n)
                                pe.nop(nofuse=True)
                            turn_rows(p_h, z_s[b.s], p, j, D).then_inc(turned_b, 1)

                        def multiply_h(b):
                            p, j = pj(b)
                            pe.wait_ge(evacuated_b, b.n + 1)
                            pe.nop(nofuse=True)
                            if b.after(1):
                                pe.wait_ge(rooted, b.n)
                                pe.nop(nofuse=True)
                            times_weight(p_y, h_t[b.s], last_w[:, :], p, j, D, D).then_inc(multiplied_b, 1)

                        stages = [(turn, 0), (multiply, 0)]
                        if last_w is not None:
                            stages = [(turn, 0), (multiply, 0), (turn_h, 1), (multiply_h, 1)]
                        pipeline(pe, NB, stages)

                    @block.scalar
                    def _(act):
                        def evacuate(b):
                            p, j = pj(b)
                            act.wait_ge(summed, b.n + 1)
                            act.nop(nofuse=True)
                            if b.after(2):
                                act.wait_ge(multiplied, b.n - 1)
                                act.nop(nofuse=True)
                            nc.scalar.copy(cols(u_t[b.s], k, p, j), cols(p_u, k, p, j)).then_inc(evacuated, 1)

                        def relu_scale(b):
                            p, j = pj(b)
                            act.wait_ge(normed, b.n + 1)
                            act.nop(nofuse=True)
                            if b.after(2):
                                act.wait_ge(stored[b.s], b.pair * DMA)
                                act.nop(nofuse=True)
                            for q in range(j):
                                last = nc.scalar.activation(o_s[b.s][0:p, q * m:(q + 1) * m],
                                                            z_s[b.s][0:p, q * m:(q + 1) * m], ACT.Relu,
                                                            scale=inv[b.s][0:p, q:q + 1])
                            last.then_inc(finished, 1)

                        def relu(b):
                            p, j = pj(b)
                            act.wait_ge(normed, b.n + 1)
                            act.nop(nofuse=True)
                            nc.scalar.activation(z_s[b.s][0:p, 0:j * D], z_s[b.s][0:p, 0:j * D], ACT.Relu
                                                 ).then_inc(spread, 1)

                        def evacuate_h(b):
                            p, j = pj(b)
                            act.wait_ge(turned_b, b.n + 1)
                            act.nop(nofuse=True)
                            if b.after(2):
                                act.wait_ge(multiplied_b, b.n - 1)
                                act.nop(nofuse=True)
                            nc.scalar.copy(cols(h_t[b.s], D, p, j), cols(p_h, D, p, j)).then_inc(evacuated_b, 1)

                        def root(b):
                            act.wait_ge(rooted, b.n + 1)
                            act.nop(nofuse=True)
                            if b.after(2):
                                act.wait_ge(normed_b, b.n - 1)
                                act.nop(nofuse=True)
                            norm.root(b, rooted_b)

                        def normalise(b):
                            p, j = pj(b)
                            v = z_s if last_w is None else y_s
                            act.wait_ge(normed_b, b.n + 1)
                            act.nop(nofuse=True)
                            if b.after(2):
                                act.wait_ge(stored[b.s], b.pair * DMA)
                                act.nop(nofuse=True)
                            scale_rows(o_s[b.s], v[b.s], norm.rstd[b.s], norm.nmr[b.s], p, j).then_inc(finished, 1)

                        if residual is None:
                            stages = [(evacuate, 0), (relu_scale, 1)]
                        elif last_w is None:
                            stages = [(evacuate, 0), (root, 1), (normalise, 1)]
                        else:
                            stages = [(root, 2), (normalise, 2), (evacuate, 0), (relu, 1), (evacuate_h, 1)]
                        pipeline(act, NB, stages)
            end_pass()

        def aggregate_last_pass(tag, own, sum_table, bias, k, weight, m, to):
            with ExitStack() as ctx:
                def sb(name, shape, dt=F32):
                    return ctx.enter_context(nc.sbuf_tensor(f"{tag}_{name}", shape, dt))

                def ps(name, shape):
                    return ctx.enter_context(nc.psum_tensor(f"{tag}_{name}", shape, F32))

                own_s = [sb(f"own{s}", [P, J * k]) for s in range(2)]
                sum_s = [sb(f"sum{s}", [P, J * k]) for s in range(2)]
                inv = [sb(f"inv{s}", [P, J]) for s in range(2)]
                h_s = [sb(f"h{s}", [P, J * k]) for s in range(2)]
                h_t = [sb(f"h_t{s}", [k, J * P]) for s in range(2)]
                o_s = [sb(f"o{s}", [P, J * m]) for s in range(2)]
                p_h = ps("p_h", [P, J * P])
                p_z = ps("p_z", [P, J * m])

                with nc.Block() as block:
                    @block.sync
                    def _(sp):
                        def load(b):
                            p, j = pj(b)
                            if b.after(2):
                                sp.wait_ge(summed, b.n - 1)
                                sp.nop(nofuse=True)
                            if b.after(2):
                                sp.wait_ge(finished, b.n - 1)
                                sp.nop(nofuse=True)
                            sp.dma_start(own_s[b.s][0:p, 0:j * k], rows(own, b)).then_inc(loaded[b.s], DMA)
                            sp.dma_start(sum_s[b.s][0:p, 0:j * k], rows(sum_table, b)).then_inc(loaded[b.s], DMA)
                            sp.dma_start(inv[b.s][0:p, 0:j], rows(dinv, b)).then_inc(loaded[b.s], DMA)

                        def store(b):
                            p, j = pj(b)
                            sp.wait_ge(finished, b.n + 1)
                            sp.nop(nofuse=True)
                            sp.dma_start(rows(to, b), o_s[b.s][0:p, 0:j * m]).then_inc(stored[b.s], DMA)

                        pipeline(sp, NB, [(store, 2), (load, 0)])
                        for s in range(2):
                            sp.wait_ge(stored[s], blocks_in(NB, s) * DMA)

                    @block.vector
                    def _(dve):
                        link = Steps(vec_step, 2)

                        def add(b):
                            p, j = pj(b)
                            link.at(b)
                            dve.wait_ge(loaded[b.s], (b.pair + 1) * 3 * DMA)
                            dve.nop(nofuse=True)
                            if b.after(2):
                                dve.wait_ge(spread, b.n - 1)
                                dve.nop(nofuse=True)
                            if b.after(2):
                                dve.wait_ge(finished, b.n - 1)
                                dve.nop(nofuse=True)
                            nc.vector.tensor_tensor(own_s[b.s][0:p, 0:j * k], own_s[b.s][0:p, 0:j * k],
                                                    sum_s[b.s][0:p, 0:j * k], ALU.add).then_inc(link.sem, 1)
                            dve.wait_ge(link.sem, link.count())
                            dve.nop(nofuse=True)
                            nc.vector.tensor_tensor(split(own_s[b.s], p, j, k), split(own_s[b.s], p, j, k),
                                                    per_row(inv[b.s], p, j, k), ALU.mult).then_inc(link.sem, 1)
                            dve.wait_ge(link.sem, link.count())
                            dve.nop(nofuse=True)
                            nc.vector.tensor_tensor(split(h_s[b.s], p, j, k), split(own_s[b.s], p, j, k),
                                                    bias[0:p, :].unsqueeze(1).to_broadcast([p, j, k]), ALU.add
                                                    ).then_inc(summed, 1)

                        def scale(b):
                            p, j = pj(b)
                            source = split(h_s[b.s], p, j, k) if weight is None else split(p_z, p, j, m)
                            dve.wait_ge(spread if weight is None else multiplied, b.n + 1)
                            dve.nop(nofuse=True)
                            if b.after(2):
                                dve.wait_ge(stored[b.s], b.pair * DMA)
                                dve.nop(nofuse=True)
                            nc.vector.tensor_tensor(split(o_s[b.s], p, j, m), source, per_row(inv[b.s], p, j, m),
                                                    ALU.mult).then_inc(finished, 1)

                        pipeline(dve, NB, [(add, 0), (scale, 1)])

                    @block.scalar
                    def _(act):
                        def relu(b):
                            p, j = pj(b)
                            act.wait_ge(summed, b.n + 1)
                            act.nop(nofuse=True)
                            nc.scalar.activation(h_s[b.s][0:p, 0:j * k], h_s[b.s][0:p, 0:j * k], ACT.Relu
                                                 ).then_inc(spread, 1)

                        def evacuate(b):
                            p, j = pj(b)
                            act.wait_ge(turned, b.n + 1)
                            act.nop(nofuse=True)
                            if b.after(2):
                                act.wait_ge(multiplied, b.n - 1)
                                act.nop(nofuse=True)
                            nc.scalar.copy(cols(h_t[b.s], k, p, j), cols(p_h, k, p, j)).then_inc(evacuated, 1)

                        pipeline(act, NB, [(relu, 0)] if weight is None else [(relu, 0), (evacuate, 0)])

                    if weight is not None:
                        @block.tensor
                        def _(pe):
                            def turn(b):
                                p, j = pj(b)
                                pe.wait_ge(spread, b.n + 1)
                                pe.nop(nofuse=True)
                                if b.after(1):
                                    pe.wait_ge(evacuated, b.n)
                                    pe.nop(nofuse=True)
                                turn_rows(p_h, h_s[b.s], p, j, k).then_inc(turned, 1)

                            def multiply(b):
                                p, j = pj(b)
                                pe.wait_ge(evacuated, b.n + 1)
                                pe.nop(nofuse=True)
                                if b.after(1):
                                    pe.wait_ge(finished, b.n)
                                    pe.nop(nofuse=True)
                                times_weight(p_z, h_t[b.s], weight[:, :], p, j, k, m).then_inc(multiplied, 1)

                            pipeline(pe, NB, [(turn, 0), (multiply, 0)])
            end_pass()

        edge_sum_pass("count", AUXW, None, aux, from_attr=True, zero=[sums[D]])
        degree_pass()
        edge_sum_pass("g1", D, wide[0], sums[D], zero=[sums[GATW]])
        aggregate_then_weight_pass("n1", wide[0], sums[D], w["L0_gnn_W1"], brow["L0_gnn_b1"], D, D, wide[1], D)
        edge_sum_pass("g2", D, wide[1], sums[D], zero=[sums[64], sums[32], sums[16]])
        aggregate_then_weight_pass("n2", wide[1], sums[D], w["L0_gnn_W2"], brow["L0_gnn_b2"], D, D, x1, D,
                                   residual=a["x"])

        def gated_edge_pass():
            with ExitStack() as ctx:
                def sb(name, shape, dt=F32):
                    return ctx.enter_context(nc.sbuf_tensor(f"cg_{name}", shape, dt))

                def ps(name, shape):
                    return ctx.enter_context(nc.psum_tensor(f"cg_{name}", shape, F32))

                two = range(2)
                src_s = [sb(f"src{s}", [P, CH], U32) for s in two]
                dst_s = [sb(f"dst{s}", [P, CH], U32) for s in two]
                end_s = [sb(f"end{s}", [P, CH], U32) for s in two]
                got_s = [sb(f"got_src{s}", [P, CH, D]) for s in two]
                got_d = [sb(f"got_dst{s}", [P, CH, D]) for s in two]
                attr = [sb(f"attr{s}", [P, CH, 17]) for s in two]
                t_d = [sb(f"t_d{s}", [D, EDGE_BLOCK]) for s in two]
                t_s = [sb(f"t_s{s}", [D, EDGE_BLOCK]) for s in two]
                t_a = [sb(f"t_a{s}", [17, EDGE_BLOCK]) for s in two]
                low = sb("low", [D, EDGE_BLOCK])
                size = sb("size", [D, EDGE_BLOCK])
                e_f = sb("e_f", [D, EDGE_BLOCK])
                soft = sb("soft", [D, EDGE_BLOCK])
                msg = sb("msg", [D, EDGE_BLOCK])
                ends = sb("ends", [D, EDGE_BLOCK])
                run = [sb(f"run{s}", [D, EDGE_BLOCK]) for s in two]
                res = [sb(f"res{s}", [P, CH * D]) for s in two]
                gamma = sb("gamma", [D, 1])
                beta = sb("beta", [D, 1])
                p_d, p_s, p_a, p_f, p_g = (ps(n, [P, EDGE_BLOCK]) for n in ("p_d", "p_s", "p_a", "p_f", "p_g"))
                p_out = [ps(f"p_out{s}", [P, CH * D]) for s in two]

                with nc.Block() as block:
                    @block.sync
                    def _(sp):
                        def load(b):
                            sp.wait_ge(prepared, 2)
                            if b.after(2):
                                sp.wait_ge(gathered[b.s], past(gathered[b.s]) + b.pair * CH * DMA)
                                sp.nop(nofuse=True)
                            if b.after(2):
                                sp.wait_ge(gathered_dst[b.s], past(gathered_dst[b.s]) + b.pair * CH * DMA)
                                sp.nop(nofuse=True)
                            if b.after(2):
                                sp.wait_ge(turned, b.n - 1)
                                sp.nop(nofuse=True)
                            sp.dma_start(src_s[b.s][:, :], src_i[bass.ds(b.n * P, P), :]).then_inc(src_loaded[b.s], DMA)
                            sp.dma_start(dst_s[b.s][:, :], dst_i[bass.ds(b.n * P, P), :]).then_inc(dst_loaded[b.s], DMA)
                            p = edge_tail_p if b.tail else P
                            sp.dma_start(attr[b.s][0:p, :, 0:16], a["edge_attr_16"][bass.ds(b.n * EDGE_BLOCK, p * CH), :]
                                         .rearrange("(p c) f -> p c f", p=p)).then_inc(attr_loaded[b.s], DMA)

                        def load_end(b):
                            if b.after(2):
                                sp.wait_ge(scattered[b.s], past(scattered[b.s]) + b.pair * CH * DMA)
                                sp.nop(nofuse=True)
                            sp.dma_start(end_s[b.s][:, :], end_i[bass.ds(b.n * P, P), :]).then_inc(end_loaded[b.s], DMA)

                        for t, name in ((gamma, "L1_gnn_bn_gamma"), (beta, "L1_gnn_bn_beta")):
                            sp.dma_start(t[:, :], a[name].rearrange("(d o) -> d o", o=1)).then_inc(setup_loaded, DMA)
                        pipeline(sp, EB, [(load, 0), (load_end, 2)])

                    @block.gpsimd
                    def _(pool):
                        def gather(b):
                            pool.wait_ge(src_loaded[b.s], (b.pair + 1) * DMA)
                            pool.nop(nofuse=True)
                            pool.wait_ge(dst_loaded[b.s], (b.pair + 1) * DMA)
                            pool.nop(nofuse=True)
                            if b.after(2):
                                pool.wait_ge(turned, b.n - 1)
                                pool.nop(nofuse=True)
                            for got, idx, done in ((got_s, src_s, gathered), (got_d, dst_s, gathered_dst)):
                                for j in range(CH):
                                    pool.indirect_dma_start(
                                        got[b.s][:, j, :], None, x1,
                                        bass.IndirectOffsetOnAxis(ap=idx[b.s][:, j:j + 1], axis=0)
                                    ).then_inc(done[b.s], DMA)

                        def scatter(b):
                            pool.wait_ge(end_loaded[b.s], (b.pair + 1) * DMA)
                            pool.nop(nofuse=True)
                            pool.wait_ge(rows_ready, b.n + 1)
                            pool.nop(nofuse=True)
                            for j in range(CH):
                                pool.indirect_dma_start(
                                    sums[D], bass.IndirectOffsetOnAxis(ap=end_s[b.s][:, j:j + 1], axis=0),
                                    res[b.s][:, j * D:(j + 1) * D], None, bounds_check=N - 1, oob_is_err=False
                                ).then_inc(scattered[b.s], DMA)

                        pipeline(pool, EB, [(gather, 0), (scatter, 2)])
                        for s in two:
                            pool.wait_ge(scattered[s], past(scattered[s]) + blocks_in(EB, s) * CH * DMA)

                    @block.tensor
                    def _(pe):
                        def turn(b):
                            pe.wait_ge(gathered[b.s], past(gathered[b.s]) + (b.pair + 1) * CH * DMA)
                            pe.nop(nofuse=True)
                            pe.wait_ge(gathered_dst[b.s], past(gathered_dst[b.s]) + (b.pair + 1) * CH * DMA)
                            pe.nop(nofuse=True)
                            pe.wait_ge(attr_loaded[b.s], (b.pair + 1) * DMA)
                            pe.nop(nofuse=True)
                            if b.after(1):
                                pe.wait_ge(evacuated, b.n)
                                pe.nop(nofuse=True)
                            for bank, got, width in ((p_d, got_d, D), (p_s, got_s, D), (p_a, attr, 17)):
                                for j in range(CH):
                                    last = nc.tensor.transpose(bank[0:width, j:EDGE_BLOCK:CH], got[b.s][:, j, :],
                                                               ident[:, :])
                            last.then_inc(turned, 1)

                        def gates(b):
                            pe.wait_ge(evacuated, b.n + 1)
                            pe.nop(nofuse=True)
                            if b.after(1):
                                pe.wait_ge(scanned, b.n)
                                pe.nop(nofuse=True)
                            for bank, g in ((p_f, "f"), (p_g, "s")):
                                for i, t in enumerate((t_d, t_s, t_a)):
                                    last = nc.tensor.matmul(bank[:, :], gate_w[g][i][:, :], t[b.s][:, :],
                                                            start=(i == 0), stop=(i == 2))
                            last.then_inc(multiplied, 1)

                        def turn_back(b):
                            pe.wait_ge(scanned, b.n + 1)
                            pe.nop(nofuse=True)
                            if b.after(2):
                                pe.wait_ge(rows_ready, b.n - 1)
                                pe.nop(nofuse=True)
                            for j in range(CH):
                                last = nc.tensor.transpose(p_out[b.s][:, j * D:(j + 1) * D],
                                                           run[b.s][:, j:EDGE_BLOCK:CH], ident[:, :])
                            last.then_inc(turned_back, 1)

                        pipeline(pe, EB, [(turn, 0), (gates, 0), (turn_back, 1)])

                    @block.vector
                    def _(dve):
                        link = Steps(vec_step, 7)

                        def clamp(b):
                            dve.wait_ge(multiplied, b.n + 1)
                            dve.nop(nofuse=True)
                            if b.after(1):
                                dve.wait_ge(gates_out, b.n)
                                dve.nop(nofuse=True)
                            nc.vector.tensor_scalar(low[:, :], p_f[:, :], -87.0, None, ALU.max).then_inc(gates_in, 1)

                        def combine(b):
                            link.at(b)
                            dve.wait_ge(gates_out, b.n + 1)
                            dve.nop(nofuse=True)
                            if b.after(2):
                                dve.wait_ge(turned_back, b.n - 1)
                                dve.nop(nofuse=True)
                            if b.after(1):
                                dve.wait_ge(scanned, b.n)
                                dve.nop(nofuse=True)
                            nc.vector.tensor_scalar(e_f[:, :], e_f[:, :], 1.0, None, ALU.add).then_inc(link.sem, 1)
                            dve.wait_ge(link.sem, link.count())
                            dve.nop(nofuse=True)
                            nc.vector.reciprocal(e_f[:, :], e_f[:, :]).then_inc(link.sem, 1)
                            dve.wait_ge(link.sem, link.count())
                            dve.nop(nofuse=True)
                            nc.vector.scalar_tensor_tensor(out=msg[:, :], in0=p_g[:, :], scalar=0.0, in1=soft[:, :],
                                                           op0=ALU.max, op1=ALU.add).then_inc(link.sem, 1)
                            dve.wait_ge(link.sem, link.count())
                            dve.nop(nofuse=True)
                            nc.vector.tensor_tensor(msg[:, :], msg[:, :], e_f[:, :], ALU.mult).then_inc(link.sem, 1)
                            dve.wait_ge(link.sem, link.count())
                            dve.nop(nofuse=True)
                            first = isinstance(b.n, int) and b.n == 0
                            nc.vector.tensor_tensor_scan(
                                run[b.s][:, :], cont[:, bass.ds(b.n * EDGE_BLOCK, EDGE_BLOCK)], msg[:, :],
                                0.0 if first else run[1 - b.s][:, EDGE_BLOCK - 1:EDGE_BLOCK],
                                ALU.mult, ALU.add).then_inc(scanned, 1)
                            dve.wait_ge(scanned, b.n + 1)
                            dve.nop(nofuse=True)
                            edges = EDGE_BLOCK
                            if b.tail:
                                edges = edge_left
                                nc.vector.memset(ends[:, :], 0.0).then_inc(link.sem, 1)
                                dve.wait_ge(link.sem, link.count())
                                dve.nop(nofuse=True)
                            nc.vector.scalar_tensor_tensor(
                           out=ends[:, 0:edges], in0=cont[:, bass.ds(b.n * EDGE_BLOCK + 1, edges)], scalar=0.0,
                           in1=run[b.s][:, 0:edges], op0=ALU.is_equal, op1=ALU.mult).then_inc(link.sem, 1)
                            dve.wait_ge(link.sem, link.count())
                            dve.nop(nofuse=True)
                            ins = nc.vector.bn_stats(bn_part[:, bass.ds(b.n * 6, 6)], ends[:, :])
                            if not b.tail:
                                ins.then_inc(vec_step, 2)
                                link.k = link.per
                                dve.wait_ge(vec_step, link.base + link.per)
                            else:
                                ins.then_inc(link.sem, 1)
                                dve.wait_ge(link.sem, link.count())
                                dve.nop(nofuse=True)

                        pipeline(dve, EB, [(clamp, 0), (combine, 0)])

                        mv = [sb(f"mv{i}", [D, 1]) for i in range(6)]
                        stat = sb("stat", [D, 2])
                        mean, square, var, sd, scale, shift = mv
                        wide_c = sb("wide_c", [D, 2 * D])
                        ratio = float(EP) / float(N)
                        then = Steps(vec_step, 99)
                        then.base = EB * 7

                        dve.wait_ge(setup_loaded, 2 * DMA)
                        nc.vector.bn_aggr(stat[:, :], bn_part[:, :]).then_inc(then.sem, 1)
                        dve.wait_ge(then.sem, then.count())
                        nc.vector.tensor_scalar(mean[:, :], stat[:, 0:1], ratio, None, ALU.mult).then_inc(then.sem, 1)
                        dve.wait_ge(then.sem, then.count())
                        nc.vector.scalar_tensor_tensor(out=square[:, :], in0=stat[:, 0:1], scalar=stat[:, 0:1],
                                                       in1=stat[:, 1:2], op0=ALU.mult, op1=ALU.add).then_inc(then.sem, 1)
                        dve.wait_ge(then.sem, then.count())
                        nc.vector.tensor_scalar(square[:, :], square[:, :], ratio, EPS, ALU.mult, ALU.add).then_inc(then.sem, 1)
                        dve.wait_ge(then.sem, then.count())
                        nc.vector.tensor_tensor(var[:, :], mean[:, :], mean[:, :], ALU.mult).then_inc(then.sem, 1)
                        dve.wait_ge(then.sem, then.count())
                        nc.vector.tensor_tensor(var[:, :], square[:, :], var[:, :], ALU.subtract).then_inc(then.sem, 1)
                        dve.wait_ge(then.sem, then.count())
                        dve.sem_inc(prepared, 1)
                        dve.wait_ge(prepared, 4)
                        nc.vector.reciprocal(scale[:, :], sd[:, :]).then_inc(then.sem, 1)
                        dve.wait_ge(then.sem, then.count())
                        nc.vector.tensor_tensor(scale[:, :], scale[:, :], gamma[:, :], ALU.mult).then_inc(then.sem, 1)
                        dve.wait_ge(then.sem, then.count())
                        nc.vector.tensor_tensor(shift[:, :], mean[:, :], scale[:, :], ALU.mult).then_inc(then.sem, 1)
                        dve.wait_ge(then.sem, then.count())
                        nc.vector.tensor_tensor(shift[:, :], beta[:, :], shift[:, :], ALU.subtract).then_inc(then.sem, 1)
                        dve.wait_ge(then.sem, then.count())
                        nc.vector.tensor_copy(wide_c[:, 0:D], scale[:, 0:1].to_broadcast([D, D])).then_inc(then.sem, 1)
                        dve.wait_ge(then.sem, then.count())
                        nc.vector.tensor_copy(wide_c[:, D:2 * D], shift[:, 0:1].to_broadcast([D, D])).then_inc(finished, 1)
                        bn_tiles.extend([var, sd, wide_c])
                        dve.wait_ge(turned, EB + 1)
                        nc.vector.tensor_copy(bn_scale[:, :], p_d[:, 0:D])
                        nc.vector.tensor_copy(bn_shift[:, :], p_d[:, D:2 * D])

                    @block.tensor
                    def _(pe):
                        var, sd, wide_c = bn_tiles
                        pe.wait_ge(finished, 1)
                        nc.tensor.transpose(p_d[:, 0:D], wide_c[:, 0:D], ident[:, :])
                        nc.tensor.transpose(p_d[:, D:2 * D], wide_c[:, D:2 * D], ident[:, :]).then_inc(turned, 1)

                    @block.scalar
                    def _(act):
                        link = Steps(act_step, 2)

                        def evacuate(b):
                            act.wait_ge(turned, b.n + 1)
                            act.nop(nofuse=True)
                            if b.after(2):
                                act.wait_ge(multiplied, b.n - 1)
                                act.nop(nofuse=True)
                            nc.scalar.copy(t_d[b.s][:, :], p_d[:, :])
                            nc.scalar.copy(t_s[b.s][:, :], p_s[:, :])
                            nc.scalar.copy(t_a[b.s][:, :], p_a[0:17, :]).then_inc(evacuated, 1)

                        def gates(b):
                            link.at(b)
                            act.wait_ge(multiplied, b.n + 1)
                            act.nop(nofuse=True)
                            if b.after(1):
                                act.wait_ge(scanned, b.n)
                                act.nop(nofuse=True)
                            nc.scalar.activation(size[:, :], p_g[:, :], ACT.Abs).then_inc(link.sem, 1)
                            act.wait_ge(link.sem, link.count())
                            act.nop(nofuse=True)
                            nc.scalar.activation(size[:, :], size[:, :], ACT.Exp, scale=-1.0).then_inc(link.sem, 1)
                            act.wait_ge(link.sem, link.count())
                            act.nop(nofuse=True)
                            nc.scalar.activation(soft[:, :], size[:, :], ACT.Ln, bias=1.0)
                            act.wait_ge(gates_in, b.n + 1)
                            act.nop(nofuse=True)
                            nc.scalar.activation(e_f[:, :], low[:, :], ACT.Exp, scale=-1.0).then_inc(gates_out, 1)

                        def copy_rows(b):
                            act.wait_ge(turned_back, b.n + 1)
                            act.nop(nofuse=True)
                            if b.after(2):
                                act.wait_ge(scattered[b.s], past(scattered[b.s]) + b.pair * CH * DMA)
                                act.nop(nofuse=True)
                            nc.scalar.copy(res[b.s][:, :], p_out[b.s][:, :]).then_inc(rows_ready, 1)

                        for s in two:
                            nc.scalar.activation(attr[s][:, :, :].rearrange("p c f -> p (c f)"),
                                                 ident[:, 0:1].to_broadcast([P, CH * 17]), ACT.Copy, scale=0.0,
                                                 bias=1.0).then_inc(prepared, 1)
                        pipeline(act, EB, [(evacuate, 0), (gates, 0), (copy_rows, 1)])
                        var, sd, _ = bn_tiles
                        act.wait_ge(prepared, 3)
                        nc.scalar.activation(sd[:, :], var[:, :], ACT.Sqrt).then_inc(prepared, 1)
            end_pass(scattered, gathered, gathered_dst)

        bn_tiles = []
        gated_edge_pass()

        def gated_node_pass():
            with ExitStack() as ctx:
                def sb(name, shape, dt=F32):
                    return ctx.enter_context(nc.sbuf_tensor(f"cn_{name}", shape, dt))

                def ps(name, shape):
                    return ctx.enter_context(nc.psum_tensor(f"cn_{name}", shape, F32))

                two = range(2)
                sum_s = [sb(f"sum{s}", [P, J * D]) for s in two]
                x_s = [sb(f"x{s}", [P, J * D]) for s in two]
                aux_s = [sb(f"aux{s}", [P, J * AUXW]) for s in two]
                y_s = [sb(f"y{s}", [P, J * D]) for s in two]
                o_s = [sb(f"o{s}", [P, J * D]) for s in two]
                att_s = [sb(f"att{s}", [P, J * ADW]) for s in two]
                x_t = sb("x_t", [D, J * P])
                part = sb("part", [P, J * 48])
                loop = sb("loop", [P, J * 3])
                count = sb("count", [P, J])
                n1, n2 = Norm(sb, "n1"), Norm(sb, "n2")
                p_x = ps("p_x", [P, J * P])
                p_sc = ps("p_sc", [P, J * 6])

                def row_of(t, p, j):
                    return t[0:p, :].unsqueeze(1).to_broadcast([p, j, D])

                with nc.Block() as block:
                    @block.sync
                    def _(sp):
                        def load(b):
                            p, j = pj(b)
                            sp.wait_ge(prepared, 2)
                            if b.after(2):
                                sp.wait_ge(attended, b.n - 1)
                                sp.nop(nofuse=True)
                            if b.after(2):
                                sp.wait_ge(stats[1], b.n - 1)
                                sp.nop(nofuse=True)
                            for t, table, width in ((sum_s, sums[D], D), (x_s, x1, D), (aux_s, aux, AUXW)):
                                sp.dma_start(t[b.s][0:p, 0:j * width], rows(table, b)).then_inc(loaded[b.s], DMA)

                        def store(b):
                            p, j = pj(b)
                            sp.wait_ge(attended, b.n + 1)
                            sp.nop(nofuse=True)
                            sp.wait_ge(normed_x[1], b.n + 1)
                            sp.nop(nofuse=True)
                            sp.dma_start(rows(x2, b), o_s[b.s][0:p, 0:j * D]).then_inc(stored[b.s], DMA)
                            sp.dma_start(rows(att, b), att_s[b.s][0:p, 0:j * ADW]).then_inc(stored[b.s], DMA)

                        pipeline(sp, NB, [(store, 2), (load, 0)])
                        for s in two:
                            sp.wait_ge(stored[s], blocks_in(NB, s) * 2 * DMA)

                    @block.vector
                    def _(dve):
                        link_a, link_b, link_c = Steps(vec_step, 5), Steps(vec_step_b, 1), Steps(vec_step_c, 3)
                        link_f, link_g = Steps(factor_step[0], 1), Steps(factor_step[1], 1)
                        link_e = Steps(vec_step_d, 7)

                        def batch_norm(b):
                            p, j = pj(b)
                            link_a.at(b)
                            dve.wait_ge(loaded[b.s], (b.pair + 1) * 3 * DMA)
                            dve.nop(nofuse=True)
                            v = split(sum_s[b.s], p, j)
                            nc.vector.tensor_tensor(v, v, row_of(bn_scale, p, j), ALU.mult).then_inc(link_a.sem, 1)
                            dve.wait_ge(link_a.sem, link_a.count())
                            dve.nop(nofuse=True)
                            nc.vector.tensor_tensor(v, v, row_of(bn_shift, p, j), ALU.add).then_inc(link_a.sem, 1)
                            dve.wait_ge(link_a.sem, link_a.count())
                            dve.nop(nofuse=True)
                            nc.vector.tensor_tensor(v, v, split(x_s[b.s], p, j), ALU.add).then_inc(link_a.sem, 1)
                            dve.wait_ge(link_a.sem, link_a.count())
                            dve.nop(nofuse=True)
                            n1.variance(link_a, sum_s[b.s], b, stats[0])

                        def factors_1(b):
                            link_f.at(b)
                            dve.wait_ge(rooted_x[0], b.n + 1)
                            dve.nop(nofuse=True)
                            n1.factors(link_f, b, factored[0])

                        def gain(b):
                            p, j = pj(b)
                            link_b.at(b)
                            dve.wait_ge(normed_x[0], b.n + 1)
                            dve.nop(nofuse=True)
                            v = split(y_s[b.s], p, j)
                            nc.vector.tensor_tensor(v, v, row_of(brow["L1_gnn_ln_gamma"], p, j), ALU.mult).then_inc(link_b.sem, 1)
                            dve.wait_ge(link_b.sem, link_b.count())
                            dve.nop(nofuse=True)
                            nc.vector.tensor_tensor(v, v, row_of(brow["L1_gnn_ln_beta"], p, j), ALU.add).then_inc(gained, 1)

                        def add_x(b):
                            p, j = pj(b)
                            link_c.at(b)
                            dve.wait_ge(rectified, b.n + 1)
                            dve.nop(nofuse=True)
                            nc.vector.scalar_tensor_tensor(out=y_s[b.s][0:p, 0:j * D], in0=x_s[b.s][0:p, 0:j * D],
                                                           scalar=2.0, in1=y_s[b.s][0:p, 0:j * D], op0=ALU.mult,
                                                           op1=ALU.add).then_inc(link_c.sem, 1)
                            dve.wait_ge(link_c.sem, link_c.count())
                            dve.nop(nofuse=True)
                            n2.variance(link_c, y_s[b.s], b, stats[1])

                        def factors_2(b):
                            link_g.at(b)
                            dve.wait_ge(rooted_x[1], b.n + 1)
                            dve.nop(nofuse=True)
                            n2.factors(link_g, b, factored[1])

                        def scores(b):
                            p, j = pj(b)
                            link_e.at(b)
                            dve.wait_ge(scored, b.n + 1)
                            dve.nop(nofuse=True)
                            if b.after(2):
                                dve.wait_ge(stored[b.s], b.pair * 2 * DMA)
                                dve.nop(nofuse=True)
                            if b.after(1):
                                dve.wait_ge(attended, b.n)
                                dve.nop(nofuse=True)
                            attrs = aux_s[b.s][0:p, 0:j * AUXW].rearrange("p (j f) -> p j f", f=AUXW)
                            for h in range(3):
                                last = nc.vector.tensor_tensor(
                                    part[0:p, h * 16 * J:h * 16 * J + j * 16].rearrange("p (j f) -> p j f", f=16),
                                    attrs[:, :, 0:16], loop_w[0:p, 16 * h:16 * h + 16].unsqueeze(1)
                                    .to_broadcast([p, j, 16]), ALU.mult)
                            last.then_inc(link_e.sem, 1)
                            dve.wait_ge(link_e.sem, link_e.count())
                            dve.nop(nofuse=True)
                            for h in range(3):
                                last = nc.vector.tensor_reduce(
                                    loop[0:p, h * J:h * J + j],
                                    part[0:p, h * 16 * J:h * 16 * J + j * 16].rearrange("p (j f) -> p j f", f=16), AX,
                                    ALU.add)
                            last.then_inc(link_e.sem, 1)
                            dve.wait_ge(link_e.sem, link_e.count())
                            dve.nop(nofuse=True)
                            nc.vector.tensor_scalar(count[0:p, 0:j], attrs[:, :, 16], 1.0, None, ALU.max).then_inc(link_e.sem, 1)
                            dve.wait_ge(link_e.sem, link_e.count())
                            dve.nop(nofuse=True)
                            nc.vector.reciprocal(count[0:p, 0:j], count[0:p, 0:j]).then_inc(link_e.sem, 1)
                            dve.wait_ge(link_e.sem, link_e.count())
                            dve.nop(nofuse=True)
                            for h in range(3):
                                last = nc.vector.tensor_tensor(loop[0:p, h * J:h * J + j], loop[0:p, h * J:h * J + j],
                                                               count[0:p, 0:j], ALU.mult)
                            last.then_inc(link_e.sem, 1)
                            dve.wait_ge(link_e.sem, link_e.count())
                            dve.nop(nofuse=True)
                            for i in (0, 3):
                                for h in range(3):
                                    last = nc.vector.tensor_tensor(loop[0:p, h * J:h * J + j], loop[0:p, h * J:h * J + j],
                                                                   p_sc[0:p, i + h:j * 6:6], ALU.add)
                                last.then_inc(link_e.sem, 1)
                                dve.wait_ge(link_e.sem, link_e.count())
                                dve.nop(nofuse=True)
                            for h in range(3):
                                nc.vector.scalar_tensor_tensor(
                                    out=att_s[b.s][0:p, 3 + h:j * ADW:ADW], in0=loop[0:p, h * J:h * J + j], scalar=0.2,
                                    in1=loop[0:p, h * J:h * J + j], op0=ALU.mult, op1=ALU.max)
                            for h in range(3):
                                last = nc.vector.tensor_copy(att_s[b.s][0:p, h:j * ADW:ADW], p_sc[0:p, 3 + h:j * 6:6])
                            last.then_inc(attended, 1)

                        for s in two:
                            nc.vector.memset(att_s[s][:, :], 0.0).then_inc(prepared, 1)
                        pipeline(dve, NB, [(scores, 2), (batch_norm, 0), (factors_1, 0), (gain, 0), (add_x, 1),
                                           (factors_2, 1)])

                    @block.scalar
                    def _(act):
                        def root_1(b):
                            act.wait_ge(stats[0], b.n + 1)
                            act.nop(nofuse=True)
                            n1.root(b, rooted_x[0])

                        def normalise_1(b):
                            p, j = pj(b)
                            act.wait_ge(factored[0], b.n + 1)
                            act.nop(nofuse=True)
                            if b.after(2):
                                act.wait_ge(stats[1], b.n - 1)
                                act.nop(nofuse=True)
                            if b.after(2):
                                act.wait_ge(normed_x[1], b.n - 1)
                                act.nop(nofuse=True)
                            scale_rows(y_s[b.s], sum_s[b.s], n1.rstd[b.s], n1.nmr[b.s], p, j).then_inc(normed_x[0], 1)

                        def rectify(b):
                            p, j = pj(b)
                            act.wait_ge(gained, b.n + 1)
                            act.nop(nofuse=True)
                            nc.scalar.activation(y_s[b.s][0:p, 0:j * D], y_s[b.s][0:p, 0:j * D], ACT.Relu
                                                 ).then_inc(rectified, 1)

                        def root_2(b):
                            act.wait_ge(stats[1], b.n + 1)
                            act.nop(nofuse=True)
                            n2.root(b, rooted_x[1])

                        def normalise_2(b):
                            p, j = pj(b)
                            act.wait_ge(factored[1], b.n + 1)
                            act.nop(nofuse=True)
                            if b.after(2):
                                act.wait_ge(stored[b.s], b.pair * 2 * DMA)
                                act.nop(nofuse=True)
                            scale_rows(o_s[b.s], y_s[b.s], n2.rstd[b.s], n2.nmr[b.s], p, j).then_inc(normed_x[1], 1)

                        def evacuate(b):
                            p, j = pj(b)
                            act.wait_ge(turned, b.n + 1)
                            act.nop(nofuse=True)
                            if b.after(1):
                                act.wait_ge(scored, b.n)
                                act.nop(nofuse=True)
                            nc.scalar.copy(cols(x_t, D, p, j), cols(p_x, D, p, j)).then_inc(evacuated, 1)

                        pipeline(act, NB, [(evacuate, 2), (root_1, 0), (normalise_1, 0), (rectify, 0), (root_2, 1),
                                           (normalise_2, 1)])

                    @block.tensor
                    def _(pe):
                        def turn(b):
                            p, j = pj(b)
                            pe.wait_ge(normed_x[1], b.n + 1)
                            pe.nop(nofuse=True)
                            if b.after(1):
                                pe.wait_ge(evacuated, b.n)
                                pe.nop(nofuse=True)
                            turn_rows(p_x, o_s[b.s], p, j, D).then_inc(turned, 1)

                        def score(b):
                            p, j = pj(b)
                            pe.wait_ge(evacuated, b.n + 1)
                            pe.nop(nofuse=True)
                            if b.after(1):
                                pe.wait_ge(attended, b.n)
                                pe.nop(nofuse=True)
                            times_weight(p_sc, x_t, score_w[:, :], p, j, D, 6).then_inc(scored, 1)

                        pipeline(pe, NB, [(turn, 0), (score, 0)])
            end_pass()

        gated_node_pass()

        def attention_edge_pass():
            with ExitStack() as ctx:
                def sb(name, shape, dt=F32):
                    return ctx.enter_context(nc.sbuf_tensor(f"ge_{name}", shape, dt))

                def ps(name, shape):
                    return ctx.enter_context(nc.psum_tensor(f"ge_{name}", shape, F32))

                two = range(2)
                B = EDGE_BLOCK
                src_s = [sb(f"src{s}", [P, CH], U32) for s in two]
                dst_s = [sb(f"dst{s}", [P, CH], U32) for s in two]
                end_s = [sb(f"end{s}", [P, CH], U32) for s in two]
                got_s = [sb(f"got_src{s}", [P, CH, D]) for s in two]
                small = [sb(f"small{s}", [P, CH, ADW + 16]) for s in two]
                t_x = [sb(f"t_x{s}", [D, B]) for s in two]
                t_a = sb("t_a", [ADW + 16, B])
                leak = sb("leak", [3, B])
                own = sb("own", [3, B])
                score = sb("score", [3, B])
                capped = sb("capped", [3, B])
                jump = sb("jump", [3, B])
                top = [sb(f"top{s}", [3, 1 + B]) for s in two]
                gaps = sb("gaps", [3, 3 * B])
                powers = [sb(f"powers{s}", [3, 3 * B]) for s in two]
                decay = [sb(f"decay{s}", [3, B]) for s in two]
                added = sb("added", [3, B])
                denom = [sb(f"denom{s}", [3, B]) for s in two]
                inv = [sb(f"inv{s}", [3, B]) for s in two]
                loop_less = [sb(f"loop_less{s}", [3, B]) for s in two]
                part = sb("part", [D, B])
                run = [[sb(f"run{h}_{s}", [D, B]) for s in two] for h in range(3)]
                res = [sb(f"res{s}", [P, CH * GATW]) for s in two]
                p_x, p_a, p_sc, p_own, p_w, p_dec = (ps(n, [P, B]) for n in ("p_x", "p_a", "p_sc", "p_own", "p_w", "p_dec"))
                p_y = [ps(f"p_y{s}", [P, B]) for s in two]

                with nc.Block() as block:
                    @block.sync
                    def _(sp):
                        def load(b):
                            sp.wait_ge(prepared, 4)
                            if b.after(2):
                                sp.wait_ge(gathered[b.s], past(gathered[b.s]) + b.pair * CH * DMA)
                                sp.nop(nofuse=True)
                            if b.after(2):
                                sp.wait_ge(gathered_dst[b.s], past(gathered_dst[b.s]) + b.pair * CH * DMA)
                                sp.nop(nofuse=True)
                            if b.after(2):
                                sp.wait_ge(turned, b.n - 1)
                                sp.nop(nofuse=True)
                            sp.dma_start(src_s[b.s][:, :], src_i[bass.ds(b.n * P, P), :]).then_inc(src_loaded[b.s], DMA)
                            sp.dma_start(dst_s[b.s][:, :], dst_i[bass.ds(b.n * P, P), :]).then_inc(dst_loaded[b.s], DMA)
                            p = edge_tail_p if b.tail else P
                            sp.dma_start(small[b.s][0:p, :, ADW:ADW + 16],
                                         a["edge_attr_16"][bass.ds(b.n * EDGE_BLOCK, p * CH), :]
                                         .rearrange("(p c) f -> p c f", p=p)).then_inc(attr_loaded[b.s], DMA)

                        def load_end(b):
                            if b.after(2):
                                sp.wait_ge(scattered[b.s], past(scattered[b.s]) + b.pair * CH * DMA)
                                sp.nop(nofuse=True)
                            sp.dma_start(end_s[b.s][:, :], end_i[bass.ds(b.n * P, P), :]).then_inc(end_loaded[b.s], DMA)

                        pipeline(sp, EB, [(load, 0), (load_end, 2)])

                    @block.gpsimd
                    def _(pool):
                        def gather(b):
                            pool.wait_ge(src_loaded[b.s], (b.pair + 1) * DMA)
                            pool.nop(nofuse=True)
                            pool.wait_ge(dst_loaded[b.s], (b.pair + 1) * DMA)
                            pool.nop(nofuse=True)
                            if b.after(2):
                                pool.wait_ge(turned, b.n - 1)
                                pool.nop(nofuse=True)
                            pool.wait_ge(prepared, 4)
                            for j in range(CH):
                                pool.indirect_dma_start(
                                    got_s[b.s][:, j, :], None, x2,
                                    bass.IndirectOffsetOnAxis(ap=src_s[b.s][:, j:j + 1], axis=0)
                                ).then_inc(gathered[b.s], DMA)
                            for j in range(CH):
                                pool.indirect_dma_start(
                                    small[b.s][:, j, 0:ADW], None, att,
                                    bass.IndirectOffsetOnAxis(ap=dst_s[b.s][:, j:j + 1], axis=0)
                                ).then_inc(gathered_dst[b.s], DMA)

                        def scatter(b):
                            pool.wait_ge(end_loaded[b.s], (b.pair + 1) * DMA)
                            pool.nop(nofuse=True)
                            pool.wait_ge(rows_ready, (b.n + 1) * CH)
                            pool.nop(nofuse=True)
                            pool.wait_ge(weights_ready, b.n + 1)
                            pool.nop(nofuse=True)
                            for j in range(CH):
                                pool.indirect_dma_start(
                                    sums[GATW], bass.IndirectOffsetOnAxis(ap=end_s[b.s][:, j:j + 1], axis=0),
                                    res[b.s][:, j * GATW:(j + 1) * GATW], None, bounds_check=N - 1, oob_is_err=False
                                ).then_inc(scattered[b.s], DMA)

                        pipeline(pool, EB, [(gather, 0), (scatter, 2)])
                        for s in two:
                            pool.wait_ge(scattered[s], past(scattered[s]) + blocks_in(EB, s) * CH * DMA)

                    @block.tensor
                    def _(pe):
                        def turn(b):
                            pe.wait_ge(gathered[b.s], past(gathered[b.s]) + (b.pair + 1) * CH * DMA)
                            pe.nop(nofuse=True)
                            pe.wait_ge(gathered_dst[b.s], past(gathered_dst[b.s]) + (b.pair + 1) * CH * DMA)
                            pe.nop(nofuse=True)
                            pe.wait_ge(attr_loaded[b.s], (b.pair + 1) * DMA)
                            pe.nop(nofuse=True)
                            if b.after(1):
                                pe.wait_ge(evacuated, b.n)
                                pe.nop(nofuse=True)
                            for bank, got, width in ((p_x, got_s, D), (p_a, small, ADW + 16)):
                                for j in range(CH):
                                    last = nc.tensor.transpose(bank[0:width, j:B:CH], got[b.s][:, j, :], ident[:, :])
                            last.then_inc(turned, 1)

                        def scores(b):
                            pe.wait_ge(evacuated, b.n + 1)
                            pe.nop(nofuse=True)
                            if b.after(1):
                                pe.wait_ge(gates_in, b.n)
                                pe.nop(nofuse=True)
                            nc.tensor.matmul(p_sc[0:3, :], score_w[:, 0:3], t_x[b.s][:, :], start=True, stop=False)
                            nc.tensor.matmul(p_sc[0:3, :], edge_w[:, 0:3], t_a[:, :], start=False, stop=True)
                            nc.tensor.matmul(p_own[0:3, :], edge_w[:, 3:6], t_a[:, :], start=True, stop=True
                                             ).then_inc(scored, 1)

                        def spread_heads(b):
                            pe.wait_ge(attended, b.n + 1)
                            pe.nop(nofuse=True)
                            for h in range(3):
                                if b.after(1) or h:
                                    pe.wait_ge(scanned, b.n * 3 + h)
                                    pe.nop(nofuse=True)
                                nc.tensor.matmul(p_w[:, :], pick[:, h * D:(h + 1) * D], powers[b.s][:, 2 * B:3 * B],
                                                 start=True, stop=True)
                                nc.tensor.matmul(p_dec[:, :], pick[:, h * D:(h + 1) * D], decay[b.s][:, :],
                                                 start=True, stop=True).then_inc(spread, 1)

                        def messages(b):
                            pe.wait_ge(scanned, b.n * 3 + 3)
                            pe.nop(nofuse=True)
                            for j in range(CH):
                                if b.after(1) or j > 1:
                                    pe.wait_ge(rows_ready, b.n * CH + j - 1)
                                    pe.nop(nofuse=True)
                                if b.after(1) or j > 1:
                                    pe.wait_ge(taken, b.n * CH + j - 1)
                                    pe.nop(nofuse=True)
                                for h in range(3):
                                    nc.tensor.matmul(p_y[j % 2][:, h * D:(h + 1) * D], run[h][b.s][:, j:B:CH],
                                                     head_w[:, h * D:(h + 1) * D], start=True, stop=True)
                                nc.tensor.transpose(p_y[j % 2][:, 3 * D:3 * D + 3], inv[b.s][:, j:B:CH],
                                                    ident[0:3, 0:3])
                                nc.tensor.transpose(p_y[j % 2][:, 3 * D + 3:3 * D + 6], loop_less[b.s][:, j:B:CH],
                                                    ident[0:3, 0:3]).then_inc(turned_back, 1)

                        pipeline(pe, EB, [(turn, 0), (scores, 0), (messages, 1), (spread_heads, 0)])

                    @block.vector
                    def _(dve):
                        link_a, link_b = Steps(vec_step, 6), Steps(vec_step_b, 5)
                        link_h, link_m = Steps(vec_step_c, 3), Steps(vec_step_d, 2 * CH)

                        def maxima(b):
                            link_a.at(b)
                            first = isinstance(b.n, int) and b.n == 0
                            now = cont[0:3, bass.ds(b.n * B, B)]
                            dve.wait_ge(scored, b.n + 1)
                            dve.nop(nofuse=True)
                            dve.wait_ge(leaked, b.n + 1)
                            dve.nop(nofuse=True)
                            if b.after(1):
                                dve.wait_ge(powered, b.n)
                                dve.nop(nofuse=True)
                            nc.vector.tensor_tensor(score[:, :], p_sc[0:3, :], leak[:, :], ALU.max).then_inc(link_a.sem, 1)
                            dve.wait_ge(link_a.sem, link_a.count())
                            dve.nop(nofuse=True)
                            nc.vector.tensor_scalar(jump[:, :], now, FAR, -FAR, ALU.mult, ALU.add)
                            nc.vector.tensor_tensor(capped[:, :], score[:, :], own[:, :], ALU.max).then_inc(link_a.sem, 1)
                            dve.wait_ge(link_a.sem, link_a.count())
                            dve.nop(nofuse=True)
                            nc.vector.tensor_tensor_scan(
                         top[b.s][:, 1:1 + B], jump[:, :], capped[:, :],
                         -FAR if first else top[1 - b.s][:, B:1 + B], ALU.add, ALU.max).then_inc(link_a.sem, 1)
                            dve.wait_ge(link_a.sem, link_a.count())
                            dve.nop(nofuse=True)
                            if first:
                                nc.vector.memset(top[b.s][:, 0:1], 0.0).then_inc(link_a.sem, 1)
                                dve.wait_ge(link_a.sem, link_a.count())
                                dve.nop(nofuse=True)
                            else:
                                nc.vector.tensor_copy(top[b.s][:, 0:1], top[1 - b.s][:, B:1 + B]).then_inc(link_a.sem, 1)
                                dve.wait_ge(link_a.sem, link_a.count())
                                dve.nop(nofuse=True)
                            nc.vector.tensor_tensor(gaps[:, 0:B], top[b.s][:, 0:B], top[b.s][:, 1:1 + B],
                                                    ALU.subtract).then_inc(link_a.sem, 1)
                            dve.wait_ge(link_a.sem, link_a.count())
                            dve.nop(nofuse=True)
                            nc.vector.tensor_scalar(gaps[:, 0:B], gaps[:, 0:B], 0.0, None, ALU.min).then_inc(link_a.sem, 1)
                            dve.wait_ge(link_a.sem, link_a.count())
                            dve.nop(nofuse=True)
                            nc.vector.tensor_tensor(gaps[:, B:2 * B], own[:, :], top[b.s][:, 1:1 + B], ALU.subtract)
                            nc.vector.tensor_tensor(gaps[:, 2 * B:3 * B], score[:, :], top[b.s][:, 1:1 + B],
                                                    ALU.subtract).then_inc(gates_in, 1)

                        def denominators(b):
                            link_b.at(b)
                            first = isinstance(b.n, int) and b.n == 0
                            now = cont[0:3, bass.ds(b.n * B, B)]
                            dve.wait_ge(powered, b.n + 1)
                            dve.nop(nofuse=True)
                            if b.after(2):
                                dve.wait_ge(spread, (b.n - 1) * 3)
                                dve.nop(nofuse=True)
                            if b.after(2):
                                dve.wait_ge(turned_back, (b.n - 1) * CH)
                                dve.nop(nofuse=True)
                            nc.vector.tensor_tensor(decay[b.s][:, :], powers[b.s][:, 0:B], now, ALU.mult)
                            nc.vector.scalar_tensor_tensor(out=added[:, :], in0=now, scalar=0.0,
                                                           in1=powers[b.s][:, B:2 * B], op0=ALU.is_equal,
                                                           op1=ALU.mult).then_inc(link_b.sem, 1)
                            dve.wait_ge(link_b.sem, link_b.count())
                            dve.nop(nofuse=True)
                            nc.vector.tensor_tensor(added[:, :], added[:, :], powers[b.s][:, 2 * B:3 * B],
                                                    ALU.add).then_inc(link_b.sem, 1)
                            dve.wait_ge(link_b.sem, link_b.count())
                            dve.nop(nofuse=True)
                            nc.vector.tensor_tensor_scan(
                         denom[b.s][:, :], decay[b.s][:, :], added[:, :],
                         0.0 if first else denom[1 - b.s][:, B - 1:B], ALU.mult, ALU.add).then_inc(link_b.sem, 1)
                            dve.wait_ge(link_b.sem, link_b.count())
                            dve.nop(nofuse=True)
                            nc.vector.reciprocal(inv[b.s][:, :], denom[b.s][:, :]).then_inc(link_b.sem, 1)
                            dve.wait_ge(link_b.sem, link_b.count())
                            dve.nop(nofuse=True)
                            nc.vector.tensor_tensor(loop_less[b.s][:, :], powers[b.s][:, B:2 * B],
                                                    inv[b.s][:, :], ALU.mult).then_inc(link_b.sem, 1)
                            dve.wait_ge(link_b.sem, link_b.count())
                            dve.nop(nofuse=True)
                            nc.vector.tensor_scalar(loop_less[b.s][:, :], loop_less[b.s][:, :], -1.0, None,
                                                    ALU.add).then_inc(attended, 1)

                        def numerators(b):
                            link_h.at(b)
                            first = isinstance(b.n, int) and b.n == 0
                            for h in range(3):
                                dve.wait_ge(spread, b.n * 3 + h + 1)
                                dve.nop(nofuse=True)
                                if b.after(2):
                                    dve.wait_ge(turned_back, (b.n - 1) * CH)
                                    dve.nop(nofuse=True)
                                nc.vector.tensor_tensor(part[:, :], t_x[b.s][:, :], p_w[:, :], ALU.mult).then_inc(link_h.sem, 1)
                                dve.wait_ge(link_h.sem, link_h.count())
                                dve.nop(nofuse=True)
                                nc.vector.tensor_tensor_scan(
                                    run[h][b.s][:, :], p_dec[:, :], part[:, :],
                                    0.0 if first else run[h][1 - b.s][:, B - 1:B], ALU.mult, ALU.add
                                ).then_inc(scanned, 1)
                                dve.wait_ge(scanned, b.n * 3 + h + 1)
                                dve.nop(nofuse=True)

                        def combine(b):
                            link_m.at(b)
                            for j in range(CH):
                                o = res[b.s][:, j * GATW:j * GATW + D]
                                y = p_y[j % 2]
                                dve.wait_ge(taken, b.n * CH + j + 1)
                                dve.nop(nofuse=True)
                                nc.vector.tensor_scalar(o, y[:, 0:D], y[:, 3 * D:3 * D + 1], None, ALU.mult).then_inc(link_m.sem, 1)
                                dve.wait_ge(link_m.sem, link_m.count())
                                dve.nop(nofuse=True)
                                nc.vector.scalar_tensor_tensor(out=o, in0=y[:, D:2 * D],
                                                               scalar=y[:, 3 * D + 1:3 * D + 2], in1=o,
                                                               op0=ALU.mult, op1=ALU.add).then_inc(link_m.sem, 1)
                                dve.wait_ge(link_m.sem, link_m.count())
                                dve.nop(nofuse=True)
                                nc.vector.scalar_tensor_tensor(out=o, in0=y[:, 2 * D:3 * D],
                                                               scalar=y[:, 3 * D + 2:3 * D + 3], in1=o, op0=ALU.mult,
                                                               op1=ALU.add).then_inc(rows_ready, 1)

                        for s in two:
                            nc.vector.memset(res[s][:, :], 0.0).then_inc(prepared, 1)
                            nc.vector.memset(small[s][:, :, :], 0.0).then_inc(prepared, 1)
                        dve.wait_ge(prepared, 4)
                        pipeline(dve, EB, [(maxima, 0), (combine, 1), (denominators, 0), (numerators, 0)])

                    @block.scalar
                    def _(act):
                        def evacuate(b):
                            act.wait_ge(turned, b.n + 1)
                            act.nop(nofuse=True)
                            if b.after(1):
                                act.wait_ge(scored, b.n)
                                act.nop(nofuse=True)
                            if b.after(2):
                                act.wait_ge(scanned, (b.n - 1) * 3)
                                act.nop(nofuse=True)
                            nc.scalar.copy(t_x[b.s][:, :], p_x[:, :])
                            nc.scalar.copy(t_a[:, :], p_a[0:ADW + 16, :]).then_inc(evacuated, 1)

                        def leaks(b):
                            act.wait_ge(scored, b.n + 1)
                            act.nop(nofuse=True)
                            if b.after(1):
                                act.wait_ge(gates_in, b.n)
                                act.nop(nofuse=True)
                            nc.scalar.mul(leak[:, :], p_sc[0:3, :], 0.2)
                            nc.scalar.copy(own[:, :], p_own[0:3, :]).then_inc(leaked, 1)

                        def raise_gaps(b):
                            act.wait_ge(gates_in, b.n + 1)
                            act.nop(nofuse=True)
                            if b.after(2):
                                act.wait_ge(spread, (b.n - 1) * 3)
                                act.nop(nofuse=True)
                            if b.after(2):
                                act.wait_ge(attended, b.n - 1)
                                act.nop(nofuse=True)
                            nc.scalar.activation(powers[b.s][:, :], gaps[:, :], ACT.Exp).then_inc(powered, 1)

                        def loop_weights(b):
                            for j in range(CH):
                                act.wait_ge(turned_back, b.n * CH + j + 1)
                                act.nop(nofuse=True)
                                if b.after(2):
                                    act.wait_ge(scattered[b.s], past(scattered[b.s]) + b.pair * CH * DMA)
                                    act.nop(nofuse=True)
                                act.wait_ge(prepared, 4)
                                ins = nc.scalar.copy(res[b.s][:, j * GATW + D:j * GATW + D + 3],
                                                     p_y[j % 2][:, 3 * D + 3:3 * D + 6])
                                ins.then_inc(taken, 1)
                            act.wait_ge(taken, (b.n + 1) * CH)
                            act.nop(nofuse=True)
                            act.sem_inc(weights_ready, 1)

                        pipeline(act, EB, [(evacuate, 0), (leaks, 0), (loop_weights, 1), (raise_gaps, 0)])
            end_pass(scattered, gathered, gathered_dst)

        def attention_node_pass():
            with ExitStack() as ctx:
                def sb(name, shape, dt=F32):
                    return ctx.enter_context(nc.sbuf_tensor(f"gn_{name}", shape, dt))

                def ps(name, shape):
                    return ctx.enter_context(nc.psum_tensor(f"gn_{name}", shape, F32))

                two = range(2)
                H1 = 64
                sum_s = [sb(f"sum{s}", [P, J * GATW]) for s in two]
                x_s = [sb(f"x{s}", [P, J * D]) for s in two]
                inv = [sb(f"inv{s}", [P, J]) for s in two]
                weight = [sb(f"weight{s}", [P, J * 3]) for s in two]
                r_s = [sb(f"r{s}", [P, J * D]) for s in two]
                o_s = [sb(f"o{s}", [P, J * D]) for s in two]
                g_s = [sb(f"g{s}", [P, J * H1]) for s in two]
                x_t = sb("x_t", [D, J * P])
                o_t = sb("o_t", [D, J * P])
                n1, n2 = Norm(sb, "n1"), Norm(sb, "n2")
                p_x = ps("p_x", [P, J * P])
                p_o = ps("p_o", [P, J * P])
                p_h = [ps(f"p_h{s}", [P, 3 * D]) for s in two]
                p_g = ps("p_g", [P, J * H1])

                def row_of(t, p, j):
                    return t[0:p, :].unsqueeze(1).to_broadcast([p, j, D])

                with nc.Block() as block:
                    @block.sync
                    def _(sp):
                        def load(b):
                            p, j = pj(b)
                            if b.after(2):
                                sp.wait_ge(finished, b.n - 1)
                                sp.nop(nofuse=True)
                            if b.after(2):
                                sp.wait_ge(stats[1], b.n - 1)
                                sp.nop(nofuse=True)
                            for t, table, width in ((sum_s, sums[GATW], GATW), (x_s, x2, D), (inv, dinv, 1)):
                                sp.dma_start(t[b.s][0:p, 0:j * width], rows(table, b)).then_inc(loaded[b.s], DMA)

                        def store(b):
                            p, j = pj(b)
                            sp.wait_ge(normed_x[1], b.n + 1)
                            sp.nop(nofuse=True)
                            sp.wait_ge(finished, b.n + 1)
                            sp.nop(nofuse=True)
                            sp.dma_start(rows(x3, b), o_s[b.s][0:p, 0:j * D]).then_inc(stored[b.s], DMA)
                            sp.dma_start(rows(scaled[64], b), g_s[b.s][0:p, 0:j * H1]).then_inc(stored[b.s], DMA)

                        pipeline(sp, NB, [(store, 2), (load, 0)])
                        for s in two:
                            sp.wait_ge(stored[s], blocks_in(NB, s) * 2 * DMA)

                    @block.vector
                    def _(dve):
                        link_a, link_w = Steps(vec_step, 2), Steps(vec_step_b, 2)
                        link_f, link_g = Steps(factor_step[0], 1), Steps(factor_step[1], 1)
                        link_b, link_c = Steps(vec_step_c, 2), Steps(vec_step_d, 2)

                        def base(b):
                            p, j = pj(b)
                            link_a.at(b)
                            dve.wait_ge(loaded[b.s], (b.pair + 1) * 3 * DMA)
                            dve.nop(nofuse=True)
                            if b.after(2):
                                dve.wait_ge(normed_x[0], b.n - 1)
                                dve.nop(nofuse=True)
                            if b.after(2):
                                dve.wait_ge(normed_x[1], b.n - 1)
                                dve.nop(nofuse=True)
                            both = split(sum_s[b.s], p, j, GATW)
                            nc.vector.tensor_scalar(weight[b.s][0:p, 0:j * 3].rearrange("p (j h) -> p j h", h=3),
                                                    both[:, :, D:D + 3], 1.0, None, ALU.add)
                            nc.vector.tensor_tensor(split(r_s[b.s], p, j), both[:, :, 0:D],
                                                    split(x_s[b.s], p, j), ALU.add).then_inc(link_a.sem, 1)
                            dve.wait_ge(link_a.sem, link_a.count())
                            dve.nop(nofuse=True)
                            nc.vector.tensor_tensor(split(r_s[b.s], p, j), split(r_s[b.s], p, j),
                                                    row_of(gat_row, p, j), ALU.add).then_inc(link_a.sem, 1)
                            dve.wait_ge(link_a.sem, link_a.count())
                            dve.nop(nofuse=True)

                        def loops(b):
                            p, j = pj(b)
                            link_w.at(b)
                            for q in range(j):
                                r = r_s[b.s][0:p, q * D:(q + 1) * D]
                                dve.wait_ge(multiplied, b.n * J + q + 1)
                                dve.nop(nofuse=True)
                                for h in range(3):
                                    ins = nc.vector.scalar_tensor_tensor(
                                        out=r, in0=p_h[q % 2][0:p, h * D:(h + 1) * D],
                                        scalar=weight[b.s][0:p, q * 3 + h:q * 3 + h + 1], in1=r, op0=ALU.mult,
                                        op1=ALU.add)
                                    ins.then_inc(loop_step, 1)
                                    dve.wait_ge(loop_step, (b.n * J + q) * 3 + h + 1)
                                    dve.nop(nofuse=True)
                            n1.variance(link_w, r_s[b.s], b, stats[0])

                        def factors_1(b):
                            link_f.at(b)
                            dve.wait_ge(rooted_x[0], b.n + 1)
                            dve.nop(nofuse=True)
                            n1.factors(link_f, b, factored[0])

                        def gain(b):
                            p, j = pj(b)
                            link_b.at(b)
                            dve.wait_ge(normed_x[0], b.n + 1)
                            dve.nop(nofuse=True)
                            v = split(r_s[b.s], p, j)
                            nc.vector.tensor_tensor(v, v, row_of(brow["L2_gnn_ln_g"], p, j), ALU.mult).then_inc(link_b.sem, 1)
                            dve.wait_ge(link_b.sem, link_b.count())
                            dve.nop(nofuse=True)
                            nc.vector.tensor_tensor(v, v, row_of(brow["L2_gnn_ln_b"], p, j), ALU.add).then_inc(link_b.sem, 1)
                            dve.wait_ge(link_b.sem, link_b.count())
                            dve.nop(nofuse=True)
                            nc.vector.tensor_tensor(v, v, split(x_s[b.s], p, j), ALU.add).then_inc(gained, 1)
                            dve.wait_ge(gained, b.n + 1)
                            dve.nop(nofuse=True)
                            link_c.at(b)
                            n2.variance(link_c, r_s[b.s], b, stats[1])

                        def factors_2(b):
                            link_g.at(b)
                            dve.wait_ge(rooted_x[1], b.n + 1)
                            dve.nop(nofuse=True)
                            n2.factors(link_g, b, factored[1])

                        def scale(b):
                            p, j = pj(b)
                            dve.wait_ge(scored, b.n + 1)
                            dve.nop(nofuse=True)
                            if b.after(2):
                                dve.wait_ge(stored[b.s], b.pair * 2 * DMA)
                                dve.nop(nofuse=True)
                            nc.vector.tensor_tensor(split(g_s[b.s], p, j, H1), split(p_g, p, j, H1),
                                                    per_row(inv[b.s], p, j, H1), ALU.mult).then_inc(finished, 1)

                        pipeline(dve, NB, [(scale, 2), (base, 0), (loops, 0), (factors_1, 0), (gain, 0), (factors_2, 0)])

                    @block.tensor
                    def _(pe):
                        def turn(b):
                            p, j = pj(b)
                            pe.wait_ge(loaded[b.s], (b.pair + 1) * 3 * DMA)
                            pe.nop(nofuse=True)
                            if b.after(1):
                                pe.wait_ge(evacuated, b.n)
                                pe.nop(nofuse=True)
                            turn_rows(p_x, x_s[b.s], p, j, D).then_inc(turned, 1)

                        def loops(b):
                            p, j = pj(b)
                            pe.wait_ge(evacuated, b.n + 1)
                            pe.nop(nofuse=True)
                            for q in range(j):
                                if b.after(1) or q > 1:
                                    pe.wait_ge(loop_step, (b.n * J + q - 1) * 3)
                                    pe.nop(nofuse=True)
                                nc.tensor.matmul(p_h[q % 2][0:p, :], x_t[:, q * P:q * P + p], head_w[:, :],
                                                 start=True, stop=True).then_inc(multiplied, 1)

                        def turn_x3(b):
                            p, j = pj(b)
                            pe.wait_ge(normed_x[1], b.n + 1)
                            pe.nop(nofuse=True)
                            if b.after(1):
                                pe.wait_ge(evacuated_b, b.n)
                                pe.nop(nofuse=True)
                            turn_rows(p_o, o_s[b.s], p, j, D).then_inc(turned_b, 1)

                        def next_weight(b):
                            p, j = pj(b)
                            pe.wait_ge(evacuated_b, b.n + 1)
                            pe.nop(nofuse=True)
                            if b.after(1):
                                pe.wait_ge(finished, b.n)
                                pe.nop(nofuse=True)
                            times_weight(p_g, o_t, w["L3_gnn_W1"][:, :], p, j, D, H1).then_inc(scored, 1)

                        pipeline(pe, NB, [(turn, 0), (loops, 0), (turn_x3, 1), (next_weight, 1)])

                    @block.scalar
                    def _(act):
                        def evacuate(b):
                            p, j = pj(b)
                            act.wait_ge(turned, b.n + 1)
                            act.nop(nofuse=True)
                            if b.after(1):
                                act.wait_ge(multiplied, b.n * J)
                                act.nop(nofuse=True)
                            nc.scalar.copy(cols(x_t, D, p, j), cols(p_x, D, p, j)).then_inc(evacuated, 1)

                        def root_1(b):
                            act.wait_ge(stats[0], b.n + 1)
                            act.nop(nofuse=True)
                            n1.root(b, rooted_x[0])

                        def normalise_1(b):
                            p, j = pj(b)
                            act.wait_ge(factored[0], b.n + 1)
                            act.nop(nofuse=True)
                            scale_rows(r_s[b.s], r_s[b.s], n1.rstd[b.s], n1.nmr[b.s], p, j).then_inc(normed_x[0], 1)

                        def root_2(b):
                            act.wait_ge(stats[1], b.n + 1)
                            act.nop(nofuse=True)
                            n2.root(b, rooted_x[1])

                        def normalise_2(b):
                            p, j = pj(b)
                            act.wait_ge(factored[1], b.n + 1)
                            act.nop(nofuse=True)
                            if b.after(2):
                                act.wait_ge(stored[b.s], b.pair * 2 * DMA)
                                act.nop(nofuse=True)
                            if b.after(2):
                                act.wait_ge(turned_b, b.n - 1)
                                act.nop(nofuse=True)
                            scale_rows(o_s[b.s], r_s[b.s], n2.rstd[b.s], n2.nmr[b.s], p, j).then_inc(normed_x[1], 1)

                        def evacuate_x3(b):
                            p, j = pj(b)
                            act.wait_ge(turned_b, b.n + 1)
                            act.nop(nofuse=True)
                            if b.after(1):
                                act.wait_ge(scored, b.n)
                                act.nop(nofuse=True)
                            nc.scalar.copy(cols(o_t, D, p, j), cols(p_o, D, p, j)).then_inc(evacuated_b, 1)

                        pipeline(act, NB, [(evacuate, 0), (evacuate_x3, 1), (root_1, 0), (normalise_1, 0), (root_2, 0),
                                           (normalise_2, 0)])
            end_pass()

        attention_edge_pass()
        attention_node_pass()

        edge_sum_pass("g3", 64, scaled[64], sums[64])
        aggregate_last_pass("n3", scaled[64], sums[64], brow["L3_gnn_b1"], 64, w["L3_gnn_W2"], 32, scaled[32])
        edge_sum_pass("g4", 32, scaled[32], sums[32])
        aggregate_last_pass("n4", scaled[32], sums[32], brow["L3_gnn_b2"], 32, w["L3_gnn_W3"], 16, scaled[16])
        edge_sum_pass("g5", 16, scaled[16], sums[16])
        aggregate_last_pass("n5", scaled[16], sums[16], brow["L3_gnn_b3"], 16, None, 16, scaled2[16])
        edge_sum_pass("g6", 16, scaled2[16], sums[16])
        aggregate_then_weight_pass("n6", scaled2[16], sums[16], w["L3_gnn_W4"], brow["L3_gnn_b4"], 16, 32, scaled2[32], 32)
        edge_sum_pass("g7", 32, scaled2[32], sums[32])
        aggregate_then_weight_pass("n7", scaled2[32], sums[32], w["L3_gnn_W5"], brow["L3_gnn_b5"], 32, 64, scaled2[64], 64)
        edge_sum_pass("g8", 64, scaled2[64], sums[64])
        aggregate_then_weight_pass("n8", scaled2[64], sums[64], w["L3_gnn_W6"], brow["L3_gnn_b6"], 64, D, out, D,
                                   residual=x3, last_w=w["L3_gnn_Wf"], last_bias=brow["L3_gnn_bf"])


_INS = [
    "x", "src", "dst", "edge_attr_16", "L0_gnn_W1", "L0_gnn_b1", "L0_gnn_W2", "L0_gnn_b2", "L1_gnn_Wf", "L1_gnn_bf",
    "L1_gnn_Ws", "L1_gnn_bs", "L1_gnn_bn_gamma", "L1_gnn_bn_beta", "L1_gnn_ln_gamma", "L1_gnn_ln_beta", "L2_gnn_W",
    "L2_gnn_W_edge", "L2_gnn_att_src", "L2_gnn_att_dst", "L2_gnn_att_edge", "L2_gnn_gat_bias", "L2_gnn_lin_W",
    "L2_gnn_lin_b", "L2_gnn_ln_g", "L2_gnn_ln_b", "L3_gnn_W1", "L3_gnn_b1", "L3_gnn_W2", "L3_gnn_b2", "L3_gnn_W3",
    "L3_gnn_b3", "L3_gnn_W4", "L3_gnn_b4", "L3_gnn_W5", "L3_gnn_b5", "L3_gnn_W6", "L3_gnn_b6", "L3_gnn_Wf", "L3_gnn_bf",
]


def kernel(**inputs):
    import numpy as _np
    import concourse.bacc as _bacc
    from concourse import mybir as _mybir
    from concourse.bass_utils import run_bass_kernel_spmd as _run

    nc = _bacc.Bacc("TRN2", target_bir_lowering=False, num_devices=1)
    arrays, aps = {}, {}
    for name in _INS:
        arr = _np.ascontiguousarray(inputs[name])
        arrays[f"in_{name}"] = arr
        aps[name] = nc.dram_tensor(f"in_{name}", arr.shape, _mybir.dt.from_np(arr.dtype), kind="ExternalInput").ap()
    shape = inputs["x"].shape
    out = nc.dram_tensor("out_0", shape, _mybir.dt.float32, kind="ExternalOutput").ap()
    build(nc, aps, out)
    r = _run(nc, [arrays], core_ids=[0])
    return r.results[0]["out_0"]
```

```python
from contextlib import ExitStack

import concourse.bass as bass
from concourse import mybir

P = 128
F32 = mybir.dt.float32
I32 = mybir.dt.int32
U32 = mybir.dt.uint32
BF16 = mybir.dt.bfloat16
ALU = mybir.AluOpType
ACT = mybir.ActivationFunctionType
AX = mybir.AxisListType.X

EDGE_BLOCK = 512
CH = EDGE_BLOCK // P
DMA = 16
NOWHERE = 1 << 20
FAR = 1.0e30
EPS = 1e-5
ZERO_RUN = 2048
D = 128
AUXW = 20
ADW = 8
GATW = 132


class Block:

    def __init__(self, pair, slot, tail):
        self.pair, self.s, self.tail = pair, slot, tail
        self.n = pair * 2 + slot

    def after(self, k):
        return not isinstance(self.n, int) or self.n >= k


def pipeline(eng, blocks, stages):
    most = max(lag for _, lag in stages)
    start = most + 2 + most % 2
    end = max(start, blocks - 2)
    end -= (end - start) % 2

    def step(pair, u):
        for fn, lag in stages:
            down, slot = divmod(u - lag, 2)
            at = pair + down
            if isinstance(at, int):
                n = 2 * at + slot
                if 0 <= n < blocks:
                    fn(Block(at, slot, n == blocks - 1))
            else:
                fn(Block(at, slot, False))

    for t in range(min(start, blocks + most)):
        step(t // 2, t % 2)
    if end > start:
        with eng.Fori(start // 2, end // 2) as i:
            step(i, 0)
            step(i, 1)
    for t in range(end, blocks + most):
        step(t // 2, t % 2)


def build(nc, a, out):
    N = a["x"].shape[0]
    E = a["src"].shape[0]
    EB = -(-E // EDGE_BLOCK)
    EP = EB * EDGE_BLOCK
    edge_left = E - (EB - 1) * EDGE_BLOCK
    assert edge_left % CH == 0
    edge_tail_p = edge_left // CH

    def node_blocks(per):
        size = P * per
        blocks = -(-N // size)
        left = N - (blocks - 1) * size
        last_p = max(p for p in range(16, P + 1, 16) if left % p == 0 and left // p <= per)

        def pj(b):
            return (last_p, left // last_p) if b.tail else (P, per)

        def rows(table, b):
            p, j = pj(b)
            return table[bass.ds(b.n * size, p * j), :].rearrange("(p j) f -> p (j f)", p=p)

        return per, blocks, pj, rows

    def can_cut(per):
        left = N % (P * per) or P * per
        return any(left % p == 0 and left // p <= per for p in range(16, P + 1, 16))

    J, NB, pj, rows = node_blocks(8)
    LONG = max(per for per in range(8, 17) if can_cut(per))

    with ExitStack() as whole:
        def keep(name, shape, dt=F32):
            return whole.enter_context(nc.sbuf_tensor(name, shape, dt))

        def dram(name, shape, dt=F32):
            return nc.dram_tensor(name, shape, dt, kind="Internal").ap()

        def sem(name):
            return whole.enter_context(nc.semaphore(name))

        src_i = dram("src_idx", [EP // CH, CH], U32)
        dst_i = dram("dst_idx", [EP // CH, CH], U32)
        end_i = dram("end_idx", [EP // CH, CH], U32)
        aux = dram("aux", [N, AUXW])
        dinv = dram("dinv", [N, 1])
        att = dram("att", [N, ADW])
        x1, x2, x3 = (dram(f"x{i}", [N, D]) for i in (1, 2, 3))
        wide = [dram(f"wide{i}", [N, D]) for i in range(2)]
        scaled = {w: dram(f"scaled{w}", [N, w]) for w in (64, 32, 16)}
        scaled2 = {w: dram(f"scaled2_{w}", [N, w]) for w in (64, 32, 16)}
        sums = {w: dram(f"sums{w}", [N, w]) for w in (GATW, 128, 64, 32, 16)}

        gathered = [sem(f"gathered{s}") for s in range(2)]
        gathered_dst = [sem(f"gathered_dst{s}") for s in range(2)]
        scattered = [sem(f"scattered{s}") for s in range(2)]
        so_far = {s.num: 0 for s in (*gathered, *gathered_dst, *scattered)}
        setup_loaded = sem("setup_loaded")
        setup_step = sem("setup_step")
        setup_pe = sem("setup_pe")
        setup_stored = sem("setup_stored")
        src_loaded = [sem(f"src_loaded{s}") for s in range(2)]
        dst_loaded = [sem(f"dst_loaded{s}") for s in range(2)]
        end_loaded = [sem(f"end_loaded{s}") for s in range(2)]
        attr_loaded = [sem(f"attr_loaded{s}") for s in range(2)]
        zeroed = sem("zeroed")
        prepared = sem("prepared")
        evicted = sem("evicted")
        piece_loaded = sem("piece_loaded")
        compared = sem("compared")
        indexed = sem("indexed")
        turned = sem("turned")
        evacuated = sem("evacuated")
        gates_in = sem("gates_in")
        act_step = sem("act_step")
        vec_step = sem("vec_step")
        scanned = sem("scanned")
        spread = sem("spread")
        turned_back = sem("turned_back")
        rows_ready = sem("rows_ready")
        loaded = [sem(f"loaded{s}") for s in range(2)]
        loaded_b = [sem(f"loaded_b{s}") for s in range(2)]
        stored = [sem(f"stored{s}") for s in range(2)]
        multiplied = sem("multiplied")
        summed = sem("summed")
        rooted = sem("rooted")
        rooted_b = sem("rooted_b")
        normed = sem("normed")
        normed_b = sem("normed_b")
        turned_b = sem("turned_b")
        evacuated_b = sem("evacuated_b")
        multiplied_b = sem("multiplied_b")
        finished = sem("finished")
        gates_out = sem("gates_out")
        stats = [sem(f"stats{i}") for i in range(2)]
        rooted_x = [sem(f"rooted_x{i}") for i in range(2)]
        factored = [sem(f"factored{i}") for i in range(2)]
        factor_step = [sem(f"factor_step{i}") for i in range(2)]
        normed_x = [sem(f"normed_x{i}") for i in range(2)]
        gained = sem("gained")
        scored = sem("scored")
        attended = sem("attended")
        leaked = sem("leaked")
        powered = sem("powered")
        taken = sem("taken")
        loop_step = sem("loop_step")
        vec_step_b = sem("vec_step_b")
        vec_step_c = sem("vec_step_c")
        vec_step_d = sem("vec_step_d")
        loaded_c = [sem(f"loaded_c{s}") for s in range(2)]
        pooled = sem("pooled")
        pooled_b = sem("pooled_b")
        pooled_c = sem("pooled_c")
        summed_b = sem("summed_b")
        pool_step = sem("pool_step")
        doubled = sem("doubled")
        g_used = sem("g_used")
        soft_ready = sem("soft_ready")
        spread_b = sem("spread_b")
        weighted = sem("weighted")
        denom_turned = sem("denom_turned")
        denom_taken = sem("denom_taken")
        high_ready = sem("high_ready")
        rest_ready = sem("rest_ready")
        middle_ready = sem("middle_ready")
        low_ready = sem("low_ready")
        parts_ready = sem("parts_ready")
        own_turned = sem("own_turned")
        per_pass = [setup_loaded, setup_step, setup_pe, setup_stored, *src_loaded, *dst_loaded, *end_loaded,
                    *attr_loaded, zeroed, prepared, evicted,
                    piece_loaded, compared, indexed, turned, evacuated,
                    gates_in, act_step, vec_step, scanned, spread, turned_back, rows_ready, *loaded, *loaded_b,
                    *stored, multiplied, summed, rooted, rooted_b, normed, normed_b, turned_b, evacuated_b,
                    multiplied_b, finished, gates_out, *stats, *rooted_x, *factored, *factor_step, *normed_x,
                    gained, scored, attended, leaked, powered, taken,
                    loop_step, vec_step_b, vec_step_c, vec_step_d, *loaded_c, pooled, pooled_b,
                    pooled_c, summed_b, pool_step, doubled, g_used, soft_ready,
                    spread_b, weighted, denom_turned, denom_taken, high_ready, rest_ready,
                    middle_ready, low_ready, parts_ready, own_turned]

        def past(s):
            return so_far[s.num]

        class Steps:

            def __init__(self, sem_, per):
                self.sem, self.per, self.k, self.base = sem_, per, 0, 0

            def at(self, b):
                assert self.k in (0, self.per)
                self.base, self.k = b.n * self.per, 0

            def count(self):
                self.k += 1
                assert self.k <= self.per
                return self.base + self.k

        def blocks_in(blocks, s):
            return (blocks - s + 1) // 2

        def end_pass(*pool_sems):
            for slots in pool_sems:
                for s in range(2):
                    so_far[slots[s].num] += blocks_in(EB, s) * CH * DMA
            lo = min(s.num for s in per_pass)
            hi = max(s.num for s in per_pass)
            assert hi - lo + 1 == len(per_pass)
            nc.gpsimd.sem_clear(range(lo, hi + 1))
            nc.all_engine_barrier()

        def write_zeros(eng, table, zeros):
            per = table.shape[0] * table.shape[1] // P
            run = max(f for f in range(1, ZERO_RUN + 1) if per % f == 0)
            eng.dma_start(table.rearrange("n f -> (n f)").rearrange("(p k f) -> p k f", p=P, f=run),
                          zeros[:, 0:run].unsqueeze(1).to_broadcast([P, per // run, run])).then_inc(zeroed, DMA)

        ident = keep("ident", [P, P])
        cont = keep("cont", [P, EP + 4], BF16)
        eps = keep("eps", [P, 1])
        w = {}
        for name, (k, m) in {
            "L0_gnn_W1": (128, 128), "L0_gnn_W2": (128, 128), "L3_gnn_W1": (128, 64), "L3_gnn_W2": (64, 32),
            "L3_gnn_W3": (32, 16), "L3_gnn_W4": (16, 32), "L3_gnn_W5": (32, 64), "L3_gnn_W6": (64, 128),
            "L3_gnn_Wf": (128, 128),
        }.items():
            w[name] = keep("sb_" + name, [k, m])
        brow = {}
        for name in ("L0_gnn_b1", "L0_gnn_b2", "L1_gnn_ln_gamma", "L1_gnn_ln_beta", "L2_gnn_ln_g", "L2_gnn_ln_b",
                     "L3_gnn_b1", "L3_gnn_b2", "L3_gnn_b3", "L3_gnn_b4", "L3_gnn_b5", "L3_gnn_b6", "L3_gnn_bf"):
            brow[name] = keep("row_" + name, [P, a[name].shape[0]])
        gate_w = {g: [keep(f"gate_{g}{i}", [k, D]) for i, k in enumerate((D, D, 17))] for g in "fs"}
        bn_scale = keep("bn_scale", [P, D])
        bn_shift = keep("bn_shift", [P, D])
        bn_part = keep("bn_part", [P, EB * 6])
        head_w = keep("head_w", [P, 3 * D])
        score_w = keep("score_w", [P, 6])
        edge_w = keep("edge_w", [ADW + 16, 6])
        loop_w = keep("loop_w", [P, 3 * 16])
        gat_row = keep("gat_row", [P, D])
        pick_b = keep("pick_b", [67, 3 * D], BF16)
        pick = keep("pick", [3, 3 * D])

        with ExitStack() as ctx:
            def sb(name, shape, dt=F32):
                return ctx.enter_context(nc.sbuf_tensor(name, shape, dt))

            dst_a = sb("dst_a", [P, EB, CH], I32)
            dst_n = sb("dst_n", [P, EB, CH], I32)
            src_a = sb("src_a", [P, EB, CH], I32)
            end_a = sb("end_a", [P, EB, CH], I32)
            PIECE = EP // 16
            dst_b = sb("dst_b", [P, PIECE + 1], I32)
            wf = sb("wf", [P, 2 * D + 16])
            ws = sb("ws", [P, 2 * D + 16])
            gat_w = sb("gat_w", [P, 3 * D])
            gat_we = sb("gat_we", [16, 3 * D])
            att_rows = sb("att_rows", [9, D])
            att_cols = sb("att_cols", [P, 9])
            lin_w = sb("lin_w", [P, 3, D])
            gat_b = sb("gat_b", [P, 3])
            gat_bb = sb("gat_bb", [P, 3, P])
            lin_b = sb("lin_b", [P, D])
            turned_w = sb("turned_w", [P, 3, D])
            turned_we = sb("turned_we", [P, 3, 16])
            veb = sb("veb", [P, 3, P])
            zeros = sb("zeros", [P, ZERO_RUN])
            ps_a = ctx.enter_context(nc.psum_tensor("ps_a", [P, 512], F32))
            ps_b = ctx.enter_context(nc.psum_tensor("ps_b", [P, 512], F32))
            main_e = (EB - 1) * EDGE_BLOCK
            n_loads = 7 + len(w) + len(brow) + 2 + 2 + 2 + 3 + 3

            with nc.Block() as block:
                @block.gpsimd
                def _(pool):
                    nc.gpsimd.memset(ident[:, :], 0.0).then_inc(setup_step, 1)
                    nc.gpsimd.memset(pick[:, :], 0.0).then_inc(setup_step, 1)
                    nc.gpsimd.memset(edge_w[:, :], 0.0).then_inc(setup_step, 1)
                    pool.wait_ge(setup_step, 3)
                    nc.gpsimd.affine_select(out=ident[:, :], in_=ident[:, :], compare_op=ALU.not_equal, fill=1.0,
                                            base=0, pattern=[[-1, P]], channel_multiplier=1).then_inc(setup_step, 1)
                    nc.gpsimd.affine_select(out=pick[:, :].rearrange("p (h f) -> p h f", h=3),
                                            in_=pick[:, :].rearrange("p (h f) -> p h f", h=3),
                                            compare_op=ALU.not_equal, fill=1.0, base=0, pattern=[[-1, 3], [0, D]],
                                            channel_multiplier=1).then_inc(setup_step, 1)
                    nc.gpsimd.affine_select(out=edge_w[:, :], in_=edge_w[:, :],
                                            compare_op=ALU.not_equal, fill=1.0, base=0, pattern=[[-1, 6]],
                                            channel_multiplier=1).then_inc(setup_step, 1)
                    nc.gpsimd.memset(src_a[:, :, :], 0).then_inc(setup_step, 1)
                    nc.gpsimd.memset(dst_a[:, :, :], NOWHERE).then_inc(setup_step, 1)
                    nc.gpsimd.memset(dst_n[:, :, :], -1).then_inc(setup_step, 1)

                @block.sync
                def _(sp):
                    def fill(tile, table, shift):
                        sp.dma_start(tile[:, 0:EB - 1, :],
                                     table[shift:shift + main_e].rearrange("(b p c) -> p b c", p=P, c=CH)
                                     ).then_inc(setup_loaded, DMA)
                        if not shift:
                            sp.dma_start(tile[0:edge_tail_p, EB - 1, :],
                                         table[main_e:E].rearrange("(p c) -> p c", c=CH)).then_inc(setup_loaded, DMA)
                        else:
                            sp.dma_start(tile[0:edge_tail_p - 1, EB - 1, :],
                                         table[main_e + 1:E - CH + 1].rearrange("(p c) -> p c", c=CH)
                                         ).then_inc(setup_loaded, DMA)
                            sp.dma_start(tile[edge_tail_p - 1:edge_tail_p, EB - 1, 0:CH - 1],
                                         table[E - CH + 1:E].rearrange("(p c) -> p c", p=1)
                                         ).then_inc(setup_loaded, DMA)

                    sp.wait_ge(setup_step, 9)
                    with nc.allow_non_contiguous_dma(reason="index tables, once"):
                        fill(src_a, a["src"], 0)
                        fill(dst_a, a["dst"], 0)
                        fill(dst_n, a["dst"], 1)
                        for name, t in w.items():
                            sp.dma_start(t[:, :], a[name]).then_inc(setup_loaded, DMA)
                        for name, t in brow.items():
                            sp.dma_start(t[:, :], a[name].partition_broadcast(P)).then_inc(setup_loaded, DMA)
                        sp.dma_start(wf[:, :], a["L1_gnn_Wf"]).then_inc(setup_loaded, DMA)
                        sp.dma_start(ws[:, :], a["L1_gnn_Ws"]).then_inc(setup_loaded, DMA)
                        for g, name in (("f", "L1_gnn_bf"), ("s", "L1_gnn_bs")):
                            sp.dma_start(gate_w[g][2][16:17, :], a[name].rearrange("(o d) -> o d", o=1)
                                         ).then_inc(setup_loaded, DMA)
                        sp.dma_start(gat_w[:, :], a["L2_gnn_W"]).then_inc(setup_loaded, DMA)
                        sp.dma_start(gat_we[:, :], a["L2_gnn_W_edge"]).then_inc(setup_loaded, DMA)
                        for i, name in enumerate(("L2_gnn_att_src", "L2_gnn_att_dst", "L2_gnn_att_edge")):
                            sp.dma_start(att_rows[3 * i:3 * i + 3, :], a[name]).then_inc(setup_loaded, DMA)
                        sp.dma_start(lin_w[:, :, :], a["L2_gnn_lin_W"].rearrange("(h c) o -> c h o", h=3)
                                     ).then_inc(setup_loaded, DMA)
                        sp.dma_start(gat_b[:, :], a["L2_gnn_gat_bias"].rearrange("(h c) -> c h", h=3)
                                     ).then_inc(setup_loaded, DMA)
                        sp.dma_start(lin_b[:, :], a["L2_gnn_lin_b"].partition_broadcast(P)).then_inc(setup_loaded, DMA)
                        for k in range(16):
                            lo, hi = k * PIECE, min((k + 1) * PIECE, E)
                            first = 1 if k == 0 else 0
                            if k:
                                sp.wait_ge(compared, k)
                            sp.dma_start(dst_b[:, first:hi - lo + 1],
                                         a["dst"][lo - 1 + first:hi].partition_broadcast(P)
                                         ).then_inc(piece_loaded, DMA)
                        for t, table in ((src_a, src_i), (dst_a, dst_i), (end_a, end_i)):
                            if t is src_a:
                                sp.wait_ge(setup_loaded, DMA * n_loads)
                                sp.wait_ge(indexed, 1)
                            sp.dma_start(table.rearrange("(b p) c -> p b c", p=P), t[:, :, :].bitcast(U32)
                                         ).then_inc(setup_stored, DMA)
                    sp.wait_ge(setup_stored, DMA * 3)

                def weight_steps(pe, done_moves):
                    bank = [ps_a, ps_b]

                    def emit(fn, shape, to):
                        k = len(done_moves)
                        out_ap = bank[k % 2][0:shape[0], 0:shape[1]]
                        done_moves.append((to, out_ap))
                        if pe is not None:
                            if k >= 2:
                                pe.wait_ge(evicted, k - 1)
                            fn(out_ap).then_inc(setup_pe, 1)

                    def turn(src_ap, to):
                        k, m = src_ap.shape
                        emit(lambda o: nc.tensor.transpose(o, src_ap, ident[0:k, 0:k]), (m, k), to)

                    for g, t in (("f", wf), ("s", ws)):
                        for i in range(2):
                            turn(t[:, i * D:(i + 1) * D], gate_w[g][i][:, :])
                        turn(t[:, 2 * D:2 * D + 16], gate_w[g][2][0:16, :])
                    turn(att_rows[:, :], att_cols)
                    for h in range(3):
                        turn(gat_w[:, h * D:(h + 1) * D], turned_w[:, h, :])
                    for h in range(3):
                        turn(gat_we[:, h * D:(h + 1) * D], turned_we[:, h, :])
                    if pe is not None:
                        pe.wait_ge(evicted, len(done_moves))
                    for h in range(3):
                        emit(lambda o, h=h: nc.tensor.matmul(o, turned_w[:, h, :], lin_w[:, h, :], start=True, stop=True),
                             (P, D), head_w[:, h * D:(h + 1) * D])
                    for i in range(2):
                        for h in range(3):
                            emit(lambda o, h=h, i=i: nc.tensor.matmul(
                                o, turned_w[:, h, :], att_cols[:, 3 * i + h:3 * i + h + 1], start=True, stop=True),
                                (P, 1), score_w[:, 3 * i + h:3 * i + h + 1])
                    for h in range(3):
                        emit(lambda o, h=h: nc.tensor.matmul(o, veb[:, h, :], turned_we[:, h, :], start=True, stop=True),
                             (P, 16), loop_w[:, 16 * h:16 * h + 16])

                    def lin(o):
                        for h in range(3):
                            last = nc.tensor.matmul(o, gat_bb[:, h, :], lin_w[:, h, :], start=(h == 0), stop=(h == 2))
                        return last
                    emit(lin, (P, D), gat_row)


                @block.scalar
                def _(act):
                    act.wait_ge(setup_step, 9)
                    nc.scalar.activation(zeros[:, :], ident[:, 0:1].to_broadcast([P, ZERO_RUN]), ACT.Copy, scale=0.0
                                         ).then_inc(prepared, 1)
                    act.wait_ge(prepared, 1)
                    write_zeros(act, aux, zeros)
                    act.wait_ge(zeroed, DMA)

                moves = []
                weight_steps(None, moves)

                @block.vector
                def _(dve):
                    step = Steps(vec_step, 999)
                    nc.vector.memset(eps[:, :], EPS)
                    nc.vector.memset(cont[:, :], 0.0).then_inc(step.sem, 1)
                    dve.wait_ge(step.sem, step.count())
                    dve.wait_ge(setup_step, 9)
                    dve.wait_ge(setup_loaded, DMA * n_loads)
                    nc.vector.memset(pick_b[:, :], 0.0).then_inc(step.sem, 1)
                    dve.wait_ge(step.sem, step.count())
                    for i in range(3):
                        nc.vector.tensor_copy(pick_b[32 * i:32 * i + 3, :], pick[:, :])
                    nc.vector.tensor_tensor(end_a[:, :, :], dst_a[:, :, :], dst_n[:, :, :], ALU.is_equal).then_inc(step.sem, 1)
                    dve.wait_ge(step.sem, step.count())
                    nc.vector.scalar_tensor_tensor(out=end_a[:, :, :], in0=end_a[:, :, :], scalar=float(NOWHERE),
                                                   in1=dst_a[:, :, :], op0=ALU.mult, op1=ALU.add).then_inc(step.sem, 1)
                    dve.wait_ge(step.sem, step.count())
                    nc.vector.tensor_scalar(dst_n[:, :, :], dst_a[:, :, :], float(NOWHERE), None, ALU.is_lt).then_inc(step.sem, 1)
                    dve.wait_ge(step.sem, step.count())
                    nc.vector.tensor_tensor(dst_a[:, :, :], dst_a[:, :, :], dst_n[:, :, :], ALU.mult).then_inc(step.sem, 1)
                    dve.wait_ge(step.sem, step.count())
                    dve.sem_inc(indexed, 1)
                    for g in range(3):
                        nc.vector.tensor_copy(gat_bb[:, g, :], gat_b[:, g:g + 1].to_broadcast([P, P])).then_inc(step.sem, 1)
                        dve.wait_ge(step.sem, step.count())

                    for k, (dst_ap, src_ap) in enumerate(moves):
                        dve.wait_ge(setup_pe, k + 1)
                        if dst_ap is att_cols:
                            nc.vector.tensor_copy(att_cols[:, :], src_ap).then_inc(step.sem, 1)
                            dve.wait_ge(step.sem, step.count())
                            for h in range(3):
                                nc.vector.tensor_copy(veb[:, h, :], att_cols[:, 6 + h:7 + h].to_broadcast([P, P])).then_inc(step.sem, 1)
                                dve.wait_ge(step.sem, step.count())
                        elif dst_ap is gat_row:
                            nc.vector.tensor_tensor(gat_row[:, :], src_ap, lin_b[:, :], ALU.add).then_inc(step.sem, 1)
                            dve.wait_ge(step.sem, step.count())
                        else:
                            nc.vector.tensor_copy(dst_ap, src_ap).then_inc(step.sem, 1)
                            dve.wait_ge(step.sem, step.count())
                        dve.sem_inc(evicted, 1)
                    for k in range(16):
                        lo, hi = k * PIECE, min((k + 1) * PIECE, E)
                        first = 1 if k == 0 else 0
                        dve.wait_ge(piece_loaded, DMA * (k + 1))
                        nc.vector.tensor_tensor(cont[:, lo + first:hi], dst_b[:, 1 + first:hi - lo + 1],
                                                dst_b[:, first:hi - lo], ALU.is_equal).then_inc(step.sem, 1)
                        dve.wait_ge(step.sem, step.count())
                        dve.sem_inc(compared, 1)

                @block.tensor
                def _(pe):
                    pe.wait_ge(setup_step, 9)
                    pe.wait_ge(setup_loaded, DMA * n_loads)
                    pe.wait_ge(vec_step, 9)
                    weight_steps(pe, [])

            end_pass()
            with nc.Block() as block:
                @block.sync
                def _(sp):
                    with nc.allow_non_contiguous_dma(reason="48 numbers"):
                        sp.dma_start(dinv[0:48, :].rearrange("n o -> o n"), loop_w[0:1, :]).then_inc(setup_stored, DMA)
                        sp.wait_ge(setup_stored, DMA)
                        sp.dma_start(edge_w[ADW:ADW + 16, 0:3], dinv[0:48, :].rearrange("(h k) o -> k (h o)", h=3)
                                     ).then_inc(setup_stored, DMA)
                        sp.wait_ge(setup_stored, 2 * DMA)
            end_pass()

        def edge_sum_pass(tag, width, table, sum_table, from_attr=False, zero=()):
            with ExitStack() as ctx:
                def sb(name, shape, dt=F32):
                    return ctx.enter_context(nc.sbuf_tensor(f"{tag}_{name}", shape, dt))

                def ps(name, shape):
                    return ctx.enter_context(nc.psum_tensor(f"{tag}_{name}", shape, F32))

                src_s = [sb(f"src{s}", [P, CH], U32) for s in range(2)]
                end_s = [sb(f"end{s}", [P, CH], U32) for s in range(2)]
                got = [sb(f"got{s}", [P, CH, width]) for s in range(2)]
                run = [sb(f"run{s}", [width, EDGE_BLOCK]) for s in range(2)]
                res = [sb(f"res{s}", [P, CH, width]) for s in range(2)]
                zeros = sb("zeros", [P, ZERO_RUN])
                p_in = [ps(f"p_in{s}", [P, EDGE_BLOCK]) for s in range(2)]
                p_out = [ps(f"p_out{s}", [P, CH * width]) for s in range(2)]
                got_sem, got_count = (attr_loaded, DMA) if from_attr else (gathered, CH * DMA)
                got_before = [0, 0] if from_attr else [past(gathered[s]) for s in range(2)]

                with nc.Block() as block:
                    @block.sync
                    def _(sp):
                        def load_src(b):
                            if b.after(2):
                                sp.wait_ge(gathered[b.s], past(gathered[b.s]) + b.pair * CH * DMA)
                                sp.nop(nofuse=True)
                            sp.dma_start(src_s[b.s][:, :], src_i[bass.ds(b.n * P, P), :]).then_inc(src_loaded[b.s], DMA)

                        def load_attr(b):
                            sp.wait_ge(prepared, 2)
                            if b.after(2):
                                sp.wait_ge(turned, b.n - 1)
                                sp.nop(nofuse=True)
                            p = edge_tail_p if b.tail else P
                            sp.dma_start(got[b.s][0:p, :, 0:16], a["edge_attr_16"][bass.ds(b.n * EDGE_BLOCK, p * CH), :]
                                         .rearrange("(p c) f -> p c f", p=p)).then_inc(attr_loaded[b.s], DMA)

                        def load_end(b):
                            if b.after(2):
                                sp.wait_ge(scattered[b.s], past(scattered[b.s]) + b.pair * CH * DMA)
                                sp.nop(nofuse=True)
                            sp.dma_start(end_s[b.s][:, :], end_i[bass.ds(b.n * P, P), :]).then_inc(end_loaded[b.s], DMA)

                        pipeline(sp, EB, [(load_attr if from_attr else load_src, 0), (load_end, 2)])

                    @block.gpsimd
                    def _(pool):
                        def gather(b):
                            pool.wait_ge(src_loaded[b.s], (b.pair + 1) * DMA)
                            pool.nop(nofuse=True)
                            if b.after(2):
                                pool.wait_ge(turned, b.n - 1)
                                pool.nop(nofuse=True)
                            for j in range(CH):
                                pool.indirect_dma_start(
                                    got[b.s][:, j, :], None, table,
                                    bass.IndirectOffsetOnAxis(ap=src_s[b.s][:, j:j + 1], axis=0)
                                ).then_inc(gathered[b.s], DMA)

                        def scatter(b):
                            pool.wait_ge(end_loaded[b.s], (b.pair + 1) * DMA)
                            pool.nop(nofuse=True)
                            pool.wait_ge(rows_ready, b.n + 1)
                            pool.nop(nofuse=True)
                            for j in range(CH):
                                pool.indirect_dma_start(
                                    sum_table, bass.IndirectOffsetOnAxis(ap=end_s[b.s][:, j:j + 1], axis=0),
                                    res[b.s][:, j, :], None, bounds_check=N - 1, oob_is_err=False
                                ).then_inc(scattered[b.s], DMA)

                        pipeline(pool, EB, [(scatter, 2)] if from_attr else [(gather, 0), (scatter, 2)])
                        for s in range(2):
                            pool.wait_ge(scattered[s], past(scattered[s]) + blocks_in(EB, s) * CH * DMA)

                    @block.tensor
                    def _(pe):
                        def turn(b):
                            pe.wait_ge(got_sem[b.s], got_before[b.s] + (b.pair + 1) * got_count)
                            pe.nop(nofuse=True)
                            if b.after(2):
                                pe.wait_ge(scanned, b.n - 1)
                                pe.nop(nofuse=True)
                            for j in range(CH):
                                last = nc.tensor.transpose(p_in[b.s][0:width, j:EDGE_BLOCK:CH], got[b.s][:, j, :],
                                                           ident[:, :])
                            last.then_inc(turned, 1)

                        def turn_back(b):
                            pe.wait_ge(scanned, b.n + 1)
                            pe.nop(nofuse=True)
                            if b.after(2):
                                pe.wait_ge(rows_ready, b.n - 1)
                                pe.nop(nofuse=True)
                            for j in range(CH):
                                last = nc.tensor.transpose(p_out[b.s][:, j * width:(j + 1) * width],
                                                           run[b.s][:, j:EDGE_BLOCK:CH], ident[0:width, 0:width])
                            last.then_inc(turned_back, 1)

                        pipeline(pe, EB, [(turn, 0), (turn_back, 1)])

                    @block.vector
                    def _(dve):
                        def scan(b):
                            dve.wait_ge(turned, b.n + 1)
                            dve.nop(nofuse=True)
                            if b.after(2):
                                dve.wait_ge(turned_back, b.n - 1)
                                dve.nop(nofuse=True)
                            if b.after(1):
                                dve.wait_ge(scanned, b.n)
                                dve.nop(nofuse=True)
                            first = isinstance(b.n, int) and b.n == 0
                            nc.vector.tensor_tensor_scan(
                                run[b.s][:, :], cont[0:width, bass.ds(b.n * EDGE_BLOCK, EDGE_BLOCK)],
                                p_in[b.s][0:width, :],
                                0.0 if first else run[1 - b.s][:, EDGE_BLOCK - 1:EDGE_BLOCK],
                                ALU.mult, ALU.add).then_inc(scanned, 1)

                        pipeline(dve, EB, [(scan, 0)])

                    @block.scalar
                    def _(act):
                        def copy_rows(b):
                            act.wait_ge(turned_back, b.n + 1)
                            act.nop(nofuse=True)
                            if b.after(2):
                                act.wait_ge(scattered[b.s], past(scattered[b.s]) + b.pair * CH * DMA)
                                act.nop(nofuse=True)
                            nc.scalar.copy(res[b.s][:, :, :].rearrange("p c f -> p (c f)"), p_out[b.s][:, :]
                                           ).then_inc(rows_ready, 1)

                        def fill(ap, value):
                            nc.scalar.activation(ap, ident[:, 0:1].to_broadcast(list(ap.shape)), ACT.Copy, scale=0.0,
                                                 bias=value).then_inc(prepared, 1)

                        if from_attr:
                            for s in range(2):
                                fill(got[s][:, :, :].rearrange("p c f -> p (c f)"), 1.0)
                        if zero:
                            fill(zeros[:, :], 0.0)
                            act.wait_ge(prepared, 3 if from_attr else 1)
                            for z in zero:
                                write_zeros(act, z, zeros)
                        pipeline(act, EB, [(copy_rows, 0)])
                        if zero:
                            act.wait_ge(zeroed, DMA * len(zero))
            end_pass(scattered, *([] if from_attr else [gathered]))


        def per_row(t, p, j, width):
            return t[0:p, 0:j].unsqueeze(2).to_broadcast([p, j, width])

        def split(t, p, j, width=D):
            return t[0:p, 0:j * width].rearrange("p (j f) -> p j f", f=width)

        def turn_rows(dst_psum, tile, p, j, width):
            for q in range(j):
                last = nc.tensor.transpose(dst_psum[0:width, q * P:q * P + p], tile[0:p, q * width:(q + 1) * width],
                                           ident[0:p, 0:p])
            return last

        def times_weight(dst_psum, turned_tile, weight, p, j, k, width):
            for q in range(j):
                last = nc.tensor.matmul(dst_psum[0:p, q * width:(q + 1) * width], turned_tile[0:k, q * P:q * P + p],
                                        weight, start=True, stop=True)
            return last

        def cols(t, k, p, j):
            return t[0:k, 0:j * P].rearrange("k (j p) -> k j p", p=P)[:, :, 0:p]

        def row_stats(link, v, stats, mv, p, j):
            for q in range(j):
                last = nc.vector.bn_stats(stats[0:p, q * 6:q * 6 + 6], v[0:p, q * D:(q + 1) * D])
            last.then_inc(link.sem, 1)
            nc.vector.wait_ge(link.sem, link.count())
            nc.vector.nop(nofuse=True)
            for q in range(j):
                last = nc.vector.bn_aggr(mv[0:p, q * 2:q * 2 + 2], stats[0:p, q * 6:q * 6 + 6])
            return last

        def scale_rows(v_out, v_in, rstd, nmr, p, j):
            for q in range(j):
                last = nc.scalar.activation(v_out[0:p, q * D:(q + 1) * D], v_in[0:p, q * D:(q + 1) * D], ACT.Identity,
                                            bias=nmr[0:p, q:q + 1], scale=rstd[0:p, q:q + 1])
            return last

        class Norm:

            def __init__(self, sb, name):
                self.stats = [sb(f"{name}_stats{s}", [P, J * 6]) for s in range(2)]
                self.mv = [sb(f"{name}_mv{s}", [P, J * 2]) for s in range(2)]
                self.sd = [sb(f"{name}_sd{s}", [P, J]) for s in range(2)]
                self.rstd = [sb(f"{name}_rstd{s}", [P, J]) for s in range(2)]
                self.nmr = [sb(f"{name}_nmr{s}", [P, J]) for s in range(2)]

            def variance(self, link, v, b, ready):
                p, j = pj(b)
                row_stats(link, v, self.stats[b.s], self.mv[b.s], p, j).then_inc(ready, 1)

            def root(self, b, ready):
                p, j = pj(b)
                nc.scalar.activation(self.sd[b.s][0:p, 0:j], self.mv[b.s][0:p, 1:2 * j:2], ACT.Sqrt,
                                     bias=eps[0:p, :]).then_inc(ready, 1)

            def factors(self, link, b, ready):
                p, j = pj(b)
                nc.vector.reciprocal(self.rstd[b.s][0:p, 0:j], self.sd[b.s][0:p, 0:j]).then_inc(link.sem, 1)
                nc.vector.wait_ge(link.sem, link.count())
                nc.vector.nop(nofuse=True)
                nc.vector.scalar_tensor_tensor(out=self.nmr[b.s][0:p, 0:j], in0=self.mv[b.s][0:p, 0:2 * j:2],
                                               scalar=-1.0, in1=self.rstd[b.s][0:p, 0:j], op0=ALU.mult,
                                               op1=ALU.mult).then_inc(ready, 1)

        def degree_pass():
            with ExitStack() as ctx:
                def sb(name, shape, dt=F32):
                    return ctx.enter_context(nc.sbuf_tensor("deg_" + name, shape, dt))

                aux_s = [sb(f"aux{s}", [P, J * AUXW]) for s in range(2)]
                x_s = [sb(f"x{s}", [P, J * D]) for s in range(2)]
                o_s = [sb(f"o{s}", [P, J * D]) for s in range(2)]
                deg = [sb(f"deg{s}", [P, J]) for s in range(2)]
                root = [sb(f"root{s}", [P, J]) for s in range(2)]
                inv = [sb(f"inv{s}", [P, J]) for s in range(2)]
                with nc.Block() as block:
                    @block.sync
                    def _(sp):
                        def load_aux(b):
                            p, j = pj(b)
                            if b.after(2):
                                sp.wait_ge(normed, b.n - 1)
                                sp.nop(nofuse=True)
                            sp.dma_start(aux_s[b.s][0:p, 0:j * AUXW], rows(aux, b)).then_inc(loaded[b.s], DMA)

                        def load_x(b):
                            p, j = pj(b)
                            if b.after(2):
                                sp.wait_ge(summed, b.n - 1)
                                sp.nop(nofuse=True)
                            sp.dma_start(x_s[b.s][0:p, 0:j * D], rows(a["x"], b)).then_inc(loaded_b[b.s], DMA)

                        def store(b):
                            p, j = pj(b)
                            sp.wait_ge(summed, b.n + 1)
                            sp.nop(nofuse=True)
                            sp.dma_start(rows(wide[0], b), o_s[b.s][0:p, 0:j * D]).then_inc(stored[b.s], DMA)
                            sp.dma_start(rows(dinv, b), inv[b.s][0:p, 0:j]).then_inc(stored[b.s], DMA)

                        pipeline(sp, NB, [(store, 3), (load_x, 1), (load_aux, 0)])
                        for s in range(2):
                            sp.wait_ge(stored[s], blocks_in(NB, s) * 2 * DMA)

                    @block.vector
                    def _(dve):
                        link = Steps(vec_step, 1)

                        def degree(b):
                            p, j = pj(b)
                            dve.wait_ge(loaded[b.s], (b.pair + 1) * DMA)
                            dve.nop(nofuse=True)
                            if b.after(2):
                                dve.wait_ge(rooted, b.n - 1)
                                dve.nop(nofuse=True)
                            nc.vector.tensor_scalar(deg[b.s][0:p, 0:j], aux_s[b.s][0:p, 16:j * AUXW:AUXW], 1.0, None,
                                                    ALU.add).then_inc(normed, 1)

                        def scale(b):
                            p, j = pj(b)
                            link.at(b)
                            dve.wait_ge(rooted, b.n + 1)
                            dve.nop(nofuse=True)
                            dve.wait_ge(loaded_b[b.s], (b.pair + 1) * DMA)
                            dve.nop(nofuse=True)
                            if b.after(2):
                                dve.wait_ge(stored[b.s], b.pair * 2 * DMA)
                                dve.nop(nofuse=True)
                            nc.vector.reciprocal(inv[b.s][0:p, 0:j], root[b.s][0:p, 0:j]).then_inc(link.sem, 1)
                            dve.wait_ge(link.sem, link.count())
                            dve.nop(nofuse=True)
                            nc.vector.tensor_tensor(split(o_s[b.s], p, j), split(x_s[b.s], p, j),
                                                    per_row(inv[b.s], p, j, D), ALU.mult).then_inc(summed, 1)

                        pipeline(dve, NB, [(degree, 1), (scale, 2)])

                    @block.scalar
                    def _(act):
                        def take_root(b):
                            p, j = pj(b)
                            act.wait_ge(normed, b.n + 1)
                            act.nop(nofuse=True)
                            if b.after(2):
                                act.wait_ge(summed, b.n - 1)
                                act.nop(nofuse=True)
                            nc.scalar.activation(root[b.s][0:p, 0:j], deg[b.s][0:p, 0:j], ACT.Sqrt).then_inc(rooted, 1)

                        pipeline(act, NB, [(take_root, 1)])
            end_pass()

        def aggregate_then_weight_pass(tag, own, sum_table, weight, bias, k, m, to, to_width, residual=None, last_w=None,
                                       last_bias=None):
            J, NB, pj, rows = node_blocks(LONG if residual is None else 8)
            with ExitStack() as ctx:
                def sb(name, shape, dt=F32):
                    return ctx.enter_context(nc.sbuf_tensor(f"{tag}_{name}", shape, dt))

                def ps(name, shape):
                    return ctx.enter_context(nc.psum_tensor(f"{tag}_{name}", shape, F32))

                own_s = [sb(f"own{s}", [P, J * k]) for s in range(2)]
                sum_s = [sb(f"sum{s}", [P, J * k]) for s in range(2)]
                inv = [sb(f"inv{s}", [P, J]) for s in range(2)]
                u_t = [sb(f"u_t{s}", [k, J * P]) for s in range(2)]
                z_s = [sb(f"z{s}", [P, J * m]) for s in range(2)]
                o_s = [sb(f"o{s}", [P, J * to_width]) for s in range(2)]
                normal, deep = residual is not None, last_w is not None
                if normal:
                    res_s = [sb(f"res{s}", [P, J * D]) for s in range(2)]
                    norm = Norm(sb, "norm")
                if deep:
                    h_t = [sb(f"h_t{s}", [P, J * P]) for s in range(2)]
                    y_s = [sb(f"y{s}", [P, J * D]) for s in range(2)]
                    p_h = ps("p_h", [P, J * P])
                    p_y = ps("p_y", [P, J * D])
                p_u = ps("p_u", [P, J * P])
                p_z = ps("p_z", [P, J * m])
                sum_rows, sum_ready = (y_s, multiplied_b) if deep else (z_s, normed)
                row_bias = last_bias if deep else bias
                rows_lag = 2 if deep else 3

                with nc.Block() as block:
                    @block.sync
                    def _(sp):
                        def load(b):
                            p, j = pj(b)
                            if b.after(2):
                                sp.wait_ge(summed, b.n - 1)
                                sp.nop(nofuse=True)
                            sp.dma_start(own_s[b.s][0:p, 0:j * k], rows(own, b)).then_inc(loaded[b.s], DMA)
                            sp.dma_start(sum_s[b.s][0:p, 0:j * k], rows(sum_table, b)).then_inc(loaded[b.s], DMA)

                        def load_inv(b):
                            p, j = pj(b)
                            if b.after(2):
                                sp.wait_ge(normed if normal else finished, b.n - 1)
                                sp.nop(nofuse=True)
                            sp.dma_start(inv[b.s][0:p, 0:j], rows(dinv, b)).then_inc(loaded_b[b.s], DMA)

                        def load_residual(b):
                            p, j = pj(b)
                            if b.after(2):
                                sp.wait_ge(summed_b if deep else normed, b.n - 1)
                                sp.nop(nofuse=True)
                            sp.dma_start(res_s[b.s][0:p, 0:j * D], rows(residual, b)).then_inc(loaded_c[b.s], DMA)

                        def store(b):
                            p, j = pj(b)
                            sp.wait_ge(finished, b.n + 1)
                            sp.nop(nofuse=True)
                            sp.dma_start(rows(to, b), o_s[b.s][0:p, 0:j * to_width]).then_inc(stored[b.s], DMA)

                        stages = [(load_inv, rows_lag - 1), (load, 0)]
                        if normal:
                            stages = [(store, 5), (load_residual, 2), *stages]
                        else:
                            stages = [(store, 4), *stages]
                        pipeline(sp, NB, stages)
                        for s in range(2):
                            sp.wait_ge(stored[s], blocks_in(NB, s) * DMA)

                    @block.gpsimd
                    def _(pool):
                        def add(b):
                            p, j = pj(b)
                            pool.wait_ge(loaded[b.s], (b.pair + 1) * 2 * DMA)
                            pool.nop(nofuse=True)
                            nc.gpsimd.tensor_tensor(own_s[b.s][0:p, 0:j * k], own_s[b.s][0:p, 0:j * k],
                                                    sum_s[b.s][0:p, 0:j * k], ALU.add).then_inc(pooled, 1)

                        def bias_residual(b):
                            p, j = pj(b)
                            pool.wait_ge(loaded_c[b.s], (b.pair + 1) * DMA)
                            pool.nop(nofuse=True)
                            nc.gpsimd.tensor_tensor(split(res_s[b.s], p, j), split(res_s[b.s], p, j),
                                                    row_bias[0:p, :].unsqueeze(1).to_broadcast([p, j, D]), ALU.add
                                                    ).then_inc(pooled_b, 1)

                        pipeline(pool, NB, [(bias_residual, 3), (add, 1)] if normal else [(add, 1)])

                    @block.vector
                    def _(dve):
                        link, link_f = Steps(vec_step, 1), Steps(factor_step[0], 1)

                        def scaled_rows(b):
                            p, j = pj(b)
                            dve.wait_ge(multiplied, b.n + 1)
                            dve.nop(nofuse=True)
                            dve.wait_ge(loaded_b[b.s], (b.pair + 1) * DMA)
                            dve.nop(nofuse=True)
                            if b.after(2):
                                dve.wait_ge(turned_b if deep else finished, b.n - 1)
                                dve.nop(nofuse=True)
                            if normal and not deep:
                                dve.wait_ge(pooled_b, b.n + 1)
                                dve.nop(nofuse=True)
                            for q in range(j):
                                more = res_s[b.s][0:p, q * D:(q + 1) * D] if normal and not deep else bias[0:p, :]
                                last = nc.vector.scalar_tensor_tensor(
                                    out=z_s[b.s][0:p, q * m:(q + 1) * m], in0=p_z[0:p, q * m:(q + 1) * m],
                                    scalar=inv[b.s][0:p, q:q + 1], in1=more, op0=ALU.mult, op1=ALU.add)
                            last.then_inc(normed, 1)

                        def last_rows(b):
                            p, j = pj(b)
                            dve.wait_ge(multiplied_b, b.n + 1)
                            dve.nop(nofuse=True)
                            dve.wait_ge(pooled_b, b.n + 1)
                            dve.nop(nofuse=True)
                            if b.after(2):
                                dve.wait_ge(finished, b.n - 1)
                                dve.nop(nofuse=True)
                            nc.vector.tensor_tensor(y_s[b.s][0:p, 0:j * D], p_y[0:p, 0:j * D], res_s[b.s][0:p, 0:j * D],
                                                    ALU.add).then_inc(summed_b, 1)

                        def variance(b):
                            link.at(b)
                            dve.wait_ge(summed_b if deep else normed, b.n + 1)
                            dve.nop(nofuse=True)
                            norm.variance(link, sum_rows[b.s], b, rooted)

                        def factors(b):
                            link_f.at(b)
                            dve.wait_ge(rooted_b, b.n + 1)
                            dve.nop(nofuse=True)
                            norm.factors(link_f, b, normed_b)

                        if not normal:
                            stages = [(scaled_rows, 3)]
                        elif not deep:
                            stages = [(scaled_rows, 3), (factors, 4), (variance, 3)]
                        else:
                            stages = [(scaled_rows, 2), (factors, 4), (last_rows, 3), (variance, 3)]
                        pipeline(dve, NB, stages)

                    @block.tensor
                    def _(pe):
                        def turn(b):
                            p, j = pj(b)
                            pe.wait_ge(pooled, b.n + 1)
                            pe.nop(nofuse=True)
                            if b.after(1):
                                pe.wait_ge(evacuated, b.n)
                                pe.nop(nofuse=True)
                            turn_rows(p_u, own_s[b.s], p, j, k).then_inc(summed, 1)

                        def multiply(b):
                            p, j = pj(b)
                            pe.wait_ge(evacuated, b.n + 1)
                            pe.nop(nofuse=True)
                            if b.after(1):
                                pe.wait_ge(normed, b.n)
                                pe.nop(nofuse=True)
                            times_weight(p_z, u_t[b.s], weight[:, :], p, j, k, m).then_inc(multiplied, 1)

                        def turn_h(b):
                            p, j = pj(b)
                            pe.wait_ge(normed, b.n + 1)
                            pe.nop(nofuse=True)
                            if b.after(1):
                                pe.wait_ge(evacuated_b, b.n)
                                pe.nop(nofuse=True)
                            turn_rows(p_h, z_s[b.s], p, j, D).then_inc(turned_b, 1)

                        def multiply_h(b):
                            p, j = pj(b)
                            pe.wait_ge(evacuated_b, b.n + 1)
                            pe.nop(nofuse=True)
                            if b.after(1):
                                pe.wait_ge(summed_b, b.n)
                                pe.nop(nofuse=True)
                            times_weight(p_y, h_t[b.s], last_w[:, :], p, j, D, D).then_inc(multiplied_b, 1)

                        if deep:
                            stages = [(multiply_h, 3), (turn, 1), (turn_h, 2), (multiply, 1)]
                        else:
                            stages = [(turn, 1), (multiply, 2)]
                        pipeline(pe, NB, stages)

                    @block.scalar
                    def _(act):
                        def evacuate(b):
                            p, j = pj(b)
                            act.wait_ge(summed, b.n + 1)
                            act.nop(nofuse=True)
                            if b.after(2):
                                act.wait_ge(multiplied, b.n - 1)
                                act.nop(nofuse=True)
                            nc.scalar.copy(cols(u_t[b.s], k, p, j), cols(p_u, k, p, j)).then_inc(evacuated, 1)

                        def relu_scale(b):
                            p, j = pj(b)
                            act.wait_ge(normed, b.n + 1)
                            act.nop(nofuse=True)
                            if b.after(2):
                                act.wait_ge(stored[b.s], b.pair * DMA)
                                act.nop(nofuse=True)
                            for q in range(j):
                                last = nc.scalar.activation(o_s[b.s][0:p, q * m:(q + 1) * m],
                                                            z_s[b.s][0:p, q * m:(q + 1) * m], ACT.Relu,
                                                            scale=inv[b.s][0:p, q:q + 1])
                            last.then_inc(finished, 1)

                        def relu_turned(b):
                            p, j = pj(b)
                            act.wait_ge(turned_b, b.n + 1)
                            act.nop(nofuse=True)
                            if b.after(2):
                                act.wait_ge(multiplied_b, b.n - 1)
                                act.nop(nofuse=True)
                            nc.scalar.activation(cols(h_t[b.s], D, p, j), cols(p_h, D, p, j), ACT.Relu
                                                 ).then_inc(evacuated_b, 1)

                        def root(b):
                            act.wait_ge(rooted, b.n + 1)
                            act.nop(nofuse=True)
                            if b.after(2):
                                act.wait_ge(normed_b, b.n - 1)
                                act.nop(nofuse=True)
                            norm.root(b, rooted_b)

                        def normalise(b):
                            p, j = pj(b)
                            act.wait_ge(normed_b, b.n + 1)
                            act.nop(nofuse=True)
                            if b.after(2):
                                act.wait_ge(stored[b.s], b.pair * DMA)
                                act.nop(nofuse=True)
                            scale_rows(o_s[b.s], sum_rows[b.s], norm.rstd[b.s], norm.nmr[b.s], p, j).then_inc(finished, 1)

                        if not normal:
                            stages = [(evacuate, 1), (relu_scale, 3)]
                        elif not deep:
                            stages = [(root, 4), (evacuate, 1), (normalise, 4)]
                        else:
                            stages = [(root, 4), (evacuate, 1), (normalise, 4), (relu_turned, 2)]
                        pipeline(act, NB, stages)
            end_pass()

        def aggregate_last_pass(tag, own, sum_table, bias, k, weight, m, to):
            J, NB, pj, rows = node_blocks(LONG)
            with ExitStack() as ctx:
                def sb(name, shape, dt=F32):
                    return ctx.enter_context(nc.sbuf_tensor(f"{tag}_{name}", shape, dt))

                def ps(name, shape):
                    return ctx.enter_context(nc.psum_tensor(f"{tag}_{name}", shape, F32))

                own_s = [sb(f"own{s}", [P, J * k]) for s in range(2)]
                sum_s = [sb(f"sum{s}", [P, J * k]) for s in range(2)]
                inv = [sb(f"inv{s}", [P, J]) for s in range(2)]
                inv_last = [sb(f"inv_last{s}", [P, J]) for s in range(2)]
                h_s = [sb(f"h{s}", [P, J * k]) for s in range(2)]
                h_t = [sb(f"h_t{s}", [k, J * P]) for s in range(2)]
                o_s = [sb(f"o{s}", [P, J * m]) for s in range(2)]
                p_h = ps("p_h", [P, J * P])
                p_z = ps("p_z", [P, J * m])
                plain = weight is None
                scale_lag = 2 if plain else 3

                with nc.Block() as block:
                    @block.sync
                    def _(sp):
                        def load(b):
                            p, j = pj(b)
                            if b.after(2):
                                sp.wait_ge(summed, b.n - 1)
                                sp.nop(nofuse=True)
                            sp.dma_start(own_s[b.s][0:p, 0:j * k], rows(own, b)).then_inc(loaded[b.s], DMA)
                            sp.dma_start(sum_s[b.s][0:p, 0:j * k], rows(sum_table, b)).then_inc(loaded[b.s], DMA)
                            sp.dma_start(inv[b.s][0:p, 0:j], rows(dinv, b)).then_inc(loaded[b.s], DMA)

                        def load_inv(b):
                            p, j = pj(b)
                            if b.after(2):
                                sp.wait_ge(finished, b.n - 1)
                                sp.nop(nofuse=True)
                            sp.dma_start(inv_last[b.s][0:p, 0:j], rows(dinv, b)).then_inc(loaded_b[b.s], DMA)

                        def store(b):
                            p, j = pj(b)
                            sp.wait_ge(finished, b.n + 1)
                            sp.nop(nofuse=True)
                            sp.dma_start(rows(to, b), o_s[b.s][0:p, 0:j * m]).then_inc(stored[b.s], DMA)

                        pipeline(sp, NB, [(store, scale_lag + 1), (load_inv, scale_lag - 1), (load, 0)])
                        for s in range(2):
                            sp.wait_ge(stored[s], blocks_in(NB, s) * DMA)

                    @block.gpsimd
                    def _(pool):
                        def add(b):
                            p, j = pj(b)
                            pool.wait_ge(loaded[b.s], (b.pair + 1) * 3 * DMA)
                            pool.nop(nofuse=True)
                            nc.gpsimd.tensor_tensor(own_s[b.s][0:p, 0:j * k], own_s[b.s][0:p, 0:j * k],
                                                    sum_s[b.s][0:p, 0:j * k], ALU.add).then_inc(pooled, 1)

                        pipeline(pool, NB, [(add, 1)])

                    @block.vector
                    def _(dve):
                        def scaled_rows(b):
                            p, j = pj(b)
                            dve.wait_ge(pooled, b.n + 1)
                            dve.nop(nofuse=True)
                            if b.after(2):
                                dve.wait_ge(finished if plain else turned, b.n - 1)
                                dve.nop(nofuse=True)
                            for q in range(j):
                                last = nc.vector.scalar_tensor_tensor(
                                    out=h_s[b.s][0:p, q * k:(q + 1) * k], in0=own_s[b.s][0:p, q * k:(q + 1) * k],
                                    scalar=inv[b.s][0:p, q:q + 1], in1=bias[0:p, :], op0=ALU.mult, op1=ALU.add)
                            last.then_inc(summed, 1)

                        def scale(b):
                            p, j = pj(b)
                            dve.wait_ge(loaded_b[b.s], (b.pair + 1) * DMA)
                            dve.nop(nofuse=True)
                            if b.after(2):
                                dve.wait_ge(stored[b.s], b.pair * DMA)
                                dve.nop(nofuse=True)
                            if plain:
                                dve.wait_ge(summed, b.n + 1)
                                dve.nop(nofuse=True)
                                nc.vector.scalar_tensor_tensor(
                                    out=split(o_s[b.s], p, j, k), in0=split(h_s[b.s], p, j, k), scalar=0.0,
                                    in1=per_row(inv_last[b.s], p, j, k), op0=ALU.max, op1=ALU.mult).then_inc(finished, 1)
                            else:
                                dve.wait_ge(multiplied, b.n + 1)
                                dve.nop(nofuse=True)
                                nc.vector.tensor_tensor(split(o_s[b.s], p, j, m), split(p_z, p, j, m),
                                                        per_row(inv_last[b.s], p, j, m), ALU.mult).then_inc(finished, 1)

                        pipeline(dve, NB, [(scaled_rows, 1), (scale, scale_lag)])

                    if not plain:
                        @block.scalar
                        def _(act):
                            def relu_turned(b):
                                p, j = pj(b)
                                act.wait_ge(turned, b.n + 1)
                                act.nop(nofuse=True)
                                if b.after(2):
                                    act.wait_ge(multiplied, b.n - 1)
                                    act.nop(nofuse=True)
                                nc.scalar.activation(cols(h_t[b.s], k, p, j), cols(p_h, k, p, j), ACT.Relu
                                                     ).then_inc(evacuated, 1)

                            pipeline(act, NB, [(relu_turned, 1)])

                        @block.tensor
                        def _(pe):
                            def turn(b):
                                p, j = pj(b)
                                pe.wait_ge(summed, b.n + 1)
                                pe.nop(nofuse=True)
                                if b.after(1):
                                    pe.wait_ge(evacuated, b.n)
                                    pe.nop(nofuse=True)
                                turn_rows(p_h, h_s[b.s], p, j, k).then_inc(turned, 1)

                            def multiply(b):
                                p, j = pj(b)
                                pe.wait_ge(evacuated, b.n + 1)
                                pe.nop(nofuse=True)
                                if b.after(1):
                                    pe.wait_ge(finished, b.n)
                                    pe.nop(nofuse=True)
                                times_weight(p_z, h_t[b.s], weight[:, :], p, j, k, m).then_inc(multiplied, 1)

                            pipeline(pe, NB, [(turn, 1), (multiply, 2)])
            end_pass()


        edge_sum_pass("count", AUXW, None, aux, from_attr=True, zero=[sums[D]])
        degree_pass()
        edge_sum_pass("g1", D, wide[0], sums[D], zero=[sums[GATW]])
        aggregate_then_weight_pass("n1", wide[0], sums[D], w["L0_gnn_W1"], brow["L0_gnn_b1"], D, D, wide[1], D)
        edge_sum_pass("g2", D, wide[1], sums[D], zero=[sums[64], sums[32], sums[16]])
        aggregate_then_weight_pass("n2", wide[1], sums[D], w["L0_gnn_W2"], brow["L0_gnn_b2"], D, D, x1, D,
                                   residual=a["x"])

        def gated_edge_pass():
            with ExitStack() as ctx:
                def sb(name, shape, dt=F32):
                    return ctx.enter_context(nc.sbuf_tensor(f"cg_{name}", shape, dt))

                def ps(name, shape):
                    return ctx.enter_context(nc.psum_tensor(f"cg_{name}", shape, F32))

                two = range(2)
                src_s = [sb(f"src{s}", [P, CH], U32) for s in two]
                dst_s = [sb(f"dst{s}", [P, CH], U32) for s in two]
                end_s = [sb(f"end{s}", [P, CH], U32) for s in two]
                got_s = [sb(f"got_src{s}", [P, CH, D]) for s in two]
                got_d = [sb(f"got_dst{s}", [P, CH, D]) for s in two]
                attr = [sb(f"attr{s}", [P, CH, 17]) for s in two]
                t_d = [sb(f"t_d{s}", [D, EDGE_BLOCK]) for s in two]
                t_s = [sb(f"t_s{s}", [D, EDGE_BLOCK]) for s in two]
                t_a = [sb(f"t_a{s}", [17, EDGE_BLOCK]) for s in two]
                low = sb("low", [D, EDGE_BLOCK])
                size = sb("size", [D, EDGE_BLOCK])
                e_f = sb("e_f", [D, EDGE_BLOCK])
                soft = sb("soft", [D, EDGE_BLOCK])
                msg = sb("msg", [D, EDGE_BLOCK])
                ends = sb("ends", [D, EDGE_BLOCK])
                run = [sb(f"run{s}", [D, EDGE_BLOCK]) for s in two]
                res = [sb(f"res{s}", [P, CH * D]) for s in two]
                gamma = sb("gamma", [D, 1])
                beta = sb("beta", [D, 1])
                p_d, p_s, p_a, p_f, p_g = (ps(n, [P, EDGE_BLOCK]) for n in ("p_d", "p_s", "p_a", "p_f", "p_g"))
                p_out = [ps(f"p_out{s}", [P, CH * D]) for s in two]

                with nc.Block() as block:
                    @block.sync
                    def _(sp):
                        def load(b):
                            if b.after(2):
                                sp.wait_ge(gathered[b.s], past(gathered[b.s]) + b.pair * CH * DMA)
                                sp.nop(nofuse=True)
                            if b.after(2):
                                sp.wait_ge(gathered_dst[b.s], past(gathered_dst[b.s]) + b.pair * CH * DMA)
                                sp.nop(nofuse=True)
                            sp.dma_start(src_s[b.s][:, :], src_i[bass.ds(b.n * P, P), :]).then_inc(src_loaded[b.s], DMA)
                            sp.dma_start(dst_s[b.s][:, :], dst_i[bass.ds(b.n * P, P), :]).then_inc(dst_loaded[b.s], DMA)

                        def load_attr(b):
                            sp.wait_ge(prepared, 2)
                            if b.after(2):
                                sp.wait_ge(turned, b.n - 1)
                                sp.nop(nofuse=True)
                            p = edge_tail_p if b.tail else P
                            sp.dma_start(attr[b.s][0:p, :, 0:16], a["edge_attr_16"][bass.ds(b.n * EDGE_BLOCK, p * CH), :]
                                         .rearrange("(p c) f -> p c f", p=p)).then_inc(attr_loaded[b.s], DMA)

                        def load_end(b):
                            if b.after(2):
                                sp.wait_ge(scattered[b.s], past(scattered[b.s]) + b.pair * CH * DMA)
                                sp.nop(nofuse=True)
                            sp.dma_start(end_s[b.s][:, :], end_i[bass.ds(b.n * P, P), :]).then_inc(end_loaded[b.s], DMA)

                        for t, name in ((gamma, "L1_gnn_bn_gamma"), (beta, "L1_gnn_bn_beta")):
                            sp.dma_start(t[:, :], a[name].rearrange("(d o) -> d o", o=1)).then_inc(setup_loaded, DMA)
                        pipeline(sp, EB, [(load_attr, 1), (load, 0), (load_end, 4)])

                    @block.gpsimd
                    def _(pool):
                        def gather(b):
                            pool.wait_ge(src_loaded[b.s], (b.pair + 1) * DMA)
                            pool.nop(nofuse=True)
                            pool.wait_ge(dst_loaded[b.s], (b.pair + 1) * DMA)
                            pool.nop(nofuse=True)
                            if b.after(2):
                                pool.wait_ge(turned, b.n - 1)
                                pool.nop(nofuse=True)
                            for got, idx, done in ((got_s, src_s, gathered), (got_d, dst_s, gathered_dst)):
                                for j in range(CH):
                                    pool.indirect_dma_start(
                                        got[b.s][:, j, :], None, x1,
                                        bass.IndirectOffsetOnAxis(ap=idx[b.s][:, j:j + 1], axis=0)
                                    ).then_inc(done[b.s], DMA)

                        def scatter(b):
                            pool.wait_ge(end_loaded[b.s], (b.pair + 1) * DMA)
                            pool.nop(nofuse=True)
                            pool.wait_ge(rows_ready, b.n + 1)
                            pool.nop(nofuse=True)
                            for j in range(CH):
                                pool.indirect_dma_start(
                                    sums[D], bass.IndirectOffsetOnAxis(ap=end_s[b.s][:, j:j + 1], axis=0),
                                    res[b.s][:, j * D:(j + 1) * D], None, bounds_check=N - 1, oob_is_err=False
                                ).then_inc(scattered[b.s], DMA)

                        pipeline(pool, EB, [(gather, 1), (scatter, 5)])
                        for s in two:
                            pool.wait_ge(scattered[s], past(scattered[s]) + blocks_in(EB, s) * CH * DMA)

                    @block.tensor
                    def _(pe):
                        def turn(b):
                            pe.wait_ge(gathered[b.s], past(gathered[b.s]) + (b.pair + 1) * CH * DMA)
                            pe.nop(nofuse=True)
                            pe.wait_ge(gathered_dst[b.s], past(gathered_dst[b.s]) + (b.pair + 1) * CH * DMA)
                            pe.nop(nofuse=True)
                            pe.wait_ge(attr_loaded[b.s], (b.pair + 1) * DMA)
                            pe.nop(nofuse=True)
                            if b.after(1):
                                pe.wait_ge(evacuated, b.n)
                                pe.nop(nofuse=True)
                            for bank, got, width in ((p_d, got_d, D), (p_s, got_s, D), (p_a, attr, 17)):
                                for j in range(CH):
                                    last = nc.tensor.transpose(bank[0:width, j:EDGE_BLOCK:CH], got[b.s][:, j, :],
                                                               ident[:, :])
                            last.then_inc(turned, 1)

                        def gates(b):
                            pe.wait_ge(evacuated, b.n + 1)
                            pe.nop(nofuse=True)
                            if b.after(1):
                                pe.wait_ge(gates_in, b.n)
                                pe.nop(nofuse=True)
                            for i, t in enumerate((t_d, t_s, t_a)):
                                last = nc.tensor.matmul(p_f[:, :], gate_w["f"][i][:, :], t[b.s][:, :],
                                                        start=(i == 0), stop=(i == 2))
                            last.then_inc(multiplied_b, 1)
                            if b.after(1):
                                pe.wait_ge(g_used, b.n)
                                pe.nop(nofuse=True)
                            for i, t in enumerate((t_d, t_s, t_a)):
                                last = nc.tensor.matmul(p_g[:, :], gate_w["s"][i][:, :], t[b.s][:, :],
                                                        start=(i == 0), stop=(i == 2))
                            last.then_inc(multiplied, 1)

                        def turn_back(b):
                            pe.wait_ge(scanned, b.n + 1)
                            pe.nop(nofuse=True)
                            if b.after(2):
                                pe.wait_ge(rows_ready, b.n - 1)
                                pe.nop(nofuse=True)
                            for j in range(CH):
                                last = nc.tensor.transpose(p_out[b.s][:, j * D:(j + 1) * D],
                                                           run[b.s][:, j:EDGE_BLOCK:CH], ident[:, :])
                            last.then_inc(turned_back, 1)

                        pipeline(pe, EB, [(turn_back, 4), (turn, 2), (gates, 2)])

                    @block.vector
                    def _(dve):
                        link = Steps(vec_step, 6)

                        def clamp(b):
                            dve.wait_ge(multiplied_b, b.n + 1)
                            dve.nop(nofuse=True)
                            if b.after(1):
                                dve.wait_ge(gates_out, b.n)
                                dve.nop(nofuse=True)
                            nc.vector.tensor_scalar(low[:, :], p_f[:, :], -87.0, None, ALU.max).then_inc(gates_in, 1)

                        def combine(b):
                            link.at(b)
                            dve.wait_ge(gates_out, b.n + 1)
                            dve.nop(nofuse=True)
                            if b.after(2):
                                dve.wait_ge(turned_back, b.n - 1)
                                dve.nop(nofuse=True)
                            if b.after(1):
                                dve.wait_ge(scanned, b.n)
                                dve.nop(nofuse=True)
                            nc.vector.tensor_scalar(e_f[:, :], e_f[:, :], 1.0, None, ALU.add).then_inc(link.sem, 1)
                            dve.wait_ge(link.sem, link.count())
                            dve.nop(nofuse=True)
                            nc.vector.reciprocal(e_f[:, :], e_f[:, :]).then_inc(link.sem, 1)
                            dve.wait_ge(link.sem, link.count())
                            dve.nop(nofuse=True)
                            dve.wait_ge(soft_ready, b.n + 1)
                            dve.nop(nofuse=True)
                            nc.vector.scalar_tensor_tensor(out=msg[:, :], in0=p_g[:, :], scalar=0.0, in1=soft[:, :],
                                                           op0=ALU.max, op1=ALU.add).then_inc(g_used, 1)
                            dve.wait_ge(g_used, b.n + 1)
                            dve.nop(nofuse=True)
                            nc.vector.tensor_tensor(msg[:, :], msg[:, :], e_f[:, :], ALU.mult).then_inc(link.sem, 1)
                            dve.wait_ge(link.sem, link.count())
                            dve.nop(nofuse=True)
                            first = isinstance(b.n, int) and b.n == 0
                            nc.vector.tensor_tensor_scan(
                                run[b.s][:, :], cont[:, bass.ds(b.n * EDGE_BLOCK, EDGE_BLOCK)], msg[:, :],
                                0.0 if first else run[1 - b.s][:, EDGE_BLOCK - 1:EDGE_BLOCK],
                                ALU.mult, ALU.add).then_inc(scanned, 1)
                            dve.wait_ge(scanned, b.n + 1)
                            dve.nop(nofuse=True)
                            edges = EDGE_BLOCK
                            if b.tail:
                                edges = edge_left
                                nc.vector.memset(ends[:, :], 0.0).then_inc(link.sem, 1)
                                dve.wait_ge(link.sem, link.count())
                                dve.nop(nofuse=True)
                            nc.vector.scalar_tensor_tensor(
                                out=ends[:, 0:edges], in0=cont[:, bass.ds(b.n * EDGE_BLOCK + 1, edges)], scalar=0.0,
                                in1=run[b.s][:, 0:edges], op0=ALU.is_equal, op1=ALU.mult).then_inc(link.sem, 1)
                            dve.wait_ge(link.sem, link.count())
                            dve.nop(nofuse=True)
                            ins = nc.vector.bn_stats(bn_part[:, bass.ds(b.n * 6, 6)], ends[:, :])
                            if not b.tail:
                                ins.then_inc(vec_step, 2)
                                link.k = link.per
                                dve.wait_ge(vec_step, link.base + link.per)
                            else:
                                ins.then_inc(link.sem, 1)
                                dve.wait_ge(link.sem, link.count())
                                dve.nop(nofuse=True)

                        pipeline(dve, EB, [(clamp, 3), (combine, 3)])

                        mv = [sb(f"mv{i}", [D, 1]) for i in range(6)]
                        stat = sb("stat", [D, 2])
                        mean, square, var, sd, scale, shift = mv
                        wide_c = sb("wide_c", [D, 2 * D])
                        ratio = float(EP) / float(N)
                        then = Steps(vec_step, 99)
                        then.base = EB * 6

                        dve.wait_ge(setup_loaded, 2 * DMA)
                        nc.vector.bn_aggr(stat[:, :], bn_part[:, :]).then_inc(then.sem, 1)
                        dve.wait_ge(then.sem, then.count())
                        nc.vector.tensor_scalar(mean[:, :], stat[:, 0:1], ratio, None, ALU.mult).then_inc(then.sem, 1)
                        dve.wait_ge(then.sem, then.count())
                        nc.vector.scalar_tensor_tensor(out=square[:, :], in0=stat[:, 0:1], scalar=stat[:, 0:1],
                                                       in1=stat[:, 1:2], op0=ALU.mult, op1=ALU.add).then_inc(then.sem, 1)
                        dve.wait_ge(then.sem, then.count())
                        nc.vector.tensor_scalar(square[:, :], square[:, :], ratio, EPS, ALU.mult, ALU.add).then_inc(then.sem, 1)
                        dve.wait_ge(then.sem, then.count())
                        nc.vector.tensor_tensor(var[:, :], mean[:, :], mean[:, :], ALU.mult).then_inc(then.sem, 1)
                        dve.wait_ge(then.sem, then.count())
                        nc.vector.tensor_tensor(var[:, :], square[:, :], var[:, :], ALU.subtract).then_inc(then.sem, 1)
                        dve.wait_ge(then.sem, then.count())
                        dve.sem_inc(prepared, 1)
                        dve.wait_ge(prepared, 4)
                        nc.vector.reciprocal(scale[:, :], sd[:, :]).then_inc(then.sem, 1)
                        dve.wait_ge(then.sem, then.count())
                        nc.vector.tensor_tensor(scale[:, :], scale[:, :], gamma[:, :], ALU.mult).then_inc(then.sem, 1)
                        dve.wait_ge(then.sem, then.count())
                        nc.vector.tensor_tensor(shift[:, :], mean[:, :], scale[:, :], ALU.mult).then_inc(then.sem, 1)
                        dve.wait_ge(then.sem, then.count())
                        nc.vector.tensor_tensor(shift[:, :], beta[:, :], shift[:, :], ALU.subtract).then_inc(then.sem, 1)
                        dve.wait_ge(then.sem, then.count())
                        nc.vector.tensor_copy(wide_c[:, 0:D], scale[:, 0:1].to_broadcast([D, D])).then_inc(then.sem, 1)
                        dve.wait_ge(then.sem, then.count())
                        nc.vector.tensor_copy(wide_c[:, D:2 * D], shift[:, 0:1].to_broadcast([D, D])).then_inc(finished, 1)
                        bn_tiles.extend([var, sd, wide_c])
                        dve.wait_ge(turned, EB + 1)
                        nc.vector.tensor_copy(bn_scale[:, :], p_d[:, 0:D])
                        nc.vector.tensor_copy(bn_shift[:, :], p_d[:, D:2 * D])

                    @block.tensor
                    def _(pe):
                        var, sd, wide_c = bn_tiles
                        pe.wait_ge(finished, 1)
                        nc.tensor.transpose(p_d[:, 0:D], wide_c[:, 0:D], ident[:, :])
                        nc.tensor.transpose(p_d[:, D:2 * D], wide_c[:, D:2 * D], ident[:, :]).then_inc(turned, 1)

                    @block.scalar
                    def _(act):
                        link = Steps(act_step, 2)

                        def evacuate(b):
                            act.wait_ge(turned, b.n + 1)
                            act.nop(nofuse=True)
                            if b.after(2):
                                act.wait_ge(multiplied, b.n - 1)
                                act.nop(nofuse=True)
                            nc.scalar.copy(t_d[b.s][:, :], p_d[:, :])
                            nc.scalar.copy(t_s[b.s][:, :], p_s[:, :])
                            nc.scalar.copy(t_a[b.s][:, :], p_a[0:17, :]).then_inc(evacuated, 1)

                        def gates(b):
                            link.at(b)
                            act.wait_ge(gates_in, b.n + 1)
                            act.nop(nofuse=True)
                            if b.after(1):
                                act.wait_ge(scanned, b.n)
                                act.nop(nofuse=True)
                            nc.scalar.activation(e_f[:, :], low[:, :], ACT.Exp, scale=-1.0).then_inc(gates_out, 1)
                            act.wait_ge(multiplied, b.n + 1)
                            act.nop(nofuse=True)
                            nc.scalar.activation(size[:, :], p_g[:, :], ACT.Abs).then_inc(link.sem, 1)
                            act.wait_ge(link.sem, link.count())
                            act.nop(nofuse=True)
                            nc.scalar.activation(size[:, :], size[:, :], ACT.Exp, scale=-1.0).then_inc(link.sem, 1)
                            act.wait_ge(link.sem, link.count())
                            act.nop(nofuse=True)
                            nc.scalar.activation(soft[:, :], size[:, :], ACT.Ln, bias=1.0).then_inc(soft_ready, 1)

                        def copy_rows(b):
                            act.wait_ge(turned_back, b.n + 1)
                            act.nop(nofuse=True)
                            if b.after(2):
                                act.wait_ge(scattered[b.s], past(scattered[b.s]) + b.pair * CH * DMA)
                                act.nop(nofuse=True)
                            nc.scalar.copy(res[b.s][:, :], p_out[b.s][:, :]).then_inc(rows_ready, 1)

                        for s in two:
                            nc.scalar.activation(attr[s][:, :, :].rearrange("p c f -> p (c f)"),
                                                 ident[:, 0:1].to_broadcast([P, CH * 17]), ACT.Copy, scale=0.0,
                                                 bias=1.0).then_inc(prepared, 1)
                        pipeline(act, EB, [(gates, 3), (evacuate, 2), (copy_rows, 4)])
                        var, sd, _ = bn_tiles
                        act.wait_ge(prepared, 3)
                        nc.scalar.activation(sd[:, :], var[:, :], ACT.Sqrt).then_inc(prepared, 1)
            end_pass(scattered, gathered, gathered_dst)

        bn_tiles = []
        gated_edge_pass()

        def gated_node_pass():
            with ExitStack() as ctx:
                def sb(name, shape, dt=F32):
                    return ctx.enter_context(nc.sbuf_tensor(f"cn_{name}", shape, dt))

                def ps(name, shape):
                    return ctx.enter_context(nc.psum_tensor(f"cn_{name}", shape, F32))

                two = range(2)
                sum_s = [sb(f"sum{s}", [P, J * D]) for s in two]
                x_s = [sb(f"x{s}", [P, J * D]) for s in two]
                twice = [sb(f"twice{s}", [P, J * D]) for s in two]
                aux_s = [sb(f"aux{s}", [P, J * AUXW]) for s in two]
                v_s = [sb(f"v{s}", [P, J * D]) for s in two]
                y_s = [sb(f"y{s}", [P, J * D]) for s in two]
                o_s = [sb(f"o{s}", [P, J * D]) for s in two]
                att_s = [sb(f"att{s}", [P, J * ADW]) for s in two]
                part = [sb(f"part{s}", [P, 3 * J * 16]) for s in two]
                count = [sb(f"count{s}", [P, J]) for s in two]
                x_t = sb("x_t", [D, J * P])
                each = sb("each", [P, J])
                loop = sb("loop", [P, 3 * J])
                n1, n2 = Norm(sb, "n1"), Norm(sb, "n2")
                p_x = ps("p_x", [P, J * P])
                p_sc = ps("p_sc", [P, J * 6])

                def row_of(t, p, j):
                    return t[0:p, :].unsqueeze(1).to_broadcast([p, j, D])

                def by_head(t, p, j, width, first):
                    return t[0:p, 0:j * width].rearrange("p (j f) -> p f j", f=width)[:, first:first + 3, :]

                with nc.Block() as block:
                    @block.sync
                    def _(sp):
                        def load(b):
                            p, j = pj(b)
                            if b.after(2):
                                sp.wait_ge(pooled, b.n - 1)
                                sp.nop(nofuse=True)
                            if b.after(2):
                                sp.wait_ge(doubled, b.n - 1)
                                sp.nop(nofuse=True)
                            sp.dma_start(sum_s[b.s][0:p, 0:j * D], rows(sums[D], b)).then_inc(loaded[b.s], DMA)
                            sp.dma_start(x_s[b.s][0:p, 0:j * D], rows(x1, b)).then_inc(loaded[b.s], DMA)

                        def load_aux(b):
                            p, j = pj(b)
                            if b.after(2):
                                sp.wait_ge(pooled_b, b.n - 1)
                                sp.nop(nofuse=True)
                            sp.dma_start(aux_s[b.s][0:p, 0:j * AUXW], rows(aux, b)).then_inc(loaded_b[b.s], DMA)

                        def store(b):
                            p, j = pj(b)
                            sp.wait_ge(attended, b.n + 1)
                            sp.nop(nofuse=True)
                            sp.wait_ge(normed_x[1], b.n + 1)
                            sp.nop(nofuse=True)
                            sp.dma_start(rows(x2, b), o_s[b.s][0:p, 0:j * D]).then_inc(stored[b.s], DMA)
                            sp.dma_start(rows(att, b), att_s[b.s][0:p, 0:j * ADW]).then_inc(stored[b.s], DMA)

                        pipeline(sp, NB, [(store, 6), (load_aux, 3), (load, 0)])
                        for s in two:
                            sp.wait_ge(stored[s], blocks_in(NB, s) * 2 * DMA)

                    @block.gpsimd
                    def _(pool):
                        link = Steps(pool_step, 2)

                        def batch_norm(b):
                            p, j = pj(b)
                            link.at(b)
                            pool.wait_ge(loaded[b.s], (b.pair + 1) * 2 * DMA)
                            pool.nop(nofuse=True)
                            if b.after(2):
                                pool.wait_ge(normed_x[0], b.n - 1)
                                pool.nop(nofuse=True)
                            v = split(v_s[b.s], p, j)
                            nc.gpsimd.tensor_tensor(v, split(sum_s[b.s], p, j), row_of(bn_scale, p, j), ALU.mult
                                                    ).then_inc(pool_step, 1)
                            pool.wait_ge(pool_step, link.count())
                            pool.nop(nofuse=True)
                            nc.gpsimd.tensor_tensor(v, v, row_of(bn_shift, p, j), ALU.add).then_inc(pool_step, 1)
                            pool.wait_ge(pool_step, link.count())
                            pool.nop(nofuse=True)
                            nc.gpsimd.tensor_tensor(v, v, split(x_s[b.s], p, j), ALU.add).then_inc(pooled, 1)

                        def gain(b):
                            p, j = pj(b)
                            pool.wait_ge(normed_x[0], b.n + 1)
                            pool.nop(nofuse=True)
                            y = split(y_s[b.s], p, j)
                            nc.gpsimd.tensor_tensor(y, y, row_of(brow["L1_gnn_ln_gamma"], p, j), ALU.mult
                                                    ).then_inc(pooled_c, 1)

                        def loop_parts(b):
                            p, j = pj(b)
                            pool.wait_ge(loaded_b[b.s], (b.pair + 1) * DMA)
                            pool.nop(nofuse=True)
                            if b.after(2):
                                pool.wait_ge(attended, b.n - 1)
                                pool.nop(nofuse=True)
                            attrs = aux_s[b.s][0:p, 0:j * AUXW].rearrange("p (j f) -> p j f", f=AUXW)
                            for h in range(3):
                                nc.gpsimd.tensor_tensor(
                                    part[b.s][0:p, h * 16 * J:h * 16 * J + j * 16].rearrange("p (j f) -> p j f", f=16),
                                    attrs[:, :, 0:16], loop_w[0:p, 16 * h:16 * h + 16].unsqueeze(1)
                                    .to_broadcast([p, j, 16]), ALU.mult)
                            nc.gpsimd.tensor_scalar(count[b.s][0:p, 0:j], attrs[:, :, 16], 1.0, None, ALU.max
                                                    ).then_inc(pooled_b, 1)

                        pipeline(pool, NB, [(gain, 3), (batch_norm, 1), (loop_parts, 4)])

                    @block.vector
                    def _(dve):
                        link_a, link_c = Steps(vec_step, 1), Steps(vec_step_c, 2)
                        link_f, link_g = Steps(factor_step[0], 1), Steps(factor_step[1], 1)
                        link_e = Steps(vec_step_d, 4)

                        def stats_1(b):
                            link_a.at(b)
                            dve.wait_ge(pooled, b.n + 1)
                            dve.nop(nofuse=True)
                            n1.variance(link_a, v_s[b.s], b, stats[0])

                        def factors_1(b):
                            link_f.at(b)
                            dve.wait_ge(rooted_x[0], b.n + 1)
                            dve.nop(nofuse=True)
                            n1.factors(link_f, b, factored[0])

                        def shift(b):
                            p, j = pj(b)
                            link_c.at(b)
                            dve.wait_ge(pooled_c, b.n + 1)
                            dve.nop(nofuse=True)
                            y = split(y_s[b.s], p, j)
                            nc.vector.tensor_tensor(y, y, row_of(brow["L1_gnn_ln_beta"], p, j), ALU.add
                                                    ).then_inc(vec_step_c, 1)

                        def rectify(b):
                            p, j = pj(b)
                            dve.wait_ge(doubled, b.n + 1)
                            dve.nop(nofuse=True)
                            dve.wait_ge(vec_step_c, link_c.count())
                            dve.nop(nofuse=True)
                            nc.vector.scalar_tensor_tensor(out=y_s[b.s][0:p, 0:j * D], in0=y_s[b.s][0:p, 0:j * D],
                                                           scalar=0.0, in1=twice[b.s][0:p, 0:j * D], op0=ALU.max,
                                                           op1=ALU.add).then_inc(gained, 1)
                            dve.wait_ge(gained, b.n + 1)
                            dve.nop(nofuse=True)
                            n2.variance(link_c, y_s[b.s], b, stats[1])

                        def factors_2(b):
                            link_g.at(b)
                            dve.wait_ge(rooted_x[1], b.n + 1)
                            dve.nop(nofuse=True)
                            n2.factors(link_g, b, factored[1])

                        def scores(b):
                            p, j = pj(b)
                            link_e.at(b)
                            dve.wait_ge(scored, b.n + 1)
                            dve.nop(nofuse=True)
                            dve.wait_ge(pooled_b, b.n + 1)
                            dve.nop(nofuse=True)
                            if b.after(2):
                                dve.wait_ge(stored[b.s], b.pair * 2 * DMA)
                                dve.nop(nofuse=True)
                            if b.after(1):
                                dve.wait_ge(attended, b.n)
                                dve.nop(nofuse=True)
                            lp = loop[0:p, :].rearrange("p (h j) -> p h j", h=3)[:, :, 0:j]
                            nc.vector.reciprocal(each[0:p, 0:j], count[b.s][0:p, 0:j])
                            nc.vector.tensor_copy(by_head(att_s[b.s], p, j, ADW, 0), by_head(p_sc, p, j, 6, 3))
                            nc.vector.tensor_reduce(
                                lp, part[b.s][0:p, :].rearrange("p (h j f) -> p h j f", h=3, f=16)[:, :, 0:j, :], AX,
                                ALU.add).then_inc(vec_step_d, 1)
                            dve.wait_ge(vec_step_d, link_e.count())
                            dve.nop(nofuse=True)
                            nc.vector.tensor_tensor(lp, lp, each[0:p, 0:j].unsqueeze(1).to_broadcast([p, 3, j]),
                                                    ALU.mult).then_inc(vec_step_d, 1)
                            dve.wait_ge(vec_step_d, link_e.count())
                            dve.nop(nofuse=True)
                            nc.vector.tensor_tensor(lp, lp, by_head(p_sc, p, j, 6, 0), ALU.add).then_inc(vec_step_d, 1)
                            dve.wait_ge(vec_step_d, link_e.count())
                            dve.nop(nofuse=True)
                            nc.vector.tensor_tensor(lp, lp, by_head(p_sc, p, j, 6, 3), ALU.add).then_inc(vec_step_d, 1)
                            dve.wait_ge(vec_step_d, link_e.count())
                            dve.nop(nofuse=True)
                            nc.vector.scalar_tensor_tensor(out=by_head(att_s[b.s], p, j, ADW, 3), in0=lp, scalar=0.2,
                                                           in1=lp, op0=ALU.mult, op1=ALU.max).then_inc(attended, 1)

                        for s in two:
                            nc.vector.memset(att_s[s][:, :], 0.0).then_inc(prepared, 1)
                        dve.wait_ge(prepared, 2)
                        pipeline(dve, NB, [(stats_1, 2), (factors_2, 4), (shift, 3), (scores, 5), (factors_1, 2),
                                           (rectify, 3)])

                    @block.scalar
                    def _(act):
                        def double(b):
                            p, j = pj(b)
                            act.wait_ge(loaded[b.s], (b.pair + 1) * 2 * DMA)
                            act.nop(nofuse=True)
                            if b.after(2):
                                act.wait_ge(gained, b.n - 1)
                                act.nop(nofuse=True)
                            nc.scalar.mul(twice[b.s][0:p, 0:j * D], x_s[b.s][0:p, 0:j * D], 2.0).then_inc(doubled, 1)

                        def root_1(b):
                            act.wait_ge(stats[0], b.n + 1)
                            act.nop(nofuse=True)
                            n1.root(b, rooted_x[0])

                        def normalise_1(b):
                            p, j = pj(b)
                            act.wait_ge(factored[0], b.n + 1)
                            act.nop(nofuse=True)
                            if b.after(2):
                                act.wait_ge(normed_x[1], b.n - 1)
                                act.nop(nofuse=True)
                            scale_rows(y_s[b.s], v_s[b.s], n1.rstd[b.s], n1.nmr[b.s], p, j).then_inc(normed_x[0], 1)

                        def root_2(b):
                            act.wait_ge(stats[1], b.n + 1)
                            act.nop(nofuse=True)
                            n2.root(b, rooted_x[1])

                        def normalise_2(b):
                            p, j = pj(b)
                            act.wait_ge(factored[1], b.n + 1)
                            act.nop(nofuse=True)
                            if b.after(2):
                                act.wait_ge(stored[b.s], b.pair * 2 * DMA)
                                act.nop(nofuse=True)
                            scale_rows(o_s[b.s], y_s[b.s], n2.rstd[b.s], n2.nmr[b.s], p, j).then_inc(normed_x[1], 1)

                        def evacuate(b):
                            p, j = pj(b)
                            act.wait_ge(turned, b.n + 1)
                            act.nop(nofuse=True)
                            if b.after(1):
                                act.wait_ge(scored, b.n)
                                act.nop(nofuse=True)
                            nc.scalar.copy(cols(x_t, D, p, j), cols(p_x, D, p, j)).then_inc(evacuated, 1)

                        pipeline(act, NB, [(root_2, 4), (root_1, 2), (normalise_2, 4), (normalise_1, 2), (evacuate, 4),
                                           (double, 1)])

                    @block.tensor
                    def _(pe):
                        def turn(b):
                            p, j = pj(b)
                            pe.wait_ge(normed_x[1], b.n + 1)
                            pe.nop(nofuse=True)
                            if b.after(1):
                                pe.wait_ge(evacuated, b.n)
                                pe.nop(nofuse=True)
                            turn_rows(p_x, o_s[b.s], p, j, D).then_inc(turned, 1)

                        def score(b):
                            p, j = pj(b)
                            pe.wait_ge(evacuated, b.n + 1)
                            pe.nop(nofuse=True)
                            if b.after(1):
                                pe.wait_ge(attended, b.n)
                                pe.nop(nofuse=True)
                            times_weight(p_sc, x_t, score_w[:, :], p, j, D, 6).then_inc(scored, 1)

                        pipeline(pe, NB, [(score, 5), (turn, 4)])
            end_pass()

        gated_node_pass()

        def attention_edge_pass():
            with ExitStack() as ctx:
                def sb(name, shape, dt=F32):
                    return ctx.enter_context(nc.sbuf_tensor(f"ge_{name}", shape, dt))

                def ps(name, shape):
                    return ctx.enter_context(nc.psum_tensor(f"ge_{name}", shape, F32))

                two = range(2)
                B = EDGE_BLOCK
                src_s = [sb(f"src{s}", [P, CH], U32) for s in two]
                dst_s = [sb(f"dst{s}", [P, CH], U32) for s in two]
                end_s = [sb(f"end{s}", [P, CH], U32) for s in two]
                got_s = [sb(f"got_src{s}", [P, CH, D]) for s in two]
                small = [sb(f"small{s}", [P, CH, ADW + 16]) for s in two]
                t_x = [sb(f"t_x{s}", [D, B]) for s in two]
                t_a = sb("t_a", [ADW + 16, B])
                score = sb("score", [3, B])
                leak = sb("leak", [3, B])
                capped = sb("capped", [3, B])
                jump = [sb(f"jump{s}", [3, B]) for s in two]
                top = [sb(f"top{s}", [3, 1 + B]) for s in two]
                gaps = sb("gaps", [3, 3 * B])
                powers = [sb(f"powers{s}", [3, 3 * B]) for s in two]
                parts = [sb(f"parts{s}", [67, 2 * B], BF16) for s in two]
                middle = sb("middle", [3, 2 * B], BF16)
                rest = sb("rest", [3, 2 * B])
                starts = [sb(f"starts{s}", [3, B]) for s in two]
                added = sb("added", [3, B])
                denom = [sb(f"denom{s}", [3, B]) for s in two]
                inv = sb("inv", [P, CH, 3])
                less = sb("less", [P, CH, 3])
                part = sb("part", [D, B])
                heads = sb("heads", [P, 3, CH * D])
                run = [[sb(f"run{h}_{s}", [D, B]) for s in two] for h in range(3)]
                res = [sb(f"res{s}", [P, CH * GATW]) for s in two]
                p_x, p_a, p_sc, p_own, p_w, p_dec = (ps(n, [P, B]) for n in ("p_x", "p_a", "p_sc", "p_own", "p_w", "p_dec"))
                p_y = [ps(f"p_y{s}", [P, B]) for s in two]

                with nc.Block() as block:
                    @block.sync
                    def _(sp):
                        def load(b):
                            if b.after(2):
                                sp.wait_ge(gathered[b.s], past(gathered[b.s]) + b.pair * CH * DMA)
                                sp.nop(nofuse=True)
                            if b.after(2):
                                sp.wait_ge(gathered_dst[b.s], past(gathered_dst[b.s]) + b.pair * CH * DMA)
                                sp.nop(nofuse=True)
                            sp.dma_start(src_s[b.s][:, :], src_i[bass.ds(b.n * P, P), :]).then_inc(src_loaded[b.s], DMA)
                            sp.dma_start(dst_s[b.s][:, :], dst_i[bass.ds(b.n * P, P), :]).then_inc(dst_loaded[b.s], DMA)

                        def load_attr(b):
                            sp.wait_ge(prepared, 6)
                            if b.after(2):
                                sp.wait_ge(turned, b.n - 1)
                                sp.nop(nofuse=True)
                            p = edge_tail_p if b.tail else P
                            sp.dma_start(small[b.s][0:p, :, ADW:ADW + 16],
                                         a["edge_attr_16"][bass.ds(b.n * EDGE_BLOCK, p * CH), :]
                                         .rearrange("(p c) f -> p c f", p=p)).then_inc(attr_loaded[b.s], DMA)

                        def load_end(b):
                            if b.after(2):
                                sp.wait_ge(scattered[b.s], past(scattered[b.s]) + b.pair * CH * DMA)
                                sp.nop(nofuse=True)
                            sp.dma_start(end_s[b.s][:, :], end_i[bass.ds(b.n * P, P), :]).then_inc(end_loaded[b.s], DMA)

                        pipeline(sp, EB, [(load_attr, 1), (load, 0), (load_end, 4)])

                    @block.gpsimd
                    def _(pool):
                        def gather(b):
                            pool.wait_ge(src_loaded[b.s], (b.pair + 1) * DMA)
                            pool.nop(nofuse=True)
                            pool.wait_ge(dst_loaded[b.s], (b.pair + 1) * DMA)
                            pool.nop(nofuse=True)
                            if b.after(2):
                                pool.wait_ge(turned, b.n - 1)
                                pool.nop(nofuse=True)
                            if b.after(2):
                                pool.wait_ge(own_turned, b.n - 1)
                                pool.nop(nofuse=True)
                            pool.wait_ge(prepared, 6)
                            for j in range(CH):
                                pool.indirect_dma_start(
                                    got_s[b.s][:, j, :], None, x2,
                                    bass.IndirectOffsetOnAxis(ap=src_s[b.s][:, j:j + 1], axis=0)
                                ).then_inc(gathered[b.s], DMA)
                            for j in range(CH):
                                pool.indirect_dma_start(
                                    small[b.s][:, j, 0:ADW], None, att,
                                    bass.IndirectOffsetOnAxis(ap=dst_s[b.s][:, j:j + 1], axis=0)
                                ).then_inc(gathered_dst[b.s], DMA)

                        def scatter(b):
                            pool.wait_ge(end_loaded[b.s], (b.pair + 1) * DMA)
                            pool.nop(nofuse=True)
                            pool.wait_ge(rows_ready, b.n + 1)
                            pool.nop(nofuse=True)
                            for j in range(CH):
                                pool.indirect_dma_start(
                                    sums[GATW], bass.IndirectOffsetOnAxis(ap=end_s[b.s][:, j:j + 1], axis=0),
                                    res[b.s][:, j * GATW:(j + 1) * GATW], None, bounds_check=N - 1, oob_is_err=False
                                ).then_inc(scattered[b.s], DMA)

                        link_p = Steps(pool_step, 1)

                        def denominator_parts(b):
                            link_p.at(b)
                            pool.wait_ge(powered, b.n + 1)
                            pool.nop(nofuse=True)
                            if b.after(1):
                                pool.wait_ge(attended, b.n)
                                pool.nop(nofuse=True)
                            nc.gpsimd.tensor_tensor(added[:, :], starts[b.s][:, :], powers[b.s][:, 2 * B:3 * B], ALU.mult
                                                    ).then_inc(pool_step, 1)
                            pool.wait_ge(pool_step, link_p.count())
                            pool.nop(nofuse=True)
                            nc.gpsimd.tensor_tensor(added[:, :], added[:, :], powers[b.s][:, B:2 * B], ALU.add
                                                    ).then_inc(pooled, 1)

                        pipeline(pool, EB, [(denominator_parts, 4), (gather, 1), (scatter, 5)])
                        for s in two:
                            pool.wait_ge(scattered[s], past(scattered[s]) + blocks_in(EB, s) * CH * DMA)

                    @block.tensor
                    def _(pe):
                        def turn(b):
                            pe.wait_ge(gathered[b.s], past(gathered[b.s]) + (b.pair + 1) * CH * DMA)
                            pe.nop(nofuse=True)
                            pe.wait_ge(gathered_dst[b.s], past(gathered_dst[b.s]) + (b.pair + 1) * CH * DMA)
                            pe.nop(nofuse=True)
                            pe.wait_ge(attr_loaded[b.s], (b.pair + 1) * DMA)
                            pe.nop(nofuse=True)
                            if b.after(1):
                                pe.wait_ge(evacuated, b.n)
                                pe.nop(nofuse=True)
                            if b.after(2):
                                pe.wait_ge(denom_taken, b.n - 1)
                                pe.nop(nofuse=True)
                            for bank, got, width in ((p_x, got_s, D), (p_a, small, ADW + 16)):
                                for j in range(CH):
                                    last = nc.tensor.transpose(bank[0:width, j:B:CH], got[b.s][:, j, :], ident[:, :])
                            last.then_inc(turned, 1)

                        def turn_own(b):
                            if b.after(1):
                                pe.wait_ge(gates_in, b.n)
                                pe.nop(nofuse=True)
                            for j in range(CH):
                                last = nc.tensor.transpose(p_own[0:3, j:B:CH], small[b.s][:, j, 3:6], ident[:, :])
                            last.then_inc(own_turned, 1)

                        def scores(b):
                            pe.wait_ge(evacuated, b.n + 1)
                            pe.nop(nofuse=True)
                            if b.after(1):
                                pe.wait_ge(gates_in, b.n)
                                pe.nop(nofuse=True)
                            nc.tensor.matmul(p_sc[0:3, :], score_w[:, 0:3], t_x[b.s][:, :], start=True, stop=False)
                            nc.tensor.matmul(p_sc[0:3, :], edge_w[:, 0:3], t_a[:, :], start=False, stop=True
                                             ).then_inc(scored, 1)

                        def spread_heads(b):
                            pe.wait_ge(low_ready, b.n + 1)
                            pe.nop(nofuse=True)
                            pe.wait_ge(parts_ready, b.n + 1)
                            pe.nop(nofuse=True)
                            for h in range(3):
                                if b.after(1) or h:
                                    pe.wait_ge(weighted, b.n * 3 + h)
                                    pe.nop(nofuse=True)
                                nc.tensor.matmul(p_w[:, :], pick_b[:, h * D:(h + 1) * D], parts[b.s][:, B:2 * B],
                                                 start=True, stop=True).then_inc(spread, 1)
                                if b.after(1) or h:
                                    pe.wait_ge(scanned, b.n * 3 + h)
                                    pe.nop(nofuse=True)
                                nc.tensor.matmul(p_dec[:, :], pick_b[:, h * D:(h + 1) * D], parts[b.s][:, 0:B],
                                                 start=True, stop=True).then_inc(spread_b, 1)

                        def turn_denominators(b):
                            pe.wait_ge(attended, b.n + 1)
                            pe.nop(nofuse=True)
                            pe.wait_ge(evacuated, min(b.n + 2, EB) if isinstance(b.n, int) else b.n + 2)
                            pe.nop(nofuse=True)
                            for j in range(CH):
                                nc.tensor.transpose(p_a[:, 6 * j:6 * j + 3], denom[b.s][:, j:B:CH], ident[0:3, 0:3])
                                last = nc.tensor.transpose(p_a[:, 6 * j + 3:6 * j + 6], powers[b.s][:, 2 * B + j:3 * B:CH],
                                                           ident[0:3, 0:3])
                            last.then_inc(denom_turned, 1)

                        def messages(b, chunks):
                            pe.wait_ge(scanned, b.n * 3 + 3)
                            pe.nop(nofuse=True)
                            for j in chunks:
                                if b.after(1) or j > 1:
                                    pe.wait_ge(taken, b.n * CH + j - 1)
                                    pe.nop(nofuse=True)
                                for h in range(3):
                                    last = nc.tensor.matmul(p_y[j % 2][:, h * D:(h + 1) * D], run[h][b.s][:, j:B:CH],
                                                            head_w[:, h * D:(h + 1) * D], start=True, stop=True)
                                last.then_inc(turned_back, 1)

                        def first_messages(b):
                            messages(b, range(CH // 2))

                        def last_messages(b):
                            messages(b, range(CH // 2, CH))

                        pipeline(pe, EB, [(scores, 3), (spread_heads, 4), (turn_denominators, 4), (first_messages, 4),
                                          (turn, 2), (last_messages, 4), (turn_own, 2)])

                    @block.vector
                    def _(dve):
                        link_a = Steps(vec_step, 3)
                        link_m = Steps(vec_step_d, 2)

                        def maxima(b):
                            link_a.at(b)
                            first = isinstance(b.n, int) and b.n == 0
                            dve.wait_ge(leaked, b.n + 1)
                            dve.nop(nofuse=True)
                            dve.wait_ge(own_turned, b.n + 1)
                            dve.nop(nofuse=True)
                            if b.after(1):
                                dve.wait_ge(powered, b.n)
                                dve.nop(nofuse=True)
                            nc.vector.tensor_tensor(score[:, :], p_sc[0:3, :], leak[:, :], ALU.max)
                            if first:
                                nc.vector.memset(top[b.s][:, 0:1], 0.0).then_inc(link_a.sem, 1)
                            else:
                                nc.vector.tensor_copy(top[b.s][:, 0:1], top[1 - b.s][:, B:1 + B]).then_inc(link_a.sem, 1)
                            dve.wait_ge(link_a.sem, link_a.count())
                            dve.nop(nofuse=True)
                            nc.vector.tensor_tensor(capped[:, :], score[:, :], p_own[0:3, :], ALU.max
                                                    ).then_inc(link_a.sem, 1)

                        def gaps_below(b):
                            first = isinstance(b.n, int) and b.n == 0
                            dve.wait_ge(link_a.sem, link_a.count())
                            dve.nop(nofuse=True)
                            nc.vector.tensor_tensor_scan(
                                top[b.s][:, 1:1 + B], jump[b.s][:, :], capped[:, :],
                                -FAR if first else top[1 - b.s][:, B:1 + B], ALU.add, ALU.max).then_inc(link_a.sem, 1)
                            dve.wait_ge(link_a.sem, link_a.count())
                            dve.nop(nofuse=True)
                            nc.vector.tensor_tensor(gaps[:, 2 * B:3 * B], p_own[0:3, :], top[b.s][:, 1:1 + B], ALU.subtract)
                            nc.vector.tensor_tensor(gaps[:, B:2 * B], score[:, :], top[b.s][:, 1:1 + B],
                                                    ALU.subtract)
                            nc.vector.tensor_tensor(capped[:, :], top[b.s][:, 0:B], jump[b.s][:, :], ALU.add
                                                    ).then_inc(gained, 1)
                            dve.wait_ge(gained, b.n + 1)
                            dve.nop(nofuse=True)
                            nc.vector.tensor_tensor(gaps[:, 0:B], capped[:, :], top[b.s][:, 1:1 + B],
                                                    ALU.subtract).then_inc(gates_in, 1)

                        def take_high(b):
                            dve.wait_ge(high_ready, b.n + 1)
                            dve.nop(nofuse=True)
                            if b.after(1):
                                dve.wait_ge(parts_ready, b.n)
                                dve.nop(nofuse=True)
                            nc.vector.tensor_tensor(rest[:, :], powers[b.s][:, 0:2 * B], parts[b.s][0:3, :],
                                                    ALU.subtract).then_inc(rest_ready, 1)

                        def take_middle(b):
                            dve.wait_ge(middle_ready, b.n + 1)
                            dve.nop(nofuse=True)
                            nc.vector.tensor_tensor(parts[b.s][64:67, :], rest[:, :], middle[:, :],
                                                    ALU.subtract).then_inc(low_ready, 1)

                        def denominators(b):
                            first = isinstance(b.n, int) and b.n == 0
                            dve.wait_ge(pooled, b.n + 1)
                            dve.nop(nofuse=True)
                            if b.after(2):
                                dve.wait_ge(denom_turned, b.n - 1)
                                dve.nop(nofuse=True)
                            nc.vector.tensor_tensor_scan(
                                denom[b.s][:, :], powers[b.s][:, 0:B], added[:, :],
                                0.0 if first else denom[1 - b.s][:, B - 1:B], ALU.mult, ALU.add).then_inc(attended, 1)

                        def numerators(b):
                            first = isinstance(b.n, int) and b.n == 0
                            if b.after(2):
                                dve.wait_ge(turned_back, (b.n - 1) * CH)
                                dve.nop(nofuse=True)
                            for h in range(3):
                                dve.wait_ge(spread, b.n * 3 + h + 1)
                                dve.nop(nofuse=True)
                                nc.vector.tensor_tensor(part[:, :], t_x[b.s][:, :], p_w[:, :], ALU.mult
                                                        ).then_inc(weighted, 1)
                                dve.wait_ge(spread_b, b.n * 3 + h + 1)
                                dve.nop(nofuse=True)
                                dve.wait_ge(weighted, b.n * 3 + h + 1)
                                dve.nop(nofuse=True)
                                nc.vector.tensor_tensor_scan(
                                    run[h][b.s][:, :], p_dec[:, :], part[:, :],
                                    0.0 if first else run[h][1 - b.s][:, B - 1:B], ALU.mult, ALU.add
                                ).then_inc(scanned, 1)
                                dve.wait_ge(scanned, b.n * 3 + h + 1)
                                dve.nop(nofuse=True)

                        def combine(b):
                            link_m.at(b)
                            dve.wait_ge(denom_turned, b.n + 1)
                            dve.nop(nofuse=True)
                            both = p_a[:, 0:6 * CH].rearrange("p (c f) -> p c f", f=6)
                            nc.vector.reciprocal(inv[:, :, :], both[:, :, 0:3]).then_inc(link_m.sem, 1)
                            dve.wait_ge(link_m.sem, link_m.count())
                            dve.nop(nofuse=True)
                            nc.vector.tensor_tensor(less[:, :, :], both[:, :, 3:6], inv[:, :, :], ALU.mult
                                                    ).then_inc(denom_taken, 1)
                            scale_messages(b, range(CH // 2))

                        def scale_messages(b, chunks):
                            for j in chunks:
                                dve.wait_ge(turned_back, b.n * CH + j + 1)
                                dve.nop(nofuse=True)
                                nc.vector.tensor_tensor(
                                    heads[:, :, j * D:(j + 1) * D], p_y[j % 2][:, 0:3 * D].rearrange("p (h f) -> p h f", h=3),
                                    inv[:, j, :].unsqueeze(2).to_broadcast([P, 3, D]), ALU.mult).then_inc(taken, 1)

                        def add_messages(b):
                            scale_messages(b, range(CH // 2, CH))
                            dve.wait_ge(taken, (b.n + 1) * CH)
                            dve.nop(nofuse=True)
                            if b.after(2):
                                dve.wait_ge(scattered[b.s], past(scattered[b.s]) + b.pair * CH * DMA)
                                dve.nop(nofuse=True)
                            rows_out = res[b.s][:, :].rearrange("p (c f) -> p c f", f=GATW)
                            nc.vector.tensor_scalar(rows_out[:, :, D:D + 3], less[:, :, :], -1.0, None, ALU.add)
                            nc.vector.tensor_tensor(heads[:, 0, :], heads[:, 0, :], heads[:, 1, :], ALU.add
                                                    ).then_inc(link_m.sem, 1)
                            dve.wait_ge(link_m.sem, link_m.count())
                            dve.nop(nofuse=True)
                            nc.vector.tensor_tensor(
                                rows_out[:, :, 0:D], heads[:, 0, :].rearrange("p (c f) -> p c f", f=D),
                                heads[:, 2, :].rearrange("p (c f) -> p c f", f=D), ALU.add).then_inc(rows_ready, 1)

                        for s in two:
                            nc.vector.memset(res[s][:, :], 0.0).then_inc(prepared, 1)
                            nc.vector.memset(small[s][:, :, :], 0.0).then_inc(prepared, 1)
                            nc.vector.memset(parts[s][:, :], 0.0).then_inc(prepared, 1)
                        dve.wait_ge(prepared, 6)
                        pipeline(dve, EB, [(take_high, 4), (denominators, 4), (take_middle, 4), (numerators, 4), (maxima, 3),
                                           (combine, 4), (gaps_below, 3), (add_messages, 4)])

                    @block.scalar
                    def _(act):
                        def evacuate(b):
                            act.wait_ge(turned, b.n + 1)
                            act.nop(nofuse=True)
                            if b.after(1):
                                act.wait_ge(scored, b.n)
                                act.nop(nofuse=True)
                            if b.after(2):
                                act.wait_ge(scanned, (b.n - 1) * 3)
                                act.nop(nofuse=True)
                            nc.scalar.copy(t_x[b.s][:, :], p_x[:, :])
                            nc.scalar.copy(t_a[:, :], p_a[0:ADW + 16, :]).then_inc(evacuated, 1)

                        def marks(b):
                            now = cont[0:3, bass.ds(b.n * B, B)]
                            if b.after(2):
                                act.wait_ge(gates_in, b.n - 1)
                                act.nop(nofuse=True)
                            if b.after(2):
                                act.wait_ge(pooled, b.n - 1)
                                act.nop(nofuse=True)
                            nc.scalar.activation(jump[b.s][:, :], now, ACT.Copy, scale=FAR, bias=-FAR)
                            nc.scalar.activation(starts[b.s][:, :], now, ACT.Copy, scale=-1.0, bias=1.0)

                        def leaks(b):
                            act.wait_ge(scored, b.n + 1)
                            act.nop(nofuse=True)
                            if b.after(1):
                                act.wait_ge(gates_in, b.n)
                                act.nop(nofuse=True)
                            nc.scalar.mul(leak[:, :], p_sc[0:3, :], 0.2).then_inc(leaked, 1)

                        def raise_gaps(b):
                            act.wait_ge(gates_in, b.n + 1)
                            act.nop(nofuse=True)
                            if b.after(2):
                                act.wait_ge(spread_b, (b.n - 1) * 3)
                                act.nop(nofuse=True)
                            if b.after(2):
                                act.wait_ge(denom_turned, b.n - 1)
                                act.nop(nofuse=True)
                            nc.scalar.activation(powers[b.s][:, :], gaps[:, :], ACT.Exp).then_inc(powered, 1)
                            act.wait_ge(powered, b.n + 1)
                            act.nop(nofuse=True)
                            act.wait_ge(prepared, 6)
                            nc.scalar.copy(parts[b.s][0:3, :], powers[b.s][:, 0:2 * B]).then_inc(high_ready, 1)

                        def round_middle(b):
                            act.wait_ge(rest_ready, b.n + 1)
                            act.nop(nofuse=True)
                            if b.after(1):
                                act.wait_ge(low_ready, b.n)
                                act.nop(nofuse=True)
                            nc.scalar.copy(middle[:, :], rest[:, :]).then_inc(middle_ready, 1)
                            nc.scalar.copy(parts[b.s][32:35, :], rest[:, :]).then_inc(parts_ready, 1)

                        pipeline(act, EB, [(round_middle, 4), (marks, 3), (leaks, 3), (evacuate, 2), (raise_gaps, 3)])
            end_pass(scattered, gathered, gathered_dst)

        def attention_node_pass():
            with ExitStack() as ctx:
                def sb(name, shape, dt=F32):
                    return ctx.enter_context(nc.sbuf_tensor(f"gn_{name}", shape, dt))

                def ps(name, shape):
                    return ctx.enter_context(nc.psum_tensor(f"gn_{name}", shape, F32))

                two = range(2)
                H1 = 64
                sum_s = [sb(f"sum{s}", [P, J * GATW]) for s in two]
                x_s = [sb(f"x{s}", [P, J * D]) for s in two]
                x_beta = [sb(f"x_beta{s}", [P, J * D]) for s in two]
                inv = [sb(f"inv{s}", [P, J]) for s in two]
                weight = [sb(f"weight{s}", [P, J * 3]) for s in two]
                r_s = [sb(f"r{s}", [P, J * D]) for s in two]
                y_s = [sb(f"y{s}", [P, J * D]) for s in two]
                o_s = [sb(f"o{s}", [P, J * D]) for s in two]
                g_s = [sb(f"g{s}", [P, J * H1]) for s in two]
                heads = sb("heads", [P, 3 * J * D])
                x_t = sb("x_t", [D, J * P])
                o_t = sb("o_t", [D, J * P])
                n1, n2 = Norm(sb, "n1"), Norm(sb, "n2")
                p_x = ps("p_x", [P, J * P])
                p_o = ps("p_o", [P, J * P])
                BANKS = 3
                p_h = [ps(f"p_h{s}", [P, 3 * D]) for s in range(BANKS)]
                p_g = ps("p_g", [P, J * H1])

                def row_of(t, p, j):
                    return t[0:p, :].unsqueeze(1).to_broadcast([p, j, D])

                def head(h, p, j):
                    return heads[0:p, h * J * D:h * J * D + j * D]

                with nc.Block() as block:
                    @block.sync
                    def _(sp):
                        def load(b):
                            p, j = pj(b)
                            if b.after(2):
                                sp.wait_ge(pooled_b, b.n - 1)
                                sp.nop(nofuse=True)
                            if b.after(2):
                                sp.wait_ge(turned, b.n - 1)
                                sp.nop(nofuse=True)
                            sp.dma_start(x_s[b.s][0:p, 0:j * D], rows(x2, b)).then_inc(loaded[b.s], DMA)
                            sp.dma_start(sum_s[b.s][0:p, 0:j * GATW], rows(sums[GATW], b)).then_inc(loaded_c[b.s], DMA)

                        def load_inv(b):
                            p, j = pj(b)
                            if b.after(2):
                                sp.wait_ge(finished, b.n - 1)
                                sp.nop(nofuse=True)
                            sp.dma_start(inv[b.s][0:p, 0:j], rows(dinv, b)).then_inc(loaded_b[b.s], DMA)

                        def store(b):
                            p, j = pj(b)
                            sp.wait_ge(normed_x[1], b.n + 1)
                            sp.nop(nofuse=True)
                            sp.wait_ge(finished, b.n + 1)
                            sp.nop(nofuse=True)
                            sp.dma_start(rows(x3, b), o_s[b.s][0:p, 0:j * D]).then_inc(stored[b.s], DMA)
                            sp.dma_start(rows(scaled[64], b), g_s[b.s][0:p, 0:j * H1]).then_inc(stored[b.s], DMA)

                        pipeline(sp, NB, [(store, 6), (load_inv, 4), (load, 0)])
                        for s in two:
                            sp.wait_ge(stored[s], blocks_in(NB, s) * 2 * DMA)

                    @block.gpsimd
                    def _(pool):
                        link = Steps(pool_step, 1)

                        def add_heads(b):
                            p, j = pj(b)
                            pool.wait_ge(loop_step, b.n * J + j)
                            pool.nop(nofuse=True)
                            nc.gpsimd.tensor_tensor(head(0, p, j), head(0, p, j), head(1, p, j), ALU.add
                                                    ).then_inc(pooled_c, 1)

                        def base(b):
                            p, j = pj(b)
                            link.at(b)
                            pool.wait_ge(loaded[b.s], (b.pair + 1) * DMA)
                            pool.nop(nofuse=True)
                            pool.wait_ge(loaded_c[b.s], (b.pair + 1) * DMA)
                            pool.nop(nofuse=True)
                            if b.after(2):
                                pool.wait_ge(normed_x[0], b.n - 1)
                                pool.nop(nofuse=True)
                            both = split(sum_s[b.s], p, j, GATW)
                            r = split(r_s[b.s], p, j)
                            nc.gpsimd.tensor_scalar(weight[b.s][0:p, 0:j * 3].rearrange("p (j h) -> p j h", h=3),
                                                    both[:, :, D:D + 3], 1.0, None, ALU.add)
                            nc.gpsimd.tensor_tensor(r, both[:, :, 0:D], split(x_s[b.s], p, j), ALU.add
                                                    ).then_inc(pool_step, 1)
                            pool.wait_ge(pool_step, link.count())
                            pool.nop(nofuse=True)
                            nc.gpsimd.tensor_tensor(r, r, row_of(gat_row, p, j), ALU.add).then_inc(pooled, 1)

                        def add_beta(b):
                            p, j = pj(b)
                            if b.after(2):
                                pool.wait_ge(gained, b.n - 1)
                                pool.nop(nofuse=True)
                            nc.gpsimd.tensor_tensor(split(x_beta[b.s], p, j), split(x_s[b.s], p, j),
                                                    row_of(brow["L2_gnn_ln_b"], p, j), ALU.add).then_inc(pooled_b, 1)

                        pipeline(pool, NB, [(add_heads, 2), (base, 1), (add_beta, 1)])

                    @block.vector
                    def _(dve):
                        link_w, link_c = Steps(vec_step_b, 3), Steps(vec_step_c, 2)
                        link_f, link_g = Steps(factor_step[0], 1), Steps(factor_step[1], 1)

                        def loops(b):
                            p, j = pj(b)
                            dve.wait_ge(pooled, b.n + 1)
                            dve.nop(nofuse=True)
                            for q in range(j):
                                dve.wait_ge(multiplied, b.n * J + q + 1)
                                dve.nop(nofuse=True)
                                nc.vector.tensor_tensor(
                                    heads[0:p, :].rearrange("p (h f) -> p h f", h=3)[:, :, q * D:(q + 1) * D],
                                    p_h[q % BANKS][0:p, :].rearrange("p (h f) -> p h f", h=3),
                                    weight[b.s][0:p, q * 3:q * 3 + 3].unsqueeze(2).to_broadcast([p, 3, D]), ALU.mult
                                ).then_inc(loop_step, 1)

                        def add_last_head(b):
                            p, j = pj(b)
                            link_w.at(b)
                            dve.wait_ge(loop_step, b.n * J + j)
                            dve.nop(nofuse=True)
                            r = r_s[b.s][0:p, 0:j * D]
                            nc.vector.tensor_tensor(r, r, head(2, p, j), ALU.add).then_inc(vec_step_b, 1)

                        def add_first_heads(b):
                            p, j = pj(b)
                            dve.wait_ge(vec_step_b, link_w.count())
                            dve.nop(nofuse=True)
                            dve.wait_ge(pooled_c, b.n + 1)
                            dve.nop(nofuse=True)
                            r = r_s[b.s][0:p, 0:j * D]
                            nc.vector.tensor_tensor(r, r, head(0, p, j), ALU.add).then_inc(vec_step_b, 1)

                        def stats_1(b):
                            dve.wait_ge(vec_step_b, link_w.count())
                            dve.nop(nofuse=True)
                            n1.variance(link_w, r_s[b.s], b, stats[0])

                        def factors_1(b):
                            link_f.at(b)
                            dve.wait_ge(rooted_x[0], b.n + 1)
                            dve.nop(nofuse=True)
                            n1.factors(link_f, b, factored[0])

                        def gain(b):
                            p, j = pj(b)
                            link_c.at(b)
                            dve.wait_ge(normed_x[0], b.n + 1)
                            dve.nop(nofuse=True)
                            y = split(y_s[b.s], p, j)
                            nc.vector.tensor_tensor(y, y, row_of(brow["L2_gnn_ln_g"], p, j), ALU.mult
                                                    ).then_inc(vec_step_c, 1)

                        def add_x(b):
                            p, j = pj(b)
                            dve.wait_ge(vec_step_c, link_c.count())
                            dve.nop(nofuse=True)
                            dve.wait_ge(pooled_b, b.n + 1)
                            dve.nop(nofuse=True)
                            y = y_s[b.s][0:p, 0:j * D]
                            nc.vector.tensor_tensor(y, y, x_beta[b.s][0:p, 0:j * D], ALU.add).then_inc(gained, 1)

                        def stats_2(b):
                            dve.wait_ge(gained, b.n + 1)
                            dve.nop(nofuse=True)
                            n2.variance(link_c, y_s[b.s], b, stats[1])

                        def factors_2(b):
                            link_g.at(b)
                            dve.wait_ge(rooted_x[1], b.n + 1)
                            dve.nop(nofuse=True)
                            n2.factors(link_g, b, factored[1])

                        def scale(b):
                            p, j = pj(b)
                            dve.wait_ge(scored, b.n + 1)
                            dve.nop(nofuse=True)
                            dve.wait_ge(loaded_b[b.s], (b.pair + 1) * DMA)
                            dve.nop(nofuse=True)
                            if b.after(2):
                                dve.wait_ge(stored[b.s], b.pair * 2 * DMA)
                                dve.nop(nofuse=True)
                            nc.vector.tensor_tensor(split(g_s[b.s], p, j, H1), split(p_g, p, j, H1),
                                                    per_row(inv[b.s], p, j, H1), ALU.mult).then_inc(finished, 1)

                        pipeline(dve, NB, [(factors_1, 3), (factors_2, 4), (add_last_head, 2), (scale, 5),
                                           (add_first_heads, 2), (stats_1, 2), (gain, 3), (add_x, 3), (stats_2, 3),
                                           (loops, 1)])

                    @block.tensor
                    def _(pe):
                        def turn(b):
                            p, j = pj(b)
                            pe.wait_ge(loaded[b.s], (b.pair + 1) * DMA)
                            pe.nop(nofuse=True)
                            if b.after(1):
                                pe.wait_ge(evacuated, b.n)
                                pe.nop(nofuse=True)
                            turn_rows(p_x, x_s[b.s], p, j, D).then_inc(turned, 1)

                        def loops(b, groups):
                            for q in groups:
                                if q >= BANKS:
                                    pe.wait_ge(loop_step, b.n * J + q - BANKS + 1)
                                    pe.nop(nofuse=True)
                                p = pj(b)[0]
                                nc.tensor.matmul(p_h[q % BANKS][0:p, :], x_t[:, q * P:q * P + p], head_w[:, :],
                                                 start=True, stop=True).then_inc(multiplied, 1)

                        def first_loops(b):
                            pe.wait_ge(evacuated, b.n + 1)
                            pe.nop(nofuse=True)
                            if b.after(1):
                                pe.wait_ge(loop_step, b.n * J)
                                pe.nop(nofuse=True)
                            loops(b, range(min(BANKS, pj(b)[1])))

                        def last_loops(b):
                            loops(b, range(BANKS, pj(b)[1]))

                        def turn_x3(b):
                            p, j = pj(b)
                            pe.wait_ge(normed_x[1], b.n + 1)
                            pe.nop(nofuse=True)
                            if b.after(1):
                                pe.wait_ge(evacuated_b, b.n)
                                pe.nop(nofuse=True)
                            turn_rows(p_o, o_s[b.s], p, j, D).then_inc(turned_b, 1)

                        def next_weight(b):
                            p, j = pj(b)
                            pe.wait_ge(evacuated_b, b.n + 1)
                            pe.nop(nofuse=True)
                            if b.after(1):
                                pe.wait_ge(finished, b.n)
                                pe.nop(nofuse=True)
                            times_weight(p_g, o_t, w["L3_gnn_W1"][:, :], p, j, D, H1).then_inc(scored, 1)

                        pipeline(pe, NB, [(next_weight, 5), (turn, 1), (turn_x3, 4), (first_loops, 1), (last_loops, 1)])

                    @block.scalar
                    def _(act):
                        def evacuate(b):
                            p, j = pj(b)
                            act.wait_ge(turned, b.n + 1)
                            act.nop(nofuse=True)
                            if b.after(1):
                                act.wait_ge(multiplied, b.n * J)
                                act.nop(nofuse=True)
                            nc.scalar.copy(cols(x_t, D, p, j), cols(p_x, D, p, j)).then_inc(evacuated, 1)

                        def root_1(b):
                            act.wait_ge(stats[0], b.n + 1)
                            act.nop(nofuse=True)
                            n1.root(b, rooted_x[0])

                        def normalise_1(b):
                            p, j = pj(b)
                            act.wait_ge(factored[0], b.n + 1)
                            act.nop(nofuse=True)
                            if b.after(2):
                                act.wait_ge(normed_x[1], b.n - 1)
                                act.nop(nofuse=True)
                            scale_rows(y_s[b.s], r_s[b.s], n1.rstd[b.s], n1.nmr[b.s], p, j).then_inc(normed_x[0], 1)

                        def root_2(b):
                            act.wait_ge(stats[1], b.n + 1)
                            act.nop(nofuse=True)
                            n2.root(b, rooted_x[1])

                        def normalise_2(b):
                            p, j = pj(b)
                            act.wait_ge(factored[1], b.n + 1)
                            act.nop(nofuse=True)
                            if b.after(2):
                                act.wait_ge(stored[b.s], b.pair * 2 * DMA)
                                act.nop(nofuse=True)
                            if b.after(2):
                                act.wait_ge(turned_b, b.n - 1)
                                act.nop(nofuse=True)
                            scale_rows(o_s[b.s], y_s[b.s], n2.rstd[b.s], n2.nmr[b.s], p, j).then_inc(normed_x[1], 1)

                        def evacuate_x3(b):
                            p, j = pj(b)
                            act.wait_ge(turned_b, b.n + 1)
                            act.nop(nofuse=True)
                            if b.after(1):
                                act.wait_ge(scored, b.n)
                                act.nop(nofuse=True)
                            nc.scalar.copy(cols(o_t, D, p, j), cols(p_o, D, p, j)).then_inc(evacuated_b, 1)

                        pipeline(act, NB, [(root_2, 4), (evacuate, 1), (normalise_1, 3), (normalise_2, 4), (root_1, 2),
                                           (evacuate_x3, 4)])
            end_pass()

        attention_edge_pass()
        attention_node_pass()

        edge_sum_pass("g3", 64, scaled[64], sums[64])
        aggregate_last_pass("n3", scaled[64], sums[64], brow["L3_gnn_b1"], 64, w["L3_gnn_W2"], 32, scaled[32])
        edge_sum_pass("g4", 32, scaled[32], sums[32])
        aggregate_last_pass("n4", scaled[32], sums[32], brow["L3_gnn_b2"], 32, w["L3_gnn_W3"], 16, scaled[16])
        edge_sum_pass("g5", 16, scaled[16], sums[16])
        aggregate_last_pass("n5", scaled[16], sums[16], brow["L3_gnn_b3"], 16, None, 16, scaled2[16])
        edge_sum_pass("g6", 16, scaled2[16], sums[16])
        aggregate_then_weight_pass("n6", scaled2[16], sums[16], w["L3_gnn_W4"], brow["L3_gnn_b4"], 16, 32, scaled2[32], 32)
        edge_sum_pass("g7", 32, scaled2[32], sums[32])
        aggregate_then_weight_pass("n7", scaled2[32], sums[32], w["L3_gnn_W5"], brow["L3_gnn_b5"], 32, 64, scaled2[64], 64)
        edge_sum_pass("g8", 64, scaled2[64], sums[64])
        aggregate_then_weight_pass("n8", scaled2[64], sums[64], w["L3_gnn_W6"], brow["L3_gnn_b6"], 64, D, out, D,
                                   residual=x3, last_w=w["L3_gnn_Wf"], last_bias=brow["L3_gnn_bf"])


_INS = [
    "x", "src", "dst", "edge_attr_16", "L0_gnn_W1", "L0_gnn_b1", "L0_gnn_W2", "L0_gnn_b2", "L1_gnn_Wf", "L1_gnn_bf",
    "L1_gnn_Ws", "L1_gnn_bs", "L1_gnn_bn_gamma", "L1_gnn_bn_beta", "L1_gnn_ln_gamma", "L1_gnn_ln_beta", "L2_gnn_W",
    "L2_gnn_W_edge", "L2_gnn_att_src", "L2_gnn_att_dst", "L2_gnn_att_edge", "L2_gnn_gat_bias", "L2_gnn_lin_W",
    "L2_gnn_lin_b", "L2_gnn_ln_g", "L2_gnn_ln_b", "L3_gnn_W1", "L3_gnn_b1", "L3_gnn_W2", "L3_gnn_b2", "L3_gnn_W3",
    "L3_gnn_b3", "L3_gnn_W4", "L3_gnn_b4", "L3_gnn_W5", "L3_gnn_b5", "L3_gnn_W6", "L3_gnn_b6", "L3_gnn_Wf", "L3_gnn_bf",
]


def kernel(**inputs):
    import numpy as _np
    import concourse.bacc as _bacc
    from concourse import mybir as _mybir
    from concourse.bass_utils import run_bass_kernel_spmd as _run

    nc = _bacc.Bacc("TRN2", target_bir_lowering=False, num_devices=1)
    arrays, aps = {}, {}
    for name in _INS:
        arr = _np.ascontiguousarray(inputs[name])
        arrays[f"in_{name}"] = arr
        aps[name] = nc.dram_tensor(f"in_{name}", arr.shape, _mybir.dt.from_np(arr.dtype), kind="ExternalInput").ap()
    shape = inputs["x"].shape
    out = nc.dram_tensor("out_0", shape, _mybir.dt.float32, kind="ExternalOutput").ap()
    build(nc, aps, out)
    r = _run(nc, [arrays], core_ids=[0])
    return r.results[0]["out_0"]
```
